# Optimizing a Trainium2 kernel written in Bass

```python
import numpy as np
import jax
import jax.numpy as jnp

def _softmax(x, axis=-1):
    return jax.nn.softmax(x, axis=axis)

def _gelu(x):
    return jax.nn.gelu(x, approximate=True)

def _silu(x):
    return jax.nn.silu(x)

def _sigmoid(x):
    return jax.nn.sigmoid(x)

def _layernorm(x, axis=-1, eps=1e-05):
    m = jnp.mean(x, axis=axis, keepdims=True)
    v = jnp.var(x, axis=axis, keepdims=True)
    return (x - m) / jnp.sqrt(v + eps)

def _scatter_add(tgt, idx, src, axis=0):
    return tgt.at[idx].add(src)

def _segment_sum(src, seg, n):
    return jax.ops.segment_sum(src, seg, n)
kernel_name = 'mk_decoder_postln_d1_seqx_r8_e5c724'

def setup_inputs(seed: int=0):
    np.random.seed(seed)
    _w = jnp.asarray

    def _rec_inputs():
        import jax
        import jax.numpy as jnp
        _rk = jax.random.key(seed)
        x = -0.0003929 + 0.9999 * jax.random.normal(jax.random.fold_in(_rk, 1), (32, 64, 128), jnp.float32)
        _lenS = 64 - jax.random.randint(jax.random.fold_in(_rk, 7), (32,), 0, max(1, 64 // 4) + 1, jnp.int32)
        _lenS2 = 64 - jax.random.randint(jax.random.fold_in(_rk, 8), (32,), 0, max(1, 64 // 4) + 1, jnp.int32)
        _ctx_1024P = jax.random.normal(jax.random.fold_in(_rk, 11), (32, 16, 128), jnp.float32)
        _ctx_1024c = jax.random.dirichlet(jax.random.fold_in(_rk, 511), 0.3 * jnp.ones((16,), jnp.float32), (32, 64))
        _ctx_1024t = jnp.einsum('bsk,bkd->bsd', _ctx_1024c, _ctx_1024P)
        _ctx_1024t = _ctx_1024t * jax.lax.rsqrt(jnp.mean(jnp.square(_ctx_1024t)) + 1e-12) * 0.953939
        ctx_1024 = 2.81802e-05 + 1.00001 * (_ctx_1024t + 0.3 * jax.random.normal(jax.random.fold_in(_rk, 611), (32, 64, 128), jnp.float32))
        _validS = jnp.arange(64)[None, :] < _lenS[:, None]
        _validS2 = jnp.arange(64)[None, :] < _lenS2[:, None]
        _causal = jnp.tril(jnp.ones((64, 64), dtype=bool))
        mask_BxS2_bf1 = jnp.ones((32, 64), dtype=bool)
        return (x, ctx_1024, mask_BxS2_bf1)
    x, ctx_1024, mask_BxS2_bf1 = _rec_inputs()

    def _L0_attn_setup():
        import jax, jax.numpy as jnp
        import numpy as np
        import math
        NUM_HEADS = 16
        HEAD_DIM = 64
        DIM = 128
        INNER = NUM_HEADS * HEAD_DIM
        BUCKETS = 32
        MAX_DIST = 128

        def _relative_position_bucket(relative_position, bidirectional=True, num_buckets=BUCKETS, max_distance=MAX_DIST):
            rp = relative_position
            if bidirectional:
                num_buckets //= 2
                relative_buckets = (rp > 0).astype(jnp.int32) * num_buckets
                rp = jnp.abs(rp)
            else:
                relative_buckets = jnp.zeros_like(rp)
                rp = -jnp.minimum(rp, 0)
            max_exact = num_buckets // 2
            is_small = rp < max_exact
            rp_safe = jnp.maximum(rp, 1).astype(jnp.float32)
            rel_if_large = max_exact + (jnp.log(rp_safe / max_exact) / math.log(max_distance / max_exact) * (num_buckets - max_exact)).astype(jnp.int32)
            rel_if_large = jnp.minimum(rel_if_large, num_buckets - 1)
            relative_buckets = relative_buckets + jnp.where(is_small, rp, rel_if_large)
            return relative_buckets

        def compute_bias(rel_bias_table, q_len, k_len):
            ctx = jnp.arange(q_len)[:, None]
            mem = jnp.arange(k_len)[None, :]
            buckets = _relative_position_bucket(mem - ctx, bidirectional=True)
            values = rel_bias_table[buckets]
            return jnp.transpose(values, (2, 0, 1))[None]
        key = jax.random.key(seed)
        ks = jax.random.split(key, 6)
        B, S = (2, 256)
        sc = 0.02
        return {'hidden_states': jax.random.normal(ks[0], (B, S, DIM), jnp.float32), 'Wq': jax.random.normal(ks[1], (DIM, INNER), jnp.float32) * sc, 'Wk': jax.random.normal(ks[2], (DIM, INNER), jnp.float32) * sc, 'Wv': jax.random.normal(ks[3], (DIM, INNER), jnp.float32) * sc, 'Wo': jax.random.normal(ks[4], (INNER, DIM), jnp.float32) * sc, 'rel_bias': jax.random.normal(ks[5], (BUCKETS, NUM_HEADS), jnp.float32) * sc}
    _L0_attn_all = _L0_attn_setup()
    _L0_attn_in = {k: v for k, v in _L0_attn_all.items() if k in ('Wq', 'Wk', 'Wv', 'Wo', 'rel_bias')}
    del _L0_attn_all

    def _L0_xattn_setup():
        import jax, jax.numpy as jnp
        import numpy as np
        B, N, D_MODEL, H, W = (4, 512, 128, 16, 32)
        D_K = D_MODEL // H

        def _look_around(x, pad_value):
            pad_width = [(0, 0), (1, 0), (0, 0)] + [(0, 0)] * (x.ndim - 3)
            padded = jnp.pad(x, pad_width, constant_values=pad_value)
            return jnp.concatenate([padded[:, :-1], padded[:, 1:]], axis=2)

        def _local_attention(q, k, v, mask):
            b, h, n, d = q.shape
            nw = n // W
            scale = d ** (-0.5)
            bq = (q * scale).reshape(b * h, nw, W, d)
            bk = _look_around(k.reshape(b * h, nw, W, d), 0.0)
            bv = _look_around(v.reshape(b * h, nw, W, d), 0.0)
            pos = jnp.arange(n).reshape(1, nw, W)
            bq_t = pos
            bq_k = _look_around(pos, -1)
            causal = bq_t[..., :, None] >= bq_k[..., None, :]
            valid = (bq_k != -1)[..., None, :]
            kmask = _look_around(mask.reshape(b, nw, W), False)
            kmask = jnp.repeat(kmask, h, axis=0)[:, :, None, :]
            full_mask = causal & valid & kmask
            sim = jnp.einsum('bnid,bnjd->bnij', bq, bk)
            sim = jnp.where(full_mask, sim, jnp.finfo(sim.dtype).min)
            attn = jax.nn.softmax(sim, axis=-1)
            out = jnp.einsum('bnij,bnjd->bnid', attn, bv)
            return out.reshape(b, h, n, d)
        key = jax.random.key(seed)
        ks = jax.random.split(key, 12)
        mk = lambda k, shape: jax.random.normal(k, shape, dtype=jnp.float32)
        inp = {'query': mk(ks[0], (B, N, D_MODEL)), 'key': mk(ks[1], (B, N, D_MODEL)), 'value': mk(ks[2], (B, N, D_MODEL)), 'mask': jnp.ones((B, N), dtype=bool)}
        scale = 0.02
        for i, nm in enumerate(['q', 'k', 'v', 'o']):
            inp[f'W_{nm}'] = mk(ks[3 + 2 * i], (D_MODEL, D_MODEL)) * scale
            inp[f'b_{nm}'] = jnp.zeros((D_MODEL,), dtype=jnp.float32)
        return inp
    _L0_xattn_all = _L0_xattn_setup()
    _L0_xattn_in = {k: v for k, v in _L0_xattn_all.items() if k in ('W_q', 'b_q', 'W_k', 'b_k', 'W_v', 'b_v', 'W_o', 'b_o')}
    del _L0_xattn_all

    def _L0_ffn_setup():
        import jax, jax.numpy as jnp
        import numpy as np
        B, S, H = (8, 512, 128)
        NAV = 128
        E = 8
        F = 2 * H
        key = jax.random.key(seed)
        ks = jax.random.split(key, 12)

        def w(k, shape, fan_in):
            return jax.random.normal(k, shape, dtype=jnp.float32) / np.sqrt(fan_in)
        return {'hidden_states': jax.random.normal(ks[0], (B, S, H), dtype=jnp.float32), 'Wp1': w(ks[1], (H, NAV), H), 'bp1': jnp.zeros((NAV,), jnp.float32), 'Wp2': w(ks[2], (NAV, E), NAV), 'bp2': jnp.zeros((E,), jnp.float32), 'W1': w(ks[3], (E, H, F), H), 'b1': jnp.zeros((E, F), jnp.float32), 'W2': w(ks[4], (E, F, H), F), 'b2': jnp.zeros((E, H), jnp.float32), 'Wo': w(ks[5], (H, H), H), 'bo': jnp.zeros((H,), jnp.float32)}
    _L0_ffn_all = _L0_ffn_setup()
    _L0_ffn_in = {k: v for k, v in _L0_ffn_all.items() if k in ('Wp1', 'bp1', 'Wp2', 'bp2', 'W1', 'b1', 'W2', 'b2', 'Wo', 'bo')}
    del _L0_ffn_all
    return {'x': x, 'ctx_1024': ctx_1024, 'mask_BxS2_bf1': mask_BxS2_bf1, 'L0_attn_Wq': _L0_attn_in['Wq'], 'L0_attn_Wk': _L0_attn_in['Wk'], 'L0_attn_Wv': _L0_attn_in['Wv'], 'L0_attn_Wo': _L0_attn_in['Wo'], 'L0_attn_rel_bias': _L0_attn_in['rel_bias'], 'L0_xattn_W_q': _L0_xattn_in['W_q'], 'L0_xattn_b_q': _L0_xattn_in['b_q'], 'L0_xattn_W_k': _L0_xattn_in['W_k'], 'L0_xattn_b_k': _L0_xattn_in['b_k'], 'L0_xattn_W_v': _L0_xattn_in['W_v'], 'L0_xattn_b_v': _L0_xattn_in['b_v'], 'L0_xattn_W_o': _L0_xattn_in['W_o'], 'L0_xattn_b_o': _L0_xattn_in['b_o'], 'L0_ffn_Wp1': _L0_ffn_in['Wp1'], 'L0_ffn_bp1': _L0_ffn_in['bp1'], 'L0_ffn_Wp2': _L0_ffn_in['Wp2'], 'L0_ffn_bp2': _L0_ffn_in['bp2'], 'L0_ffn_W1': _L0_ffn_in['W1'], 'L0_ffn_b1': _L0_ffn_in['b1'], 'L0_ffn_W2': _L0_ffn_in['W2'], 'L0_ffn_b2': _L0_ffn_in['b2'], 'L0_ffn_Wo': _L0_ffn_in['Wo'], 'L0_ffn_bo': _L0_ffn_in['bo']}

def reference(x, ctx_1024, mask_BxS2_bf1, L0_attn_Wq, L0_attn_Wk, L0_attn_Wv, L0_attn_Wo, L0_attn_rel_bias, L0_xattn_W_q, L0_xattn_b_q, L0_xattn_W_k, L0_xattn_b_k, L0_xattn_W_v, L0_xattn_b_v, L0_xattn_W_o, L0_xattn_b_o, L0_ffn_Wp1, L0_ffn_bp1, L0_ffn_Wp2, L0_ffn_bp2, L0_ffn_W1, L0_ffn_b1, L0_ffn_W2, L0_ffn_b2, L0_ffn_Wo, L0_ffn_bo):
    import jax
    import jax.numpy as jnp

    def _L0_attn_ref(hidden_states, Wq, Wk, Wv, Wo, rel_bias):
        import jax, jax.numpy as jnp
        import numpy as np
        import math
        NUM_HEADS = 16
        HEAD_DIM = 64
        DIM = 128
        INNER = NUM_HEADS * HEAD_DIM
        BUCKETS = 32
        MAX_DIST = 128

        def _relative_position_bucket(relative_position, bidirectional=True, num_buckets=BUCKETS, max_distance=MAX_DIST):
            rp = relative_position
            if bidirectional:
                num_buckets //= 2
                relative_buckets = (rp > 0).astype(jnp.int32) * num_buckets
                rp = jnp.abs(rp)
            else:
                relative_buckets = jnp.zeros_like(rp)
                rp = -jnp.minimum(rp, 0)
            max_exact = num_buckets // 2
            is_small = rp < max_exact
            rp_safe = jnp.maximum(rp, 1).astype(jnp.float32)
            rel_if_large = max_exact + (jnp.log(rp_safe / max_exact) / math.log(max_distance / max_exact) * (num_buckets - max_exact)).astype(jnp.int32)
            rel_if_large = jnp.minimum(rel_if_large, num_buckets - 1)
            relative_buckets = relative_buckets + jnp.where(is_small, rp, rel_if_large)
            return relative_buckets

        def compute_bias(rel_bias_table, q_len, k_len):
            ctx = jnp.arange(q_len)[:, None]
            mem = jnp.arange(k_len)[None, :]
            buckets = _relative_position_bucket(mem - ctx, bidirectional=True)
            values = rel_bias_table[buckets]
            return jnp.transpose(values, (2, 0, 1))[None]
        B, S, _ = hidden_states.shape

        def shape_heads(x):
            return jnp.transpose(x.reshape(B, S, NUM_HEADS, HEAD_DIM), (0, 2, 1, 3))
        q = shape_heads(hidden_states @ Wq)
        k = shape_heads(hidden_states @ Wk)
        v = shape_heads(hidden_states @ Wv)
        scores = jnp.einsum('bhqd,bhkd->bhqk', q, k)
        position_bias = compute_bias(rel_bias, S, S)
        scores = scores + position_bias
        weights = jax.nn.softmax(scores, axis=-1)
        attn = jnp.einsum('bhqk,bhkd->bhqd', weights, v)
        attn = jnp.transpose(attn, (0, 2, 1, 3)).reshape(B, S, INNER)
        return attn @ Wo

    def _L0_xattn_ref(query, key, value, mask, W_q, b_q, W_k, b_k, W_v, b_v, W_o, b_o):
        import jax, jax.numpy as jnp
        import numpy as np
        B, N, D_MODEL, H, W = (4, 512, 128, 16, 32)
        D_K = D_MODEL // H

        def _look_around(x, pad_value):
            pad_width = [(0, 0), (1, 0), (0, 0)] + [(0, 0)] * (x.ndim - 3)
            padded = jnp.pad(x, pad_width, constant_values=pad_value)
            return jnp.concatenate([padded[:, :-1], padded[:, 1:]], axis=2)

        def _local_attention(q, k, v, mask):
            b, h, n, d = q.shape
            nw = n // W
            scale = d ** (-0.5)
            bq = (q * scale).reshape(b * h, nw, W, d)
            bk = _look_around(k.reshape(b * h, nw, W, d), 0.0)
            bv = _look_around(v.reshape(b * h, nw, W, d), 0.0)
            pos = jnp.arange(n).reshape(1, nw, W)
            bq_t = pos
            bq_k = _look_around(pos, -1)
            causal = bq_t[..., :, None] >= bq_k[..., None, :]
            valid = (bq_k != -1)[..., None, :]
            kmask = _look_around(mask.reshape(b, nw, W), False)
            kmask = jnp.repeat(kmask, h, axis=0)[:, :, None, :]
            full_mask = causal & valid & kmask
            sim = jnp.einsum('bnid,bnjd->bnij', bq, bk)
            sim = jnp.where(full_mask, sim, jnp.finfo(sim.dtype).min)
            attn = jax.nn.softmax(sim, axis=-1)
            out = jnp.einsum('bnij,bnjd->bnid', attn, bv)
            return out.reshape(b, h, n, d)
        b, n, _ = query.shape

        def proj(x, Wm, bias):
            return (x @ Wm.T + bias).reshape(b, n, H, D_K).transpose(0, 2, 1, 3)
        q = proj(query, W_q, b_q)
        k = proj(key, W_k, b_k)
        v = proj(value, W_v, b_v)
        x = _local_attention(q, k, v, mask)
        x = x.transpose(0, 2, 1, 3).reshape(b, n, H * D_K)
        return x @ W_o.T + b_o

    def _L0_ffn_ref(hidden_states, Wp1, bp1, Wp2, bp2, W1, b1, W2, b2, Wo, bo):
        import jax, jax.numpy as jnp
        import numpy as np
        B, S, H = (8, 512, 128)
        NAV = 128
        E = 8
        F = 2 * H
        last = hidden_states[:, -1, :]
        logits = jax.nn.gelu(last @ Wp1 + bp1, approximate=False) @ Wp2 + bp2
        action_probs = jax.nn.softmax(logits, axis=-1)
        sel = jnp.argmax(action_probs, axis=-1)
        w1 = W1[sel]
        w2 = W2[sel]
        h = jax.nn.gelu(jnp.einsum('bsh,bhf->bsf', hidden_states, w1) + b1[sel][:, None, :], approximate=False)
        reasoned = jnp.einsum('bsf,bfh->bsh', h, w2) + b2[sel][:, None, :]
        out = reasoned @ Wo + bo
        return hidden_states + 0.3 * out
    x = _layernorm(x + _L0_attn_ref(x, L0_attn_Wq, L0_attn_Wk, L0_attn_Wv, L0_attn_Wo, L0_attn_rel_bias), axis=-1)
    x = _layernorm(x + _L0_xattn_ref(x, ctx_1024, ctx_1024, mask_BxS2_bf1, L0_xattn_W_q, L0_xattn_b_q, L0_xattn_W_k, L0_xattn_b_k, L0_xattn_W_v, L0_xattn_b_v, L0_xattn_W_o, L0_xattn_b_o), axis=-1)
    x = _layernorm(x + _L0_ffn_ref(x, L0_ffn_Wp1, L0_ffn_bp1, L0_ffn_Wp2, L0_ffn_bp2, L0_ffn_W1, L0_ffn_b1, L0_ffn_W2, L0_ffn_b2, L0_ffn_Wo, L0_ffn_bo), axis=-1)
    return x

_drawn_inputs = setup_inputs


def setup_inputs(seed=0):
    import zlib

    import numpy as np

    out = dict(_drawn_inputs(seed))
    spreads = {'L0_xattn_b_q': (0.0, 0.8),
     'L0_xattn_b_k': (0.0, 0.8),
     'L0_xattn_b_v': (0.0, 0.1),
     'L0_xattn_b_o': (0.0, 0.1),
     'L0_ffn_bp1': (0.0, 0.1),
     'L0_ffn_bp2': (0.0, 0.1),
     'L0_ffn_b1': (0.0, 0.785),
     'L0_ffn_b2': (0.0, 0.56),
     'L0_ffn_bo': (0.0, 0.542)}
    factors = {'L0_attn_Wq': 2.929,
     'L0_attn_Wk': 2.937,
     'L0_attn_Wo': 2.815,
     'L0_attn_rel_bias': 8.0,
     'L0_xattn_W_q': 8.0,
     'L0_xattn_W_k': 8.0}
    for name, (base, spread) in spreads.items():
        noise = np.random.default_rng([zlib.crc32(name.encode()), seed]).standard_normal(out[name].shape)
        drawn = base * np.exp(spread * noise) if base else spread * noise
        out[name] = jnp.asarray(drawn.astype(out[name].dtype))
    for name, factor in factors.items():
        out[name] = (out[name] * factor).astype(out[name].dtype)
    return out
```

```python
from contextlib import ExitStack

import numpy as np

import concourse.bass as bass
from concourse import mybir

F32 = mybir.dt.float32
F32R = mybir.dt.float32r
I32 = mybir.dt.int32
U32 = mybir.dt.uint32
U8 = mybir.dt.uint8
ALU = mybir.AluOpType
ACT = mybir.ActivationFunctionType
AX = mybir.AxisListType.X

B, S, D = 32, 64, 128
TOK = B * S
P = 128
NT = TOK // P
NP = NT // 2
PT = 2 * P
H, HD = 16, 64
J = H // 2
XD = D // H
BUCKETS, MAX_DIST = 32, 128
NREL = 2 * S - 1
E, F = 8, 256
FC = F // P
EPS = 1e-5
FMAX = float(np.finfo(np.float32).max)
VW = 2 * XD + 1
WSEL = 2 * F + FC + D
O_W2, O_B1, O_B2 = F, 2 * F, 2 * F + FC


def need(eng, sem, value):
    if isinstance(value, int) and value <= 0:
        return
    eng.wait_ge(sem, value)


def apart(eng, sem):
    eng.sem_inc(sem, 1)


def build(nc, din, out_dram):
    with ExitStack() as ctx:
        def sb(name, shape, dt=F32):
            return ctx.enter_context(nc.sbuf_tensor(name, shape, dt))

        def sem(name):
            return ctx.enter_context(nc.semaphore(name))

        SC = ctx.enter_context(nc.psum_tensor("SC", [P, 2, 512], F32))
        TR = ctx.enter_context(nc.psum_tensor("TR", [P, 2, 512], F32))
        AV = ctx.enter_context(nc.psum_tensor("AV", [P, 2, 512], F32))
        G = ctx.enter_context(nc.psum_tensor("G", [P, 2, 512], F32))

        ident = sb("ident", [P, P])
        causal = sb("causal", [P, P])
        headmask = sb("headmask", [P, J])
        w0flag = sb("w0flag", [P, 1])
        ones = sb("ones", [1, S])
        onehot = sb("onehot", [BUCKETS, NREL])
        table = sb("table", [BUCKETS, H])
        rel = sb("rel", [H, NREL])
        bias = sb("bias", [P, J, S])
        maskadd = sb("maskadd", [P, TOK])
        kmask = sb("kmask", [P, TOK], U8)
        mhi = sb("mhi", [P, H, D], F32R)
        mlo = sb("mlo", [P, H, D], F32R)
        wvhi = sb("wvhi", [P, H * HD], F32R)
        wvlo = sb("wvlo", [P, H * HD], F32R)
        wo = sb("wo", [P, J, D])
        xwq = sb("xwq", [P, D])
        xwk = sb("xwk", [P, D])
        xwv = sb("xwv", [P, D])
        xwo = sb("xwo", [P, D])
        xbq = sb("xbq", [P, 1])
        xbk = sb("xbk", [P, 1])
        xbv = sb("xbv", [P, D])
        xbo = sb("xbo", [P, D])
        wp1 = sb("wp1", [D, P])
        bp1 = sb("bp1", [P, 1])
        wp2 = sb("wp2", [P, E])
        bp2 = sb("bp2", [B, E])
        w12 = sb("w12", [P, E * WSEL])
        w12v = w12[:, :].rearrange("p (e w) -> p e w", e=E)
        fwo = sb("fwo", [P, D])
        fbo = sb("fbo", [P, D])
        b2t = sb("b2t", [P, E])

        xt_in = sb("xt_in", [P, PT])
        xhi = sb("xhi", [P, PT], F32R)
        xlo = sb("xlo", [P, PT], F32R)
        xts = sb("xts", [P, PT])
        xk = sb("xk", [P, 2, D])
        ctxt = sb("ctxt", [P, PT])
        Y = sb("Y", [P, 2, J, PT])
        V = sb("V", [P, 2, H * HD])
        s1 = sb("s1", [P, J, 2, S])
        p1 = sb("p1", [P, J, 2, S])
        pt1 = sb("pt1", [P, J, P])
        at = sb("at", [P, J, 2, S])
        mx1, sm1, rc1 = (sb(n, [P, J, 2]) for n in ("mx1", "sm1", "rc1"))
        z1, x1 = sb("z1", [P, D]), sb("x1", [P, D])
        x1b = sb("x1b", [P, 2, D])
        x1t = sb("x1t", [P, D])
        qpad = sb("qpad", [P, 2, 2, S])
        ktb = sb("ktb", [P, P])
        kbd = sb("kbd", [P, 2, J, S])
        vbd = sb("vbd", [P, 2, J, 2 * VW])
        s2 = sb("s2", [P, J, 2, S])
        mx2, corr, den, rc2 = (sb(n, [P, J, 2]) for n in ("mx2", "corr", "den", "rc2"))
        pt2 = sb("pt2", [P, J, P])
        on = sb("on", [P, 2, J, XD])
        ot = sb("ot", [P, P])
        z2, x2s = sb("z2", [P, D]), sb("x2s", [P, D])
        st1, st2, st3 = (sb(n, [P, 6]) for n in ("st1", "st2", "st3"))
        mv1, mv2 = (sb(n, [P, 2]) for n in ("mv1", "mv2"))
        ve1, ve2, rs1, rs2 = (sb(n, [P, 1]) for n in ("ve1", "ve2", "rs1", "rs2"))
        mv3, ve3, rs3 = sb("mv3", [P, 2, 2]), sb("ve3", [P, 2]), sb("rs3", [P, 2])
        half = sb("half", [P, 1])
        x2 = sb("x2", [P, TOK])
        x2t = sb("x2t", [P, TOK])
        wkt = w12[:, 0:J * D].rearrange("p (j n) -> p j n", j=J)
        wqt = w12[:, J * D:2 * J * D].rearrange("p (j n) -> p j n", j=J)
        wvr = w12[:, 2 * J * D:3 * J * D]
        w2t = Y[:, :, :, :].rearrange("p a j t -> p (a j t)")[:, 0:E * F].rearrange("p (e f) -> p e f", e=E)
        wsel = sb("wsel", [P, 2, 2, WSEL])
        ht = sb("ht", [P, 2, 2, FC, S])
        gp = sb("gp", [P, B])
        lg, pe_, pr = (sb(n, [B, E]) for n in ("lg", "pexp", "prob"))
        lm, ls, lr = (sb(n, [B, 1]) for n in ("lm", "ls", "lr"))
        pm8 = sb("pm8", [B, 8])
        ix8 = sb("ix8", [B, 8], U32)
        ixf = sb("ixf", [B, 1])
        sel = sb("sel", [1, B], I32)
        scratch = nc.dram_tensor("rel_scratch", (H, S, NREL), F32).ap()

        names = """wait_apart c_ident c_table c_small c_m c_v c_wo c_x c_rel c_relst c_bias c_mask c_ffn c_w2t
            memset_done rel_ps rel_sb mask_f mask_mul mask_add m_ps m_hi m_lo wv_hi wv_lo
            xt_ld xk_ld ctx_ld xhi_ok xlo_ok xts_ok y_ps y_sb v_ps v_sb kt_ps kt_sb vx_ps vbd_ok kbd_ok
            s1_ps s1_in s1_mx s1_sub s1_exp s1_sum s1_rc p1_ok pt1_ps pt1_sb av_ps at_sb wo_ps
            z1_ok st1_ok mv1_ok ve1_ok rs1_ok x1_ok x1b_ok x1t_ps x1t_sb q_ps qpad_ok
            s2_ps s2_in s2_mx s2_sub s2_exp p2_zero pt2_ps pt2_sb pv2_ps corr_ok den_ok rc2_ok on_ok ot_ps ot_sb wox_ps
            z2_ok st2_ok mv2_ok ve2_ok rs2_ok x2_ok x2_keep x2t_ps x2t_sb
            w2_ps w2_sb b2_ps b2_sb hid_ps hid_sb lg_ps lg_sb lm_ok pexp_ok ls_ok lr_ok prob_ok pm_ok ix_ok ixf_ok ixt_ps sel_ok
            wsel_ok h_ps h_sb f_ps y3_ok st3_ok mv3_ok ve3_ok rs3_ok out_ok out_st""".split()
        s = {n: sem(n) for n in names}
        block = ctx.enter_context(nc.Block())

        @block.sync
        def _(sp):
            def load_xt(q):
                need(sp, s["xts_ok"], q)
                need(sp, s["xlo_ok"], q)
                sp.dma_start(xt_in[:, :], din["xT"][:, bass.ds(q * PT, PT)]).then_inc(s["xt_ld"], 16)

            def load_ctx(q):
                need(sp, s["kt_ps"], 2 * q)
                need(sp, s["vx_ps"], 2 * q)
                sp.dma_start(ctxt[:, :], din["ctxT"][:, bass.ds(q * PT, PT)]).then_inc(s["ctx_ld"], 16)

            def load_xk(q):
                need(sp, s["z1_ok"], 2 * q)
                sp.dma_start(xk[:, :, :], din["x"][bass.ds(q * PT, PT), :].rearrange("(t p) d -> p t d", p=P)
                             ).then_inc(s["xk_ld"], 16)

            sp.dma_start(wkt, din["WkT"].rearrange("(j p) n -> p j n", p=P)).then_inc(s["c_m"], 16)
            sp.dma_start(wqt, din["WqT"].rearrange("(j p) n -> p j n", p=P)).then_inc(s["c_m"], 16)
            sp.dma_start(wvr, din["Wv"]).then_inc(s["c_v"], 16)
            load_ctx(0)
            load_xk(0)
            sp.dma_start(wo[:, :, :], din["Wo"].rearrange("(j p) n -> p j n", p=P)).then_inc(s["c_wo"], 16)
            sp.wait_ge(s["m_ps"], 4)
            sp.wait_ge(s["wv_lo"], 1)
            sp.dma_start(w12v[:, :, 0:F], din["W1"].rearrange("e h f -> h e f")).then_inc(s["c_ffn"], 16)
            sp.dma_start(w12v[:, :, O_B1:O_B2], din["b1T"]).then_inc(s["c_ffn"], 16)
            sp.dma_start(fwo[:, :], din["fWo"]).then_inc(s["c_ffn"], 16)
            sp.dma_start(fbo[:, :], din["fbo"].partition_broadcast(P)).then_inc(s["c_ffn"], 16)
            sp.dma_start(b2t[:, :], din["b2T"]).then_inc(s["c_ffn"], 16)
            sp.dma_start(wp1[:, :], din["Wp1"]).then_inc(s["c_ffn"], 16)
            sp.dma_start(bp1[:, :], din["bp1"]).then_inc(s["c_ffn"], 16)
            sp.dma_start(wp2[:, :], din["Wp2"]).then_inc(s["c_ffn"], 16)
            sp.dma_start(bp2[:, :], din["bp2"].partition_broadcast(B)).then_inc(s["c_ffn"], 16)
            with sp.Fori(1, NP) as q:
                load_xt(q)
                load_ctx(q)
                load_xk(q)
            sp.wait_ge(s["s1_ps"], 2 * NT)
            sp.dma_start(w2t, din["W2T"].rearrange("e h f -> h e f")).then_inc(s["c_w2t"], 16)
            with sp.Fori(0, NT) as t:
                sp.wait_ge(s["out_ok"], t + 1)
                sp.dma_start(out_dram[bass.ds(t * P, P), :], x2[:, bass.ds(t * D, D)]).then_inc(s["out_st"], 16)
            sp.wait_ge(s["out_st"], 16 * NT)

        @block.scalar
        def _(act):
            A = nc.scalar.activation
            act.dma_start(table[:, :], din["table"]).then_inc(s["c_table"], 16)
            act.dma_start(onehot[:, :], din["onehot"]).then_inc(s["c_table"], 16)
            act.dma_start(xt_in[:, :], din["xT"][:, 0:PT]).then_inc(s["xt_ld"], 16)
            act.dma_start(ident[:, :], din["ident"]).then_inc(s["c_ident"], 16)
            act.dma_start(headmask[:, :], din["headmask"]).then_inc(s["c_small"], 16)
            act.dma_start(w0flag[:, :], din["w0flag"]).then_inc(s["c_small"], 16)
            for dst, name in ((xwq, "xWqT"), (xwk, "xWkT"), (xwv, "xWvT"), (xwo, "xWoT"), (xbq, "xbq"), (xbk, "xbk")):
                act.dma_start(dst[:, :], din[name]).then_inc(s["c_small"], 16)
            act.dma_start(xbv[:, :], din["xbv"].partition_broadcast(P)).then_inc(s["c_small"], 16)
            act.dma_start(xbo[:, :], din["xbo"].partition_broadcast(P)).then_inc(s["c_small"], 16)
            nc.scalar.preload_act_table(ACT.Exp)

            def split_hi(q):
                act.wait_ge(s["xt_ld"], 16 * (q + 1))
                need(act, s["v_ps"], 4 * q)
                A(xhi[:, :], xt_in[:, :], ACT.Copy).then_inc(s["xhi_ok"], 1)

            def copy_xts(q):
                need(act, s["s1_ps"], 4 * q)
                A(xts[:, :], xt_in[:, :], ACT.Copy).then_inc(s["xts_ok"], 1)

            def y_out(q, u, g):
                act.wait_ge(s["y_ps"], 8 * q + u + 1)
                A(Y[:, :, u, :], G[:, g, :].rearrange("p (a t) -> p a t", a=2), ACT.Copy).then_inc(s["y_sb"], 1)

            def v_out(q, u, g):
                act.wait_ge(s["v_ps"], 4 * q + u + 1)
                A(V[:, u // 2, (u % 2) * 512:(u % 2) * 512 + 512], G[:, g, :], ACT.Copy).then_inc(s["v_sb"], 1)

            def kt_out(t):
                act.wait_ge(s["kt_ps"], t + 1)
                need(act, s["kbd_ok"], 2 * t)
                A(ktb[:, :], G[:, 1, 0:P], ACT.Identity, bias=xbk[:, 0:1]).then_inc(s["kt_sb"], 1)

            def exp1(t, hh):
                act.wait_ge(s["s1_sub"], 2 * t + hh + 1)
                A(s1[:, 4 * hh:4 * hh + 4], s1[:, 4 * hh:4 * hh + 4], ACT.Exp).then_inc(s["s1_exp"], 1)

            def exp2(t, hh):
                act.wait_ge(s["s2_sub"], 2 * t + hh + 1)
                A(s2[:, 4 * hh:4 * hh + 4], s2[:, 4 * hh:4 * hh + 4], ACT.Exp).then_inc(s["s2_exp"], 1)

            def step(t, odd, prev=True, nxt=True, fill=True, q=None):
                cur = not isinstance(t, int) or t < NT
                if fill and not odd:
                    split_hi(q + 1)
                if cur:
                    for hh in range(2):
                        act.wait_ge(s["pt1_ps"], 2 * t + hh + 1)
                        A(pt1[:, 4 * hh:4 * hh + 4, :], TR[:, hh, :].rearrange("p (j n) -> p j n", j=4),
                          ACT.Copy).then_inc(s["pt1_sb"], 1)
                if prev:
                    for hh in range(2):
                        act.wait_ge(s["pt2_ps"], 2 * t + hh - 1)
                        A(pt2[:, 4 * hh:4 * hh + 4, :], G[:, hh, :].rearrange("p (j n) -> p j n", j=4),
                          ACT.Copy).then_inc(s["pt2_sb"], 1)
                if cur:
                    for b in range(2):
                        act.wait_ge(s["av_ps"], 2 * t + b + 1)
                        A(at[:, :, b, :], AV[:, b, :].rearrange("p (j q) -> p j q", j=J), ACT.Copy
                          ).then_inc(s["at_sb"], 1)
                if prev:
                    act.wait_ge(s["ot_ps"], t)
                    A(ot[:, :], G[:, 1, 0:P], ACT.Copy).then_inc(s["ot_sb"], 1)
                if cur:
                    act.wait_ge(s["x1t_ps"], t + 1)
                    A(x1t[:, :], TR[:, 1, 0:P], ACT.Copy).then_inc(s["x1t_sb"], 1)
                if fill and not odd:
                    y_out(q + 1, 0, 1)
                    y_out(q + 1, 1, 0)
                    exp1(t + 1, 0)
                    y_out(q + 1, 2, 1)
                    exp1(t + 1, 1)
                    y_out(q + 1, 3, 0)
                    y_out(q + 1, 4, 1)
                    exp2(t, 0)
                    y_out(q + 1, 5, 0)
                    exp2(t, 1)
                    y_out(q + 1, 6, 1)
                    y_out(q + 1, 7, 0)
                    copy_xts(q + 1)
                    kt_out(t + 1)
                elif fill:
                    v_out(q + 1, 0, 1)
                    v_out(q + 1, 1, 0)
                    exp1(t + 1, 0)
                    v_out(q + 1, 2, 1)
                    exp1(t + 1, 1)
                    v_out(q + 1, 3, 0)
                    kt_out(t + 1)
                    exp2(t, 0)
                    exp2(t, 1)
                else:
                    if nxt:
                        kt_out(t + 1)
                        exp1(t + 1, 0)
                        exp1(t + 1, 1)
                    if cur:
                        exp2(t, 0)
                        exp2(t, 1)
                if prev:
                    act.wait_ge(s["x2t_ps"], t)
                    A(x2t[:, bass.ds((t - 1) * P, P)], G[:, 1, 0:P], ACT.Copy).then_inc(s["x2t_sb"], 1)

            split_hi(0)
            copy_xts(0)
            act.wait_ge(s["rel_ps"], 1)
            A(rel[:, :], SC[0:H, 0, 0:NREL], ACT.Copy).then_inc(s["rel_sb"], 1)
            act.wait_ge(s["rel_sb"], 1)
            act.dma_start(scratch, rel[:, :].unsqueeze(1).broadcast_to([H, S, NREL])).then_inc(s["c_relst"], 16)
            act.wait_ge(s["c_relst"], 16)
            for par in range(2):
                act.dma_start(bias[par * S:(par + 1) * S, :, :],
                              bass.AP(scratch.tensor, par * S * NREL + S - 1,
                                      [[NREL - 1, S], [2 * S * NREL, J], [1, S]])
                              ).then_inc(s["c_bias"], 16)
            for n in range(4):
                act.wait_ge(s["m_ps"], n + 1)
                src = (TR, AV)[n // 2][:, n % 2, :].rearrange("p (j n) -> p j n", j=4)
                h0 = 8 * (n // 2) + n % 2
                A(mhi[:, h0:h0 + 7:2, :], src, ACT.Copy).then_inc(s["m_hi"], 1)
            act.wait_ge(s["c_v"], 16)
            A(wvhi[:, :], wvr, ACT.Copy).then_inc(s["wv_hi"], 1)
            for u in range(8):
                y_out(0, u, (u + 1) % 2)
            for u in range(4):
                v_out(0, u, (u + 1) % 2)
            act.wait_ge(s["c_small"], 160)
            kt_out(0)
            exp1(0, 0)
            exp1(0, 1)
            step(0, False, prev=False, q=0)
            step(1, True, q=0)
            with act.Fori(1, NP - 1) as q:
                step(2 * q, False, q=q)
                step(2 * q + 1, True, q=q)
            step(NT - 2, False, fill=False)
            step(NT - 1, True, fill=False, nxt=False)
            step(NT, False, fill=False, nxt=False)

            act.wait_ge(s["hid_ps"], 1)
            A(gp[:, :], G[:, 0, 0:B], ACT.Gelu, bias=bp1[:, 0:1]).then_inc(s["hid_sb"], 1)
            for n in range(2):
                act.wait_ge(s["w2_ps"], n + 1)
                A(w12v[:, 2 * n:2 * n + 2, O_W2:O_B1].rearrange("p e (c n) -> p e c n", c=FC),
                  TR[:, n, :].rearrange("p (e c n) -> p e c n", e=2, c=FC), ACT.Copy).then_inc(s["w2_sb"], 1)
            act.wait_ge(s["lm_ok"], 1)
            A(pe_[:, :], lg[:, :], ACT.Exp, bias=lm[:, 0:1]).then_inc(s["pexp_ok"], 1)
            nc.scalar.preload_act_table(ACT.Gelu)

            def gelus(t, c):
                act.wait_ge(s["h_ps"], t + 1)
                need(act, s["f_ps"], t - 1)
                for b in range(2):
                    for f in range(FC):
                        A(ht[:, c, b, f, :], G[:, c, (b * FC + f) * S:(b * FC + f + 1) * S], ACT.Gelu,
                          bias=wsel[:, c, b, O_B1 + f:O_B1 + f + 1]).then_inc(s["h_sb"], 1)

            gelus(0, 0)
            gelus(1, 1)
            with act.Fori(1, NP) as q:
                gelus(2 * q, 0)
                gelus(2 * q + 1, 1)

        @block.gpsimd
        def _(pool):
            pl = nc.gpsimd
            pool.dma_start(causal[:, :], din["causal"]).then_inc(s["c_mask"], 16)
            pool.dma_start(kmask[:, :], din["mask"].partition_broadcast(P)).then_inc(s["c_mask"], 16)
            pl.memset(half[:, :], -0.5).then_inc(s["memset_done"], 1)
            pl.memset(ones[:, :], 1.0).then_inc(s["memset_done"], 1)
            pl.memset(qpad[:, :, :, :], 0.0).then_inc(s["memset_done"], 1)
            pl.memset(vbd[:, :, :, :], 0.0).then_inc(s["memset_done"], 1)
            pool.wait_ge(s["memset_done"], 4)
            for b in range(2):
                for c in range(2):
                    pl.memset(vbd[b * S:(b + 1) * S, c, :, b * VW + 2 * XD:b * VW + 2 * XD + 1], 1.0
                              ).then_inc(s["memset_done"], 1)
                    pool.wait_ge(s["memset_done"], 5 + 2 * b + c)
            pool.wait_ge(s["c_mask"], 32)
            pl.tensor_scalar(maskadd[:, :], kmask[:, :], 1.0, None, ALU.mult).then_inc(s["mask_f"], 1)
            pool.wait_ge(s["mask_f"], 1)
            pl.tensor_tensor(maskadd[:, :].rearrange("p (t k) -> p t k", k=P),
                             maskadd[:, :].rearrange("p (t k) -> p t k", k=P),
                             causal[:, :].unsqueeze(1).broadcast_to([P, NT, P]), ALU.mult).then_inc(s["mask_mul"], 1)
            pool.wait_ge(s["mask_mul"], 1)
            pl.tensor_scalar(maskadd[:, :], maskadd[:, :], -1.0, FMAX, ALU.add, ALU.mult).then_inc(s["mask_add"], 1)
            pool.wait_ge(s["c_small"], 160)

            def key_block(t):
                pool.wait_ge(s["kt_sb"], t + 1)
                need(pool, s["s2_ps"], 2 * t)
                for b in range(2):
                    pl.tensor_tensor(kbd[:, b, :, :], ktb[:, b * S:(b + 1) * S].unsqueeze(1).broadcast_to([P, J, S]),
                                     headmask[:, :].unsqueeze(2).broadcast_to([P, J, S]), ALU.mult
                                     ).then_inc(s["kbd_ok"], 1)

            def normalise1(t, hh):
                pool.wait_ge(s["s1_rc"], 2 * t + hh + 1)
                need(pool, s["pt1_ps"], 2 * t)
                js = slice(4 * hh, 4 * hh + 4)
                pl.tensor_tensor(p1[:, js, :, :].rearrange("p j b k -> p (j b) k"),
                                 s1[:, js, :, :].rearrange("p j b k -> p (j b) k"),
                                 rc1[:, js, :].rearrange("p j b -> p (j b)").unsqueeze(2).broadcast_to([P, 8, S]),
                                 ALU.mult).then_inc(s["p1_ok"], 1)

            def step(t, c, prev=True, nxt=True):
                cur = not isinstance(t, int) or t < NT
                if cur:
                    pool.wait_ge(s["ve1_ok"], t + 1)
                    pl.tensor_tensor(rs1[:, :], ve1[:, :], half[:, :], ALU.pow).then_inc(s["rs1_ok"], 1)
                    pool.wait_ge(s["x1_ok"], t + 1)
                    need(pool, s["z2_ok"], t - 1)
                    pl.tensor_tensor(x1b[:, c, :], x1[:, :], xbo[:, :], ALU.add).then_inc(s["x1b_ok"], 1)
                if prev:
                    pool.wait_ge(s["ve2_ok"], t)
                    pl.tensor_tensor(rs2[:, :], ve2[:, :], half[:, :], ALU.pow).then_inc(s["rs2_ok"], 1)
                if nxt:
                    normalise1(t + 1, 0)
                    normalise1(t + 1, 1)
                if cur:
                    if nxt:
                        pool.wait_ge(s["p1_ok"], 2 * t + 4)
                    else:
                        pool.wait_ge(s["x1b_ok"], t + 1)
                        if prev:
                            pool.wait_ge(s["rs2_ok"], t)
                    pool.wait_ge(s["s2_exp"], 2 * t + 2)
                    apart(pool, s["wait_apart"])
                    for r in range(2):
                        pl.memset(s2[r * S:r * S + S // 2, :, :, S // 2:S].rearrange("p j b k -> p (j b) k"), 0.0
                                  ).then_inc(s["p2_zero"], 1)
                        pool.wait_ge(s["p2_zero"], 2 * t + r + 1)
                        apart(pool, s["wait_apart"])
                if prev:
                    pool.wait_ge(s["x2_ok"], t)
                    pl.tensor_tensor(x2[:, bass.ds((t - 1) * D, D)], x2s[:, :], x2s[:, :], ALU.add
                                     ).then_inc(s["x2_keep"], 1)
                if nxt:
                    key_block(t + 1)

            key_block(0)
            normalise1(0, 0)
            normalise1(0, 1)
            step(0, 0, prev=False)
            step(1, 1)
            with pool.Fori(1, NP - 1) as q:
                step(2 * q, 0)
                step(2 * q + 1, 1)
            step(NT - 2, 0)
            step(NT - 1, 1, nxt=False)
            step(NT, 0, nxt=False)

            def ln3(t, c):
                pool.wait_ge(s["ve3_ok"], t + 1)
                pl.tensor_tensor(rs3[:, c:c + 1], ve3[:, c:c + 1], half[:, :], ALU.pow).then_inc(s["rs3_ok"], 1)

            with pool.Fori(0, NP) as q:
                ln3(2 * q, 0)
                ln3(2 * q + 1, 1)

        @block.vector
        def _(dve):
            v = nc.vector

            def flat(x):
                return x.rearrange("p j b k -> p (j b) k")

            def wide(x, js):
                return x[:, js, :].rearrange("p j b -> p (j b)").unsqueeze(2).broadcast_to([P, 8, S])

            def bias1(t, hh):
                dve.wait_ge(s["s1_ps"], 2 * t + hh + 1)
                need(dve, s["p1_ok"], 2 * t)
                js = slice(4 * hh, 4 * hh + 4)
                v.tensor_tensor(s1[:, js, :, :], SC[:, hh, :].rearrange("p (j b k) -> p j b k", j=4, b=2),
                                bias[:, js, :].unsqueeze(2).broadcast_to([P, 4, 2, S]), ALU.add
                                ).then_inc(s["s1_in"], 1)

            def max1(t, hh):
                dve.wait_ge(s["s1_in"], 2 * t + hh + 1)
                js = slice(4 * hh, 4 * hh + 4)
                v.tensor_reduce(mx1[:, js, :].rearrange("p j b -> p (j b)"), flat(s1[:, js, :, :]), axis=AX, op=ALU.max
                                ).then_inc(s["s1_mx"], 1)

            def sub1(t, hh):
                dve.wait_ge(s["s1_mx"], 2 * t + hh + 1)
                js = slice(4 * hh, 4 * hh + 4)
                v.tensor_tensor(flat(s1[:, js, :, :]), flat(s1[:, js, :, :]), wide(mx1, js), ALU.subtract
                                ).then_inc(s["s1_sub"], 1)

            def sum1(t, hh):
                dve.wait_ge(s["s1_exp"], 2 * t + hh + 1)
                js = slice(4 * hh, 4 * hh + 4)
                v.tensor_reduce(sm1[:, js, :].rearrange("p j b -> p (j b)"), flat(s1[:, js, :, :]), axis=AX, op=ALU.add
                                ).then_inc(s["s1_sum"], 1)

            def recip1(t, hh):
                dve.wait_ge(s["s1_sum"], 2 * t + hh + 1)
                js = slice(4 * hh, 4 * hh + 4)
                v.reciprocal(rc1[:, js, :], sm1[:, js, :]).then_inc(s["s1_rc"], 1)

            def mask2(t, hh):
                dve.wait_ge(s["s2_ps"], 2 * t + hh + 1)
                need(dve, s["pt2_ps"], 2 * t)
                js = slice(4 * hh, 4 * hh + 4)
                v.tensor_tensor(s2[:, js, :, :].rearrange("p j b k -> p j (b k)"),
                                SC[:, hh, :].rearrange("p (j n) -> p j n", j=4),
                                maskadd[:, bass.ds(t * P, P)].unsqueeze(1).broadcast_to([P, 4, P]), ALU.add
                                ).then_inc(s["s2_in"], 1)

            def max2(t, hh):
                dve.wait_ge(s["s2_in"], 2 * t + hh + 1)
                js = slice(4 * hh, 4 * hh + 4)
                v.tensor_reduce(mx2[:, js, :].rearrange("p j b -> p (j b)"), flat(s2[:, js, :, :]), axis=AX, op=ALU.max
                                ).then_inc(s["s2_mx"], 1)

            def sub2(t, hh):
                dve.wait_ge(s["s2_mx"], 2 * t + hh + 1)
                js = slice(4 * hh, 4 * hh + 4)
                v.tensor_tensor(flat(s2[:, js, :, :]), flat(s2[:, js, :, :]), wide(mx2, js), ALU.subtract
                                ).then_inc(s["s2_sub"], 1)

            def value_block(t, c):
                dve.wait_ge(s["vx_ps"], t + 1)
                for b in range(2):
                    rows = slice(b * S, (b + 1) * S)
                    dst = vbd[rows, c, :, b * VW:b * VW + 2 * XD].rearrange("p j (r d) -> p r j d", r=2)
                    src = G[rows, 0, 0:D].rearrange("p (r j d) -> p r j d", r=2, j=J)
                    add = xbv[rows, :].rearrange("p (r j d) -> p r j d", r=2, j=J)
                    v.tensor_tensor(dst, src, add, ALU.add).then_inc(s["vbd_ok"], 1)

            def split_lo(q):
                dve.wait_ge(s["xhi_ok"], q + 1)
                v.tensor_tensor(xlo[:, :], xt_in[:, :], xhi[:, :].bitcast(F32), ALU.subtract).then_inc(s["xlo_ok"], 1)

            def out_norm(t):
                dve.wait_ge(s["s2_mx"], 2 * t + 2)
                v.tensor_scalar(corr[:, :, :], mx2[:, :, :], -FMAX, w0flag[:, 0:1], ALU.is_equal, ALU.mult
                                ).then_inc(s["corr_ok"], 1)
                dve.wait_ge(s["pv2_ps"], t + 1)
                dve.wait_ge(s["corr_ok"], t + 1)
                o = G[:, 0, 0:J * 2 * VW].rearrange("p (j b w) -> p j b w", j=J, b=2)
                v.tensor_tensor(den[:, :, :].unsqueeze(3), o[:, :, :, 2 * XD:VW], corr[:, :, :].unsqueeze(3), ALU.add
                                ).then_inc(s["den_ok"], 1)
                dve.wait_ge(s["den_ok"], t + 1)
                v.reciprocal(rc2[:, :, :], den[:, :, :]).then_inc(s["rc2_ok"], 1)
                dve.wait_ge(s["rc2_ok"], t + 1)
                for r in range(2):
                    rows = slice(r * S, (r + 1) * S)
                    for b in range(2):
                        v.tensor_tensor(on[b * S:(b + 1) * S, r, :, :], o[rows, :, b, r * XD:(r + 1) * XD],
                                        rc2[rows, :, b].unsqueeze(2).broadcast_to([S, J, XD]), ALU.mult
                                        ).then_inc(s["on_ok"], 1)

            def step(t, odd, prev=True, nxt=True, fill=True, q=None):
                cur = not isinstance(t, int) or t < NT
                c = 1 if odd else 0
                if fill and not odd:
                    split_lo(q + 1)
                if prev:
                    out_norm(t - 1)
                if cur:
                    dve.wait_ge(s["wo_ps"], t + 1)
                    dve.wait_ge(s["xk_ld"], 16 * (q + 1))
                    v.tensor_tensor(z1[:, :], TR[:, 0, 0:D], xk[:, c, :], ALU.add).then_inc(s["z1_ok"], 1)
                    dve.wait_ge(s["z1_ok"], t + 1)
                    v.bn_stats(st1[:, :], z1[:, :]).then_inc(s["st1_ok"], 1)
                    dve.wait_ge(s["st1_ok"], t + 1)
                    apart(dve, s["wait_apart"])
                    v.bn_aggr(mv1[:, :], st1[:, :]).then_inc(s["mv1_ok"], 1)
                    dve.wait_ge(s["mv1_ok"], t + 1)
                    v.tensor_scalar(ve1[:, :], mv1[:, 1:2], EPS, None, ALU.add).then_inc(s["ve1_ok"], 1)
                if nxt:
                    bias1(t + 1, 0)
                if cur:
                    dve.wait_ge(s["rs1_ok"], t + 1)
                    need(dve, s["x1b_ok"], t)
                    need(dve, s["x1t_ps"], t)
                    v.tensor_scalar(x1[:, :], z1[:, :], mv1[:, 0:1], rs1[:, 0:1], ALU.subtract, ALU.mult
                                    ).then_inc(s["x1_ok"], 1)
                if nxt:
                    bias1(t + 1, 1)
                if prev:
                    dve.wait_ge(s["wox_ps"], t)
                    dve.wait_ge(s["x1b_ok"], t)
                    v.tensor_tensor(z2[:, :], G[:, 0, 0:D], x1b[:, 1 - c, :], ALU.add).then_inc(s["z2_ok"], 1)
                    dve.wait_ge(s["z2_ok"], t)
                    v.bn_stats(st2[:, :], z2[:, :]).then_inc(s["st2_ok"], 1)
                    dve.wait_ge(s["st2_ok"], t)
                    apart(dve, s["wait_apart"])
                    v.bn_aggr(mv2[:, :], st2[:, :]).then_inc(s["mv2_ok"], 1)
                    dve.wait_ge(s["mv2_ok"], t)
                    v.tensor_scalar(ve2[:, :], mv2[:, 1:2], EPS, None, ALU.add).then_inc(s["ve2_ok"], 1)
                if nxt:
                    max1(t + 1, 0)
                if prev:
                    dve.wait_ge(s["rs2_ok"], t)
                    need(dve, s["x2_keep"], t - 1)
                    need(dve, s["x2t_ps"], t - 1)
                    v.tensor_scalar(x2s[:, :], z2[:, :], mv2[:, 0:1], rs2[:, 0:1],
                                    ALU.subtract, ALU.mult).then_inc(s["x2_ok"], 1)
                if cur:
                    dve.wait_ge(s["q_ps"], t + 1)
                    for r in range(2):
                        rows = slice(r * S, (r + 1) * S)
                        v.tensor_scalar(qpad[rows, :, r, :], TR[rows, 0, 0:P].rearrange("p (b q) -> p b q", b=2),
                                        xbq[rows, 0:1], float(np.float32(XD ** -0.5)), ALU.add, ALU.mult
                                        ).then_inc(s["qpad_ok"], 1)
                if nxt:
                    max1(t + 1, 1)
                    sub1(t + 1, 0)
                    sub1(t + 1, 1)
                if cur:
                    mask2(t, 0)
                    mask2(t, 1)
                    max2(t, 0)
                    max2(t, 1)
                if nxt:
                    sum1(t + 1, 0)
                    recip1(t + 1, 0)
                if cur:
                    sub2(t, 0)
                if nxt:
                    sum1(t + 1, 1)
                    recip1(t + 1, 1)
                if cur:
                    sub2(t, 1)
                if nxt:
                    value_block(t + 1, 1 - c)

            split_lo(0)
            dve.wait_ge(s["wv_hi"], 1)
            v.tensor_tensor(wvlo[:, :], wvr, wvhi[:, :].bitcast(F32), ALU.subtract).then_inc(s["wv_lo"], 1)
            for n in range(4):
                dve.wait_ge(s["m_hi"], n + 1)
                src = (TR, AV)[n // 2][:, n % 2, :].rearrange("p (j n) -> p j n", j=4)
                h0 = 8 * (n // 2) + n % 2
                v.tensor_tensor(mlo[:, h0:h0 + 7:2, :], src, mhi[:, h0:h0 + 7:2, :].bitcast(F32), ALU.subtract
                                ).then_inc(s["m_lo"], 1)
            dve.wait_ge(s["c_bias"], 32)
            for hh in range(2):
                bias1(0, hh)
            for hh in range(2):
                max1(0, hh)
                sub1(0, hh)
            for hh in range(2):
                sum1(0, hh)
                recip1(0, hh)
            dve.wait_ge(s["c_small"], 160)
            dve.wait_ge(s["memset_done"], 8)
            dve.wait_ge(s["mask_add"], 1)
            value_block(0, 0)
            step(0, False, prev=False, q=0)
            step(1, True, q=0)
            with dve.Fori(1, NP - 1) as q:
                step(2 * q, False, q=q)
                step(2 * q + 1, True, q=q)
            step(NT - 2, False, fill=False, q=NP - 1)
            step(NT - 1, True, fill=False, nxt=False, q=NP - 1)
            step(NT, False, fill=False, nxt=False)

            dve.wait_ge(s["c_ffn"], 144)
            dve.wait_ge(s["lg_ps"], 1)
            v.tensor_tensor(lg[:, :], G[0:B, 1, 0:E], bp2[:, :], ALU.add).then_inc(s["lg_sb"], 1)
            dve.wait_ge(s["lg_sb"], 1)
            v.tensor_reduce(lm[:, :], lg[:, :], axis=AX, op=ALU.max, negate=True).then_inc(s["lm_ok"], 1)
            for n in range(2):
                dve.wait_ge(s["w2_ps"], 3 + n)
                v.tensor_copy(w12v[:, 4 + 2 * n:6 + 2 * n, O_W2:O_B1], AV[:, n, :].rearrange("p (e n) -> p e n", e=2)
                              ).then_inc(s["w2_sb"], 1)
            dve.wait_ge(s["pexp_ok"], 1)
            v.tensor_reduce(ls[:, :], pe_[:, :], axis=AX, op=ALU.add).then_inc(s["ls_ok"], 1)
            dve.wait_ge(s["ls_ok"], 1)
            v.reciprocal(lr[:, :], ls[:, :]).then_inc(s["lr_ok"], 1)
            dve.wait_ge(s["lr_ok"], 1)
            v.tensor_scalar(pr[:, :], pe_[:, :], lr[:, 0:1], None, ALU.mult).then_inc(s["prob_ok"], 1)
            dve.wait_ge(s["prob_ok"], 1)
            v.max(pm8[:, :], pr[:, :]).then_inc(s["pm_ok"], 1)
            dve.wait_ge(s["pm_ok"], 1)
            v.max_index(ix8[:, :], pm8[:, :], pr[:, :]).then_inc(s["ix_ok"], 1)
            dve.wait_ge(s["ix_ok"], 1)
            v.tensor_copy(ixf[:, :], ix8[:, 0:1]).then_inc(s["ixf_ok"], 1)
            for n in range(2):
                dve.wait_ge(s["b2_ps"], n + 1)
                v.tensor_tensor(w12v[:, 4 * n:4 * n + 4, O_B2:WSEL], SC[:, n, :].rearrange("p (e n) -> p e n", e=4),
                                fbo[:, :].unsqueeze(1).broadcast_to([P, 4, D]), ALU.add).then_inc(s["b2_sb"], 1)
            dve.wait_ge(s["ixt_ps"], 1)
            v.tensor_copy(sel[:, :], G[0:1, 0, 0:B]).then_inc(s["sel_ok"], 1)
            dve.wait_ge(s["sel_ok"], 1)
            dve.wait_ge(s["w2_sb"], 4)
            dve.wait_ge(s["b2_sb"], 2)

            dve.wait_ge(s["x2_keep"], NT)

            def choose(t, c):
                need(dve, s["f_ps"], t - 1)
                for b in range(2):
                    e = dve.value_load(sel[0:1, bass.ds(2 * t + b, 1)], min_val=0, max_val=E - 1)
                    v.tensor_copy(wsel[:, c, b, :], w12[:, bass.ds(e * WSEL, WSEL)]).then_inc(s["wsel_ok"], 1)

            def residual(t, c):
                dve.wait_ge(s["f_ps"], t + 1)
                cols = bass.ds(t * D, D)
                v.scalar_tensor_tensor(out=x2[:, cols], in0=TR[:, c, 0:D], scalar=0.3, in1=x2[:, cols],
                                       op0=ALU.mult, op1=ALU.add).then_inc(s["y3_ok"], 1)
                dve.wait_ge(s["y3_ok"], t + 1)
                apart(dve, s["wait_apart"])
                v.bn_stats(st3[:, :], x2[:, cols]).then_inc(s["st3_ok"], 1)
                dve.wait_ge(s["st3_ok"], t + 1)
                apart(dve, s["wait_apart"])
                v.bn_aggr(mv3[:, c, :], st3[:, :]).then_inc(s["mv3_ok"], 1)
                dve.wait_ge(s["mv3_ok"], t + 1)
                v.tensor_scalar(ve3[:, c:c + 1], mv3[:, c, 1:2], EPS, None, ALU.add).then_inc(s["ve3_ok"], 1)

            def scale(t, c):
                dve.wait_ge(s["rs3_ok"], t + 1)
                cols = bass.ds(t * D, D)
                v.tensor_scalar(x2[:, cols], x2[:, cols], mv3[:, c, 0:1], rs3[:, c:c + 1], ALU.subtract, ALU.mult
                                ).then_inc(s["out_ok"], 1)

            choose(0, 0)
            choose(1, 1)
            residual(0, 0)
            choose(2, 0)
            residual(1, 1)
            scale(0, 0)
            with dve.Fori(1, NP - 1) as q:
                choose(2 * q + 1, 1)
                residual(2 * q, 0)
                scale(2 * q - 1, 1)
                choose(2 * q + 2, 0)
                residual(2 * q + 1, 1)
                scale(2 * q, 0)
            choose(NT - 1, 1)
            residual(NT - 2, 0)
            scale(NT - 3, 1)
            residual(NT - 1, 1)
            scale(NT - 2, 0)
            scale(NT - 1, 1)

        @block.tensor
        def _(pe):
            mm = nc.tensor.matmul

            def split3(out, lhi, llo, rhi, rlo):
                mm(out, lhi, rhi, start=True, stop=False)
                mm(out, lhi, rlo, start=False, stop=False)
                return mm(out, llo, rhi, start=False, stop=True)

            def transposes(dst, src, free, done):
                for hh in range(2):
                    free(hh)
                    for j in range(4):
                        last = nc.tensor.transpose(dst[:, hh, j * P:(j + 1) * P],
                                                   src[:, 4 * hh + j, :, :].rearrange("p b k -> p (b k)"), ident[:, :])
                    last.then_inc(done, 1)

            def y_units(q, last_free, next_free):
                need(pe, s["xlo_ok"], q + 1)
                for u in range(8):
                    g = (u + 1) % 2
                    if u == 0:
                        last_free()
                    elif u == 1:
                        next_free()
                    else:
                        pe.wait_ge(s["y_sb"], 8 * q + u - 1)
                    for par in range(2):
                        last = split3(G[:, g, par * PT:(par + 1) * PT], mhi[:, 2 * u + par, :], mlo[:, 2 * u + par, :],
                                      xhi[:, :], xlo[:, :])
                    last.then_inc(s["y_ps"], 1)

            def v_units(q, last_free, next_free):
                for u in range(4):
                    g = (u + 1) % 2
                    if u == 0:
                        last_free()
                    elif u == 1:
                        next_free()
                    else:
                        pe.wait_ge(s["v_sb"], 4 * q + u - 1)
                    toks = slice((u // 2) * P, (u // 2 + 1) * P)
                    cols = slice((u % 2) * 512, (u % 2 + 1) * 512)
                    split3(G[:, g, :], xhi[:, toks], xlo[:, toks], wvhi[:, cols], wvlo[:, cols]).then_inc(s["v_ps"], 1)

            def scores1(t, c):
                for hh in range(2):
                    need(pe, s["s2_in"], 2 * t - 2 + hh - 1)
                    for j in range(0, 4, 4):
                        for b in range(2):
                            for par in range(2):
                                dst = SC[par * S:(par + 1) * S, hh, :].rearrange("p (j b k) -> p j b k", j=4, b=2)
                                last = mm(dst[:, :, b, :], xts[:, c * P + b * S:c * P + (b + 1) * S],
                                          Y[:, par, 4 * hh:4 * hh + 4, c * P + b * S:c * P + (b + 1) * S],
                                          start=True, stop=True)
                    last.then_inc(s["s1_ps"], 1)

            def kv(t, c, kt_free, v_free):
                kt_free()
                mm(G[:, 1, 0:P], xwk[:, :], ctxt[:, c * P:(c + 1) * P], start=True, stop=True).then_inc(s["kt_ps"], 1)
                v_free()
                mm(G[:, 0, 0:D], ctxt[:, c * P:(c + 1) * P], xwv[:, :], start=True, stop=True).then_inc(s["vx_ps"], 1)

            def step(t, odd, prev=True, nxt=True, fill=True, q=None):
                cur = not isinstance(t, int) or t < NT
                c = 1 if odd else 0
                if cur:
                    transposes(TR, p1, lambda hh: pe.wait_ge(s["p1_ok"], 2 * t + hh + 1), s["pt1_ps"])
                if prev:
                    def free2(hh):
                        if hh == 0:
                            pe.wait_ge(s["p2_zero"], 2 * t)
                            need(pe, s["vbd_ok"], 2 * (t + 1) if cur else 0)
                        else:
                            if cur:
                                pe.wait_ge(s["kt_sb"], t + 1)
                            need(pe, s["x2t_sb"], t - 1)
                    transposes(G, s2, free2, s["pt2_ps"])
                if cur:
                    need(pe, s["v_sb"], 2 * (t + 1))
                    for b in range(2):
                        rows = slice(b * S, (b + 1) * S)
                        for j in range(J):
                            if b == 0 and j % 4 == 0:
                                pe.wait_ge(s["pt1_sb"], 2 * t + j // 4 + 1)
                                apart(pe, s["wait_apart"])
                            for par in range(2):
                                h = 2 * j + par
                                last = mm(AV[par * S:(par + 1) * S, b, j * S:(j + 1) * S],
                                          V[rows, c, h * HD:(h + 1) * HD], pt1[rows, j, par * S:(par + 1) * S],
                                          start=True, stop=True)
                        last.then_inc(s["av_ps"], 1)
                if prev:
                    pe.wait_ge(s["pt2_sb"], 2 * t)
                    for j in range(J):
                        last = mm(G[:, 0, j * 2 * VW:(j + 1) * 2 * VW], pt2[:, j, :], vbd[:, 1 - c, j, :],
                                  start=True, stop=True)
                    last.then_inc(s["pv2_ps"], 1)
                if cur:
                    pe.wait_ge(s["at_sb"], 2 * (t + 1))
                    for j in range(J):
                        last = mm(TR[:, 0, 0:D], at[:, j, :, :].rearrange("p b q -> p (b q)"), wo[:, j, :],
                                  start=(j == 0), stop=(j == J - 1))
                    last.then_inc(s["wo_ps"], 1)
                if prev:
                    pe.wait_ge(s["on_ok"], 4 * t)
                    nc.tensor.transpose(G[:, 1, 0:P], on[:, :, :, :].rearrange("p r j d -> p (r j d)"), ident[:, :]
                                        ).then_inc(s["ot_ps"], 1)
                if nxt:
                    if not odd:
                        pass
                    else:
                        need(pe, s["xts_ok"], q + 2)
                        need(pe, s["y_sb"], 8 * (q + 2))
                    scores1(t + 1, 1 - c)
                if prev:
                    pe.wait_ge(s["ot_sb"], t)
                    mm(G[:, 0, 0:D], ot[:, :], xwo[:, :], start=True, stop=True).then_inc(s["wox_ps"], 1)
                if cur:
                    pe.wait_ge(s["x1_ok"], t + 1)
                    nc.tensor.transpose(TR[:, 1, 0:P], x1[:, :], ident[:, :]).then_inc(s["x1t_ps"], 1)
                    pe.wait_ge(s["x1t_sb"], t + 1)
                    mm(TR[:, 0, 0:P], xwq[:, :], x1t[:, :], start=True, stop=True).then_inc(s["q_ps"], 1)
                    pe.wait_ge(s["qpad_ok"], 2 * (t + 1))
                    pe.wait_ge(s["kbd_ok"], 2 * (t + 1))
                    for hh in range(2):
                        if nxt:
                            pe.wait_ge(s["s1_in"], 2 * t + 3 + hh)
                        dst = SC[:, hh, :].rearrange("p (j b k) -> p j b k", j=4, b=2)
                        for b in range(2):
                            last = mm(dst[:, :, b, :], qpad[:, b, :, :].rearrange("p r q -> p (r q)"),
                                      kbd[:, b, 4 * hh:4 * hh + 4, :], start=True, stop=True)
                        last.then_inc(s["s2_ps"], 1)

                def free_g0():
                    need(pe, s["z2_ok"], t if prev else 0)
                if fill and not odd:
                    y_units(q + 1, lambda: None, free_g0)
                    kv(t + 1, 1 - c, lambda: pe.wait_ge(s["y_sb"], 8 * (q + 1) + 7),
                       lambda: pe.wait_ge(s["y_sb"], 8 * (q + 1) + 8))
                elif fill:
                    v_units(q + 1, lambda: None, free_g0)
                    pe.wait_ge(s["ctx_ld"], 16 * (q + 2))
                    kv(t + 1, 1 - c, lambda: pe.wait_ge(s["v_sb"], 4 * (q + 1) + 3),
                       lambda: pe.wait_ge(s["v_sb"], 4 * (q + 1) + 4))
                elif nxt:
                    kv(t + 1, 1 - c, lambda: None, free_g0)
                if prev:
                    pe.wait_ge(s["x2_ok"], t)
                    if nxt:
                        pe.wait_ge(s["kt_sb"], t + 2)
                    nc.tensor.transpose(G[:, 1, 0:P], x2s[:, :], ident[:, :]).then_inc(s["x2t_ps"], 1)

            pe.wait_ge(s["c_table"], 32)
            mm(SC[0:H, 0, 0:NREL], table[:, :], onehot[:, :], start=True, stop=True).then_inc(s["rel_ps"], 1)
            pe.wait_ge(s["c_m"], 32)
            for n in range(4):
                par, j0 = n % 2, 4 * (n // 2)
                rows = slice(par * S, (par + 1) * S)
                for j in range(4):
                    last = mm((TR, AV)[n // 2][:, n % 2, j * D:(j + 1) * D], wkt[rows, j0 + j, :], wqt[rows, j0 + j, :],
                              start=True, stop=True)
                last.then_inc(s["m_ps"], 1)
            pe.wait_ge(s["m_lo"], 4)
            y_units(0, lambda: None, lambda: None)
            pe.wait_ge(s["wv_lo"], 1)
            v_units(0, lambda: pe.wait_ge(s["y_sb"], 7), lambda: pe.wait_ge(s["y_sb"], 8))
            pe.wait_ge(s["rel_sb"], 1)
            pe.wait_ge(s["xts_ok"], 1)
            scores1(0, 0)
            pe.wait_ge(s["c_small"], 160)
            pe.wait_ge(s["ctx_ld"], 16)
            kv(0, 0, lambda: pe.wait_ge(s["v_sb"], 3), lambda: pe.wait_ge(s["v_sb"], 4))
            pe.wait_ge(s["kt_sb"], 1)
            pe.wait_ge(s["vbd_ok"], 2)
            pe.wait_ge(s["c_ident"], 16)
            pe.wait_ge(s["c_wo"], 16)
            step(0, False, prev=False, q=0)
            step(1, True, q=0)
            with pe.Fori(1, NP - 1) as q:
                step(2 * q, False, q=q)
                step(2 * q + 1, True, q=q)
            step(NT - 2, False, fill=False)
            step(NT - 1, True, fill=False, nxt=False)
            step(NT, False, fill=False, nxt=False)

            pe.wait_ge(s["c_ffn"], 144)
            pe.wait_ge(s["x2t_sb"], NT)
            mm(G[:, 0, 0:B], wp1[:, :], x2t[:, S - 1::S], start=True, stop=True).then_inc(s["hid_ps"], 1)
            pe.wait_ge(s["c_w2t"], 16)

            def w2wo(n):
                for i in range(4):
                    e, f = 2 * n + i // 2, i % 2
                    last = mm((TR, AV)[n // 2][:, n % 2, i * D:(i + 1) * D], w2t[:, e, f * P:(f + 1) * P], fwo[:, :],
                              start=True, stop=True)
                last.then_inc(s["w2_ps"], 1)

            w2wo(0)
            pe.wait_ge(s["hid_sb"], 1)
            mm(G[0:B, 1, 0:E], gp[:, :], wp2[:, :], start=True, stop=True).then_inc(s["lg_ps"], 1)
            for n in range(1, 4):
                w2wo(n)
            for n in range(2):
                for i in range(4):
                    last = mm(SC[:, n, i * D:(i + 1) * D], b2t[:, 4 * n + i:4 * n + i + 1].broadcast_to([P, P]),
                              fwo[:, :], start=True, stop=True)
                last.then_inc(s["b2_ps"], 1)
            pe.wait_ge(s["ixf_ok"], 1)
            mm(G[0:1, 0, 0:B], ixf[:, :], ident[0:B, 0:B], start=True, stop=True).then_inc(s["ixt_ps"], 1)
            pe.wait_ge(s["sel_ok"], 1)
            pe.wait_ge(s["w2_sb"], 4)

            def up(t, c):
                pe.wait_ge(s["wsel_ok"], 2 * (t + 1))
                need(pe, s["h_sb"], 4 * (t - 1))
                for b in range(2):
                    for f in range(FC):
                        last = mm(G[:, c, (b * FC + f) * S:(b * FC + f + 1) * S], wsel[:, c, b, f * P:(f + 1) * P],
                                  x2t[:, bass.ds(t * P + b * S, S)], start=True, stop=True)
                last.then_inc(s["h_ps"], 1)

            def down(t, c):
                pe.wait_ge(s["h_sb"], 4 * (t + 1))
                need(pe, s["y3_ok"], t - 1)
                for b in range(2):
                    dst = TR[b * S:(b + 1) * S, c, 0:D]
                    for f in range(FC):
                        mm(dst, ht[:, c, b, f, :], wsel[:, c, b, O_W2 + f * D:O_W2 + (f + 1) * D],
                           start=(f == 0), stop=False)
                    last = mm(dst, ones[0:1, :], wsel[0:1, c, b, O_B2:WSEL], start=False, stop=True)
                last.then_inc(s["f_ps"], 1)

            up(0, 0)
            up(1, 1)
            down(0, 0)
            with pe.Fori(1, NP) as q:
                up(2 * q, 0)
                down(2 * q - 1, 1)
                up(2 * q + 1, 1)
                down(2 * q, 0)
            down(NT - 1, 1)


def bucket_rows():
    dist = np.arange(-(S - 1), S)
    nb = BUCKETS // 2
    exact = nb // 2
    out = (dist > 0).astype(np.int32) * nb
    a = np.abs(dist)
    safe = np.maximum(a, 1).astype(np.float32)
    large = exact + (np.log(safe / np.float32(exact)) / np.float32(np.log(MAX_DIST / exact))
                     * np.float32(nb - exact)).astype(np.int32)
    out += np.where(a < exact, a, np.minimum(large, nb - 1))
    return (np.arange(BUCKETS)[:, None] == out[None, :]).astype(np.float32)


def kernel(**inputs):
    import concourse.bacc as bacc
    from concourse.bass_utils import run_bass_kernel_spmd

    a = {k: np.asarray(v) for k, v in inputs.items()}
    x = a["x"].reshape(TOK, D)
    pos = np.arange(S)
    row = np.arange(P)
    arrays = {
        "x": x, "xT": x.T, "ctxT": a["ctx_1024"].reshape(TOK, D).T,
        "mask": a["mask_BxS2_bf1"].reshape(TOK).view(np.uint8),
        "WkT": a["L0_attn_Wk"].T, "WqT": a["L0_attn_Wq"].T, "Wv": a["L0_attn_Wv"], "Wo": a["L0_attn_Wo"],
        "table": a["L0_attn_rel_bias"],
        "xWqT": a["L0_xattn_W_q"].T, "xWkT": a["L0_xattn_W_k"].T, "xWvT": a["L0_xattn_W_v"].T,
        "xWoT": a["L0_xattn_W_o"].T, "xbq": a["L0_xattn_b_q"].reshape(D, 1), "xbk": a["L0_xattn_b_k"].reshape(D, 1),
        "xbv": a["L0_xattn_b_v"], "xbo": a["L0_xattn_b_o"],
        "Wp1": a["L0_ffn_Wp1"], "bp1": a["L0_ffn_bp1"].reshape(P, 1), "Wp2": a["L0_ffn_Wp2"], "bp2": a["L0_ffn_bp2"],
        "W1": a["L0_ffn_W1"], "b1T": a["L0_ffn_b1"].reshape(E, FC, P).transpose(2, 0, 1),
        "W2T": a["L0_ffn_W2"].transpose(0, 2, 1), "b2T": a["L0_ffn_b2"].T,
        "fWo": a["L0_ffn_Wo"], "fbo": a["L0_ffn_bo"],
        "onehot": bucket_rows(),
        "ident": np.eye(P, dtype=np.float32),
        "causal": np.tile((pos[:, None] >= pos[None, :]).astype(np.float32), (2, 2)),
        "headmask": ((row[:, None] // XD) % J == np.arange(J)[None, :]).astype(np.float32),
        "w0flag": np.where(row % S < S // 2, S // 2, 0).astype(np.float32).reshape(P, 1),
    }
    nc = bacc.Bacc("TRN2", target_bir_lowering=False, num_devices=1)
    arrays = {k: np.ascontiguousarray(v) for k, v in arrays.items()}
    din = {k: nc.dram_tensor(f"in_{k}", v.shape, mybir.dt.from_np(v.dtype), kind="ExternalInput").ap()
           for k, v in arrays.items()}
    out = nc.dram_tensor("out_x", (TOK, D), F32, kind="ExternalOutput").ap()
    build(nc, din, out)
    r = run_bass_kernel_spmd(nc, [{f"in_{k}": v for k, v in arrays.items()}], core_ids=[0])
    return r.results[0]["out_x"].reshape(B, S, D)
```

```python
from contextlib import ExitStack

import numpy as np

import concourse.bass as bass
from concourse import mybir

F32 = mybir.dt.float32
F32R = mybir.dt.float32r
I32 = mybir.dt.int32
U32 = mybir.dt.uint32
U8 = mybir.dt.uint8
ALU = mybir.AluOpType
ACT = mybir.ActivationFunctionType
AX = mybir.AxisListType.X

B, S, D = 32, 64, 128
TOK = B * S
P = 128
NT = TOK // P
NP = NT // 2
PT = 2 * P
H, HD = 16, 64
J = H // 2
XD = D // H
BUCKETS, MAX_DIST = 32, 128
NREL = 2 * S - 1
E, F = 8, 256
FC = F // P
EPS = 1e-5
NEG = float(np.finfo(np.float32).max) / 2
VW = 2 * XD + 1
WSEL = 2 * F + FC + D
O_W2, O_B1, O_B2 = F, 2 * F, 2 * F + FC
WS = 4
NR = NT // WS


def need(eng, sem, value):
    if isinstance(value, int) and value <= 0:
        return
    eng.wait_ge(sem, value)


def apart(eng, sem):
    eng.sem_inc(sem, 1)


def build(nc, din, out_dram):
    with ExitStack() as ctx:
        def sb(name, shape, dt=F32):
            return ctx.enter_context(nc.sbuf_tensor(name, shape, dt))

        def sem(name):
            return ctx.enter_context(nc.semaphore(name))

        SC = ctx.enter_context(nc.psum_tensor("SC", [P, 2, 512], F32))
        TR = ctx.enter_context(nc.psum_tensor("TR", [P, 2, 512], F32))
        AV = ctx.enter_context(nc.psum_tensor("AV", [P, 2, 512], F32))
        G = ctx.enter_context(nc.psum_tensor("G", [P, 2, 512], F32))

        def y_bank(u):
            return G[:, u, :] if u < 2 else AV[:, u % 2, :]

        def v_bank(u):
            return AV[:, u % 2, :]

        ident = sb("ident", [P, P])
        causal = sb("causal", [P, P])
        window = sb("window", [P, P])
        headmask = sb("headmask", [P, J])
        w0flag = sb("w0flag", [P, 1])
        ones = sb("ones", [1, S])
        onehot = sb("onehot", [BUCKETS, NREL])
        table = sb("table", [BUCKETS, H])
        rel = sb("rel", [H, NREL])
        bias = sb("bias", [P, J, S])
        maskadd = sb("maskadd", [P, TOK])
        kmask = sb("kmask", [P, TOK], U8)
        mhi = sb("mhi", [P, H, D], F32R)
        mlo = sb("mlo", [P, H, D], F32R)
        wvhi = sb("wvhi", [P, H * HD], F32R)
        wvlo = sb("wvlo", [P, H * HD], F32R)
        wo = sb("wo", [P, J, D])
        xwq = sb("xwq", [P, D])
        xwk = sb("xwk", [P, D])
        xwv = sb("xwv", [P, D])
        xwo = sb("xwo", [P, D])
        xbq = sb("xbq", [P, 1])
        xbk = sb("xbk", [P, 1])
        xbv = sb("xbv", [P, D])
        xbo = sb("xbo", [P, D])
        wp1 = sb("wp1", [D, P])
        bp1 = sb("bp1", [P, 1])
        wp2 = sb("wp2", [P, E])
        bp2 = sb("bp2", [B, E])
        w12 = sb("w12", [P, E * WSEL])
        w12v = w12[:, :].rearrange("p (e w) -> p e w", e=E)
        fwo = sb("fwo", [P, D])
        fbo = sb("fbo", [P, D])
        b2t = sb("b2t", [P, E])

        xt_in = sb("xt_in", [P, PT])
        xhi = sb("xhi", [P, PT], F32R)
        xlo = sb("xlo", [P, PT], F32R)
        xts = sb("xts", [P, PT])
        xk = sb("xk", [P, 2, D])
        ctxt = sb("ctxt", [P, PT])
        Y = sb("Y", [P, 2, J, PT])
        V = sb("V", [P, 2, H * HD])
        s1 = sb("s1", [P, J, 2, S])
        p1 = sb("p1", [P, J, 2, S])
        pt1 = sb("pt1", [P, J, P])
        at = sb("at", [P, J, 2, S])
        mx1, sm1, rc1 = (sb(n, [P, J, 2]) for n in ("mx1", "sm1", "rc1"))
        z1, x1 = sb("z1", [P, D]), sb("x1", [P, D])
        x1b = sb("x1b", [P, 2, D])
        x1t = sb("x1t", [P, D])
        qpad = sb("qpad", [P, 2, 2, S])
        ktb = sb("ktb", [P, P])
        kbd = sb("kbd", [P, 2, J, S])
        vbd = sb("vbd", [P, 2, J, 2 * VW])
        s2 = sb("s2", [P, J, 2, S])
        mx2, corr, den, rc2 = (sb(n, [P, J, 2]) for n in ("mx2", "corr", "den", "rc2"))
        pt2 = sb("pt2", [P, J, P])
        on = sb("on", [P, 2, J, XD])
        ot = sb("ot", [P, P])
        z2, x2s = sb("z2", [P, D]), sb("x2s", [P, D])
        st1, st2, st3 = (sb(n, [P, 6]) for n in ("st1", "st2", "st3"))
        mv1, mv2 = (sb(n, [P, 2]) for n in ("mv1", "mv2"))
        ve1, ve2, rs1, rs2 = (sb(n, [P, 1]) for n in ("ve1", "ve2", "rs1", "rs2"))
        mv3, ve3, rs3 = sb("mv3", [P, 2, 2]), sb("ve3", [P, 2]), sb("rs3", [P, 2])
        half = sb("half", [P, 1])
        x2 = sb("x2", [P, TOK])
        x2t = sb("x2t", [P, TOK])
        wkt = w12[:, 0:J * D].rearrange("p (j n) -> p j n", j=J)
        wqt = w12[:, J * D:2 * J * D].rearrange("p (j n) -> p j n", j=J)
        wvr = w12[:, 2 * J * D:3 * J * D]
        w2t = Y[:, :, :, :].rearrange("p a j t -> p (a j t)")[:, 0:E * F].rearrange("p (e f) -> p e f", e=E)
        wsel = sb("wsel", [P, WS, 2, WSEL])
        ht = sb("ht", [P, 2, 2, FC, S])
        gp = sb("gp", [P, B])
        lg, pe_, pr = (sb(n, [B, E]) for n in ("lg", "pexp", "prob"))
        lm, ls, lr = (sb(n, [B, 1]) for n in ("lm", "ls", "lr"))
        pm8 = sb("pm8", [B, 8])
        ix8 = sb("ix8", [B, 8], U32)
        ixf = sb("ixf", [B, 1])
        sel = sb("sel", [1, B], I32)
        scratch = nc.dram_tensor("rel_scratch", (H, S, NREL), F32).ap()

        names = """wait_apart c_ident c_table c_small c_m c_v c_wo c_x c_rel c_relst c_bias c_mask c_ffn c_w2t
            memset_done rel_ps rel_sb mask_mul mask_add m_ps m_hi m_lo wv_hi wv_lo
            xt_ld xk_ld ctx_ld xhi_ok xlo_ok xts_ok y_ps y_sb v_ps v_sb kt_ps kt_sb vx_ps vbd_ok kbd_ok
            s1_ps s1_in s1_mx s1_sub s1_exp s1_sum s1_rc p1_ok pt1_ps pt1_sb av_ps at_sb wo_ps
            z1_ok st1_ok mv1_ok ve1_ok rs1_ok x1_ok x1b_ok x1t_ps x1t_sb q_ps qpad_ok
            s2_ps s2_in s2_mx s2_sub s2_exp pt2_ps pt2_sb pv2_ps corr_ok den_ok rc2_ok on_ok ot_ps ot_sb wox_ps
            z2_ok st2_ok mv2_ok ve2_ok rs2_ok x2_ok x2_keep x2t_ps x2t_sb
            w2_ps w2_sb b2_ps b2_sb hid_ps hid_sb lg_ps lg_sb lm_ok pexp_ok ls_ok lr_ok prob_ok pm_ok ix_ok ixf_ok ixt_ps sel_ok
            wsel0_ok wsel1_ok h_ps h_sb f_ps y3_ok st3_ok mv3_ok ve3_ok rs3_ok out_ok out_st""".split()
        s = {n: sem(n) for n in names}
        block = ctx.enter_context(nc.Block())

        @block.sync
        def _(sp):
            def load_xt(q):
                need(sp, s["xts_ok"], q)
                need(sp, s["xlo_ok"], q)
                sp.dma_start(xt_in[:, :], din["xT"][:, bass.ds(q * PT, PT)]).then_inc(s["xt_ld"], 16)

            def load_ctx(q):
                need(sp, s["kt_ps"], 2 * q)
                need(sp, s["vx_ps"], 2 * q)
                sp.dma_start(ctxt[:, :], din["ctxT"][:, bass.ds(q * PT, PT)]).then_inc(s["ctx_ld"], 16)

            def load_xk(q):
                need(sp, s["z1_ok"], 2 * q)
                sp.dma_start(xk[:, :, :], din["x"][bass.ds(q * PT, PT), :].rearrange("(t p) d -> p t d", p=P)
                             ).then_inc(s["xk_ld"], 16)

            sp.dma_start(wkt, din["WkT"].rearrange("(j p) n -> p j n", p=P)).then_inc(s["c_m"], 16)
            sp.dma_start(wqt, din["WqT"].rearrange("(j p) n -> p j n", p=P)).then_inc(s["c_m"], 16)
            sp.dma_start(wvr, din["Wv"]).then_inc(s["c_v"], 16)
            load_ctx(0)
            for dst, name in ((xwq, "xWqT"), (xwk, "xWkT"), (xwv, "xWvT"), (xwo, "xWoT"), (xbq, "xbq"), (xbk, "xbk"),
                              (headmask, "headmask"), (w0flag, "w0flag")):
                sp.dma_start(dst[:, :], din[name]).then_inc(s["c_small"], 16)
            sp.dma_start(xbv[:, :], din["xbv"].partition_broadcast(P)).then_inc(s["c_small"], 16)
            sp.dma_start(xbo[:, :], din["xbo"].partition_broadcast(P)).then_inc(s["c_small"], 16)
            sp.dma_start(ident[:, :], din["ident"]).then_inc(s["c_ident"], 16)
            sp.dma_start(wo[:, :, :], din["Wo"].rearrange("(j p) n -> p j n", p=P)).then_inc(s["c_wo"], 16)
            load_xk(0)
            sp.wait_ge(s["m_ps"], 4)
            sp.wait_ge(s["wv_lo"], 1)
            sp.dma_start(w12v[:, :, 0:F], din["W1"].rearrange("e h f -> h e f")).then_inc(s["c_ffn"], 16)
            sp.dma_start(w12v[:, :, O_B1:O_B2], din["b1T"]).then_inc(s["c_ffn"], 16)
            sp.dma_start(fwo[:, :], din["fWo"]).then_inc(s["c_ffn"], 16)
            sp.dma_start(fbo[:, :], din["fbo"].partition_broadcast(P)).then_inc(s["c_ffn"], 16)
            sp.dma_start(b2t[:, :], din["b2T"]).then_inc(s["c_ffn"], 16)
            sp.dma_start(wp1[:, :], din["Wp1"]).then_inc(s["c_ffn"], 16)
            sp.dma_start(bp1[:, :], din["bp1"]).then_inc(s["c_ffn"], 16)
            sp.dma_start(wp2[:, :], din["Wp2"]).then_inc(s["c_ffn"], 16)
            sp.dma_start(bp2[:, :], din["bp2"].partition_broadcast(B)).then_inc(s["c_ffn"], 16)
            with sp.Fori(1, NP) as q:
                load_xt(q)
                load_ctx(q)
                load_xk(q)
            sp.wait_ge(s["s1_ps"], 2 * NT)
            sp.dma_start(w2t, din["W2T"].rearrange("e h f -> h e f")).then_inc(s["c_w2t"], 16)
            with sp.Fori(0, NT) as t:
                sp.wait_ge(s["out_ok"], t + 1)
                sp.dma_start(out_dram[bass.ds(t * P, P), :], x2[:, bass.ds(t * D, D)]).then_inc(s["out_st"], 16)
            sp.wait_ge(s["out_st"], 16 * NT)

        @block.scalar
        def _(act):
            A = nc.scalar.activation
            act.dma_start(table[:, :], din["table"]).then_inc(s["c_table"], 16)
            act.dma_start(onehot[:, :], din["onehot"]).then_inc(s["c_table"], 16)
            act.dma_start(xt_in[:, :], din["xT"][:, 0:PT]).then_inc(s["xt_ld"], 16)
            nc.scalar.preload_act_table(ACT.Exp)

            def split_hi(q):
                act.wait_ge(s["xt_ld"], 16 * (q + 1))
                need(act, s["v_ps"], 4 * q)
                A(xhi[:, :], xt_in[:, :], ACT.Copy).then_inc(s["xhi_ok"], 1)

            def copy_xts(q):
                need(act, s["s1_ps"], 4 * q)
                A(xts[:, :], xt_in[:, :], ACT.Copy).then_inc(s["xts_ok"], 1)

            def y_out(q, u):
                act.wait_ge(s["y_ps"], 8 * q + u + 1)
                A(Y[:, :, u, :], y_bank(u).rearrange("p (a t) -> p a t", a=2), ACT.Copy).then_inc(s["y_sb"], 1)

            def v_out(q, u):
                act.wait_ge(s["v_ps"], 4 * q + u + 1)
                A(V[:, u // 2, (u % 2) * 512:(u % 2) * 512 + 512], v_bank(u), ACT.Copy).then_inc(s["v_sb"], 1)

            def kt_out(t):
                act.wait_ge(s["kt_ps"], t + 1)
                need(act, s["kbd_ok"], 2 * t)
                A(ktb[:, :], G[:, 0, 0:P], ACT.Identity, bias=xbk[:, 0:1]).then_inc(s["kt_sb"], 1)

            def exp1(t, hh):
                act.wait_ge(s["s1_sub"], 2 * t + hh + 1)
                A(s1[:, 4 * hh:4 * hh + 4], s1[:, 4 * hh:4 * hh + 4], ACT.Exp).then_inc(s["s1_exp"], 1)

            def exp2(t, hh):
                act.wait_ge(s["s2_sub"], 2 * t + hh + 1)
                A(s2[:, 4 * hh:4 * hh + 4], s2[:, 4 * hh:4 * hh + 4], ACT.Exp).then_inc(s["s2_exp"], 1)

            def step(t, odd, prev=True, nxt=True, fill=True, q=None):
                cur = not isinstance(t, int) or t < NT
                if fill and not odd:
                    split_hi(q + 1)
                if cur:
                    for hh in range(2):
                        act.wait_ge(s["pt1_ps"], 2 * t + hh + 1)
                        A(pt1[:, 4 * hh:4 * hh + 4, :], TR[:, hh, :].rearrange("p (j n) -> p j n", j=4),
                          ACT.Copy).then_inc(s["pt1_sb"], 1)
                if prev:
                    exp2(t - 1, 0)
                    exp2(t - 1, 1)
                if not cur:
                    nc.scalar.preload_act_table(ACT.Gelu)
                if fill and not odd:
                    y_out(q + 1, 0)
                    y_out(q + 1, 1)
                    copy_xts(q + 1)
                if cur:
                    for b in range(2):
                        act.wait_ge(s["av_ps"], 2 * t + b + 1)
                        A(at[:, :, b, :], AV[:, b, :].rearrange("p (j q) -> p j q", j=J), ACT.Copy
                          ).then_inc(s["at_sb"], 1)
                if prev:
                    for hh in range(2):
                        act.wait_ge(s["pt2_ps"], 2 * t + hh - 1)
                        A(pt2[:, 4 * hh:4 * hh + 4, :], G[:, hh, :].rearrange("p (j n) -> p j n", j=4),
                          ACT.Copy).then_inc(s["pt2_sb"], 1)
                if nxt:
                    exp1(t + 1, 0)
                    exp1(t + 1, 1)
                if cur:
                    act.wait_ge(s["x1t_ps"], t + 1)
                    A(x1t[:, :], TR[:, 1, 0:P], ACT.Copy).then_inc(s["x1t_sb"], 1)
                if fill:
                    for f in range(2):
                        y_out(q + 1, 2 + f) if not odd else v_out(q + 1, f)
                if prev:
                    act.wait_ge(s["ot_ps"], t)
                    A(ot[:, :], G[:, 1, 0:P], ACT.Copy).then_inc(s["ot_sb"], 1)
                if fill:
                    for f in range(2, 4):
                        y_out(q + 1, 2 + f) if not odd else v_out(q + 1, f)
                    if not odd:
                        y_out(q + 1, 6)
                        y_out(q + 1, 7)
                if nxt:
                    kt_out(t + 1)
                if prev:
                    act.wait_ge(s["x2t_ps"], t)
                    A(x2t[:, bass.ds((t - 1) * P, P)], AV[:, 0, 0:P], ACT.Copy).then_inc(s["x2t_sb"], 1)

            act.wait_ge(s["rel_ps"], 1)
            A(rel[:, :], SC[0:H, 0, 0:NREL], ACT.Copy).then_inc(s["rel_sb"], 1)
            act.wait_ge(s["rel_sb"], 1)
            act.dma_start(scratch, rel[:, :].unsqueeze(1).broadcast_to([H, S, NREL])).then_inc(s["c_relst"], 16)
            split_hi(0)
            for n in range(4):
                act.wait_ge(s["m_ps"], n + 1)
                src = (TR, AV)[n // 2][:, n % 2, :].rearrange("p (j n) -> p j n", j=4)
                h0 = 8 * (n // 2) + n % 2
                A(mhi[:, h0:h0 + 7:2, :], src, ACT.Copy).then_inc(s["m_hi"], 1)
            copy_xts(0)
            act.wait_ge(s["c_relst"], 16)
            for par in range(2):
                act.dma_start(bias[par * S:(par + 1) * S, :, :],
                              bass.AP(scratch.tensor, par * S * NREL + S - 1,
                                      [[NREL - 1, S], [2 * S * NREL, J], [1, S]])
                              ).then_inc(s["c_bias"], 16)
            act.wait_ge(s["c_v"], 16)
            A(wvhi[:, :], wvr, ACT.Copy).then_inc(s["wv_hi"], 1)
            for u in range(8):
                y_out(0, u)
            v_out(0, 0)
            v_out(0, 1)
            exp1(0, 0)
            v_out(0, 2)
            exp1(0, 1)
            v_out(0, 3)
            act.wait_ge(s["c_small"], 160)
            kt_out(0)
            step(0, False, prev=False, q=0)
            step(1, True, q=0)
            with act.Fori(1, NP - 1) as q:
                step(2 * q, False, q=q)
                step(2 * q + 1, True, q=q)
            step(NT - 2, False, fill=False)
            step(NT - 1, True, fill=False, nxt=False)
            step(NT, False, fill=False, nxt=False)

            act.wait_ge(s["hid_ps"], 1)
            A(gp[:, :], G[:, 0, 0:B], ACT.Gelu, bias=bp1[:, 0:1]).then_inc(s["hid_sb"], 1)
            nc.scalar.preload_act_table(ACT.Exp)
            for n in range(2):
                act.wait_ge(s["w2_ps"], n + 1)
                A(w12v[:, 2 * n:2 * n + 2, O_W2:O_B1].rearrange("p e (c n) -> p e c n", c=FC),
                  TR[:, n, :].rearrange("p (e c n) -> p e c n", e=2, c=FC), ACT.Copy).then_inc(s["w2_sb"], 1)
            act.wait_ge(s["lm_ok"], 1)
            A(pe_[:, :], lg[:, :], ACT.Exp, bias=lm[:, 0:1]).then_inc(s["pexp_ok"], 1)
            nc.scalar.preload_act_table(ACT.Gelu)

            def gelus(t, w):
                c = w % 2
                act.wait_ge(s["h_ps"], t + 1)
                need(act, s["f_ps"], t - 1)
                for b in range(2):
                    for f in range(FC):
                        A(ht[:, c, b, f, :], G[:, c, (b * FC + f) * S:(b * FC + f + 1) * S], ACT.Gelu,
                          bias=wsel[:, w, b, O_B1 + f:O_B1 + f + 1]).then_inc(s["h_sb"], 1)

            def choose(t, w):
                need(act, s["f_ps"], t - WS + 1)
                e = act.value_load(sel[0:1, bass.ds(2 * t + 1, 1)], min_val=0, max_val=E - 1)
                A(wsel[:, w, 1, :], w12[:, bass.ds(e * WSEL, WSEL)], ACT.Copy).then_inc(s["wsel1_ok"], 1)

            def tile(t, w):
                if not isinstance(t, int) or t + 1 < NT:
                    gelus(t + 1, (w + 1) % WS)
                if not isinstance(t, int) or t + 3 < NT:
                    choose(t + 3, (w + 3) % WS)

            act.wait_ge(s["sel_ok"], 1)
            act.wait_ge(s["w2_sb"], 4)
            act.wait_ge(s["b2_sb"], 2)
            choose(0, 0)
            choose(1, 1)
            gelus(0, 0)
            choose(2, 2)
            for w in range(WS):
                tile(w, w)
            with act.Fori(1, NR - 1) as r:
                for w in range(WS):
                    tile(WS * r + w, w)
            for w in range(WS):
                tile(NT - WS + w, w)

        @block.gpsimd
        def _(pool):
            pl = nc.gpsimd
            pool.dma_start(causal[:, :], din["causal"]).then_inc(s["c_mask"], 16)
            pool.dma_start(window[:, :], din["window"]).then_inc(s["c_mask"], 16)
            pool.dma_start(kmask[:, :], din["mask"].partition_broadcast(P)).then_inc(s["c_mask"], 16)
            pl.memset(half[:, :], -0.5).then_inc(s["memset_done"], 1)
            pl.memset(ones[:, :], 1.0).then_inc(s["memset_done"], 1)
            pl.memset(qpad[:, :, :, :], 0.0).then_inc(s["memset_done"], 1)
            pl.memset(vbd[:, :, :, :], 0.0).then_inc(s["memset_done"], 1)
            pool.wait_ge(s["memset_done"], 4)
            for b in range(2):
                for c in range(2):
                    pl.memset(vbd[b * S:(b + 1) * S, c, :, b * VW + 2 * XD:b * VW + 2 * XD + 1], 1.0
                              ).then_inc(s["memset_done"], 1)
                    pool.wait_ge(s["memset_done"], 5 + 2 * b + c)
            pool.wait_ge(s["c_small"], 160)

            def key_block(t):
                pool.wait_ge(s["kt_sb"], t + 1)
                need(pool, s["s2_ps"], 2 * t)
                for b in range(2):
                    pl.tensor_tensor(kbd[:, b, :, :], ktb[:, b * S:(b + 1) * S].unsqueeze(1).broadcast_to([P, J, S]),
                                     headmask[:, :].unsqueeze(2).broadcast_to([P, J, S]), ALU.mult
                                     ).then_inc(s["kbd_ok"], 1)

            def normalise1(t, hh):
                pool.wait_ge(s["s1_rc"], 2 * t + hh + 1)
                need(pool, s["pt1_ps"], 2 * t)
                js = slice(4 * hh, 4 * hh + 4)
                pl.tensor_tensor(p1[:, js, :, :].rearrange("p j b k -> p (j b) k"),
                                 s1[:, js, :, :].rearrange("p j b k -> p (j b) k"),
                                 rc1[:, js, :].rearrange("p j b -> p (j b)").unsqueeze(2).broadcast_to([P, 8, S]),
                                 ALU.mult).then_inc(s["p1_ok"], 1)

            def step(t, c, prev=True, nxt=True):
                cur = not isinstance(t, int) or t < NT
                if nxt:
                    normalise1(t + 1, 0)
                if cur:
                    pool.wait_ge(s["ve1_ok"], t + 1)
                    pl.tensor_tensor(rs1[:, :], ve1[:, :], half[:, :], ALU.pow).then_inc(s["rs1_ok"], 1)
                    pool.wait_ge(s["x1_ok"], t + 1)
                    need(pool, s["z2_ok"], t - 1)
                    pl.tensor_tensor(x1b[:, c, :], x1[:, :], xbo[:, :], ALU.add).then_inc(s["x1b_ok"], 1)
                if nxt:
                    normalise1(t + 1, 1)
                if prev:
                    pool.wait_ge(s["ve2_ok"], t)
                    pl.tensor_tensor(rs2[:, :], ve2[:, :], half[:, :], ALU.pow).then_inc(s["rs2_ok"], 1)
                    pool.wait_ge(s["x2_ok"], t)
                    pl.tensor_tensor(x2[:, bass.ds((t - 1) * D, D)], x2s[:, :], x2s[:, :], ALU.add
                                     ).then_inc(s["x2_keep"], 1)
                if nxt:
                    key_block(t + 1)

            key_block(0)
            normalise1(0, 0)
            normalise1(0, 1)
            step(0, 0, prev=False)
            step(1, 1)
            with pool.Fori(1, NP - 1) as q:
                step(2 * q, 0)
                step(2 * q + 1, 1)
            step(NT - 2, 0)
            step(NT - 1, 1, nxt=False)
            step(NT, 0, nxt=False)

            def ln3(t, c):
                pool.wait_ge(s["ve3_ok"], t + 1)
                pl.tensor_tensor(rs3[:, c:c + 1], ve3[:, c:c + 1], half[:, :], ALU.pow).then_inc(s["rs3_ok"], 1)

            with pool.Fori(0, NP) as q:
                ln3(2 * q, 0)
                ln3(2 * q + 1, 1)

        @block.vector
        def _(dve):
            v = nc.vector

            def flat(x):
                return x.rearrange("p j b k -> p (j b) k")

            def wide(x, js):
                return x[:, js, :].rearrange("p j b -> p (j b)").unsqueeze(2).broadcast_to([P, 8, S])

            def bias1(t, hh):
                dve.wait_ge(s["s1_ps"], 2 * t + hh + 1)
                need(dve, s["p1_ok"], 2 * t)
                js = slice(4 * hh, 4 * hh + 4)
                v.tensor_tensor(s1[:, js, :, :], SC[:, hh, :].rearrange("p (j b k) -> p j b k", j=4, b=2),
                                bias[:, js, :].unsqueeze(2).broadcast_to([P, 4, 2, S]), ALU.add
                                ).then_inc(s["s1_in"], 1)

            def max1(t, hh):
                dve.wait_ge(s["s1_in"], 2 * t + hh + 1)
                js = slice(4 * hh, 4 * hh + 4)
                v.tensor_reduce(mx1[:, js, :].rearrange("p j b -> p (j b)"), flat(s1[:, js, :, :]), axis=AX, op=ALU.max
                                ).then_inc(s["s1_mx"], 1)

            def sub1(t, hh):
                dve.wait_ge(s["s1_mx"], 2 * t + hh + 1)
                js = slice(4 * hh, 4 * hh + 4)
                v.tensor_tensor(flat(s1[:, js, :, :]), flat(s1[:, js, :, :]), wide(mx1, js), ALU.subtract
                                ).then_inc(s["s1_sub"], 1)

            def sum1(t, hh):
                dve.wait_ge(s["s1_exp"], 2 * t + hh + 1)
                js = slice(4 * hh, 4 * hh + 4)
                v.tensor_reduce(sm1[:, js, :].rearrange("p j b -> p (j b)"), flat(s1[:, js, :, :]), axis=AX, op=ALU.add
                                ).then_inc(s["s1_sum"], 1)

            def recip1(t, hh):
                dve.wait_ge(s["s1_sum"], 2 * t + hh + 1)
                js = slice(4 * hh, 4 * hh + 4)
                v.reciprocal(rc1[:, js, :], sm1[:, js, :]).then_inc(s["s1_rc"], 1)

            def mask2(t, hh):
                dve.wait_ge(s["s2_ps"], 2 * t + hh + 1)
                need(dve, s["pt2_ps"], 2 * t)
                js = slice(4 * hh, 4 * hh + 4)
                v.tensor_tensor(s2[:, js, :, :].rearrange("p j b k -> p j (b k)"),
                                SC[:, hh, :].rearrange("p (j n) -> p j n", j=4),
                                maskadd[:, bass.ds(t * P, P)].unsqueeze(1).broadcast_to([P, 4, P]), ALU.add
                                ).then_inc(s["s2_in"], 1)

            def max2(t, hh):
                dve.wait_ge(s["s2_in"], 2 * t + hh + 1)
                js = slice(4 * hh, 4 * hh + 4)
                v.tensor_reduce(mx2[:, js, :].rearrange("p j b -> p (j b)"), flat(s2[:, js, :, :]), axis=AX, op=ALU.max
                                ).then_inc(s["s2_mx"], 1)

            def sub2(t, hh):
                dve.wait_ge(s["s2_mx"], 2 * t + hh + 1)
                js = slice(4 * hh, 4 * hh + 4)
                v.tensor_tensor(flat(s2[:, js, :, :]), flat(s2[:, js, :, :]), wide(mx2, js), ALU.subtract
                                ).then_inc(s["s2_sub"], 1)

            def value_block(t, c):
                dve.wait_ge(s["vx_ps"], t + 1)
                for b in range(2):
                    rows = slice(b * S, (b + 1) * S)
                    dst = vbd[rows, c, :, b * VW:b * VW + 2 * XD].rearrange("p j (r d) -> p r j d", r=2)
                    src = G[rows, 1, 0:D].rearrange("p (r j d) -> p r j d", r=2, j=J)
                    add = xbv[rows, :].rearrange("p (r j d) -> p r j d", r=2, j=J)
                    v.tensor_tensor(dst, src, add, ALU.add).then_inc(s["vbd_ok"], 1)

            def split_lo(q):
                dve.wait_ge(s["xhi_ok"], q + 1)
                v.tensor_tensor(xlo[:, :], xt_in[:, :], xhi[:, :].bitcast(F32), ALU.subtract).then_inc(s["xlo_ok"], 1)

            def padding(t):
                dve.wait_ge(s["s2_mx"], 2 * t + 2)
                v.tensor_scalar(corr[:, :, :], mx2[:, :, :], -NEG, w0flag[:, 0:1], ALU.is_equal, ALU.mult
                                ).then_inc(s["corr_ok"], 1)

            def out_norm(t):
                dve.wait_ge(s["pv2_ps"], t + 1)
                dve.wait_ge(s["corr_ok"], t + 1)
                o = G[:, 0, 0:J * 2 * VW].rearrange("p (j b w) -> p j b w", j=J, b=2)
                v.tensor_tensor(den[:, :, :].unsqueeze(3), o[:, :, :, 2 * XD:VW], corr[:, :, :].unsqueeze(3), ALU.add
                                ).then_inc(s["den_ok"], 1)
                dve.wait_ge(s["den_ok"], t + 1)
                v.reciprocal(rc2[:, :, :], den[:, :, :]).then_inc(s["rc2_ok"], 1)
                dve.wait_ge(s["rc2_ok"], t + 1)
                for r in range(2):
                    rows = slice(r * S, (r + 1) * S)
                    for b in range(2):
                        v.tensor_tensor(on[b * S:(b + 1) * S, r, :, :], o[rows, :, b, r * XD:(r + 1) * XD],
                                        rc2[rows, :, b].unsqueeze(2).broadcast_to([S, J, XD]), ALU.mult
                                        ).then_inc(s["on_ok"], 1)

            def step(t, odd, prev=True, nxt=True, fill=True, q=None):
                cur = not isinstance(t, int) or t < NT
                c = 1 if odd else 0
                if prev:
                    max2(t - 1, 0)
                    max2(t - 1, 1)
                if fill and not odd:
                    split_lo(q + 1)
                if prev:
                    sub2(t - 1, 0)
                if nxt:
                    bias1(t + 1, 0)
                if prev:
                    sub2(t - 1, 1)
                if nxt:
                    bias1(t + 1, 1)
                if prev:
                    padding(t - 1)
                if nxt:
                    max1(t + 1, 0)
                    max1(t + 1, 1)
                    sub1(t + 1, 0)
                    sub1(t + 1, 1)
                    sum1(t + 1, 0)
                    recip1(t + 1, 0)
                if cur:
                    dve.wait_ge(s["wo_ps"], t + 1)
                    dve.wait_ge(s["xk_ld"], 16 * (q + 1))
                    v.tensor_tensor(z1[:, :], TR[:, 0, 0:D], xk[:, c, :], ALU.add).then_inc(s["z1_ok"], 1)
                    dve.wait_ge(s["z1_ok"], t + 1)
                    v.bn_stats(st1[:, :], z1[:, :]).then_inc(s["st1_ok"], 1)
                    dve.wait_ge(s["st1_ok"], t + 1)
                    apart(dve, s["wait_apart"])
                    v.bn_aggr(mv1[:, :], st1[:, :]).then_inc(s["mv1_ok"], 1)
                    dve.wait_ge(s["mv1_ok"], t + 1)
                    v.tensor_scalar(ve1[:, :], mv1[:, 1:2], EPS, None, ALU.add).then_inc(s["ve1_ok"], 1)
                if nxt:
                    sum1(t + 1, 1)
                if cur:
                    dve.wait_ge(s["rs1_ok"], t + 1)
                    need(dve, s["x1b_ok"], t)
                    need(dve, s["x1t_ps"], t)
                    v.tensor_scalar(x1[:, :], z1[:, :], mv1[:, 0:1], rs1[:, 0:1], ALU.subtract, ALU.mult
                                    ).then_inc(s["x1_ok"], 1)
                if nxt:
                    recip1(t + 1, 1)
                if prev:
                    out_norm(t - 1)
                if cur:
                    dve.wait_ge(s["q_ps"], t + 1)
                    for r in range(2):
                        rows = slice(r * S, (r + 1) * S)
                        v.tensor_scalar(qpad[rows, :, r, :], TR[rows, 0, 0:P].rearrange("p (b q) -> p b q", b=2),
                                        xbq[rows, 0:1], float(np.float32(XD ** -0.5)), ALU.add, ALU.mult
                                        ).then_inc(s["qpad_ok"], 1)
                if prev:
                    dve.wait_ge(s["wox_ps"], t)
                    dve.wait_ge(s["x1b_ok"], t)
                    v.tensor_tensor(z2[:, :], G[:, 1, 0:D], x1b[:, 1 - c, :], ALU.add).then_inc(s["z2_ok"], 1)
                    dve.wait_ge(s["z2_ok"], t)
                    v.bn_stats(st2[:, :], z2[:, :]).then_inc(s["st2_ok"], 1)
                    dve.wait_ge(s["st2_ok"], t)
                    apart(dve, s["wait_apart"])
                    v.bn_aggr(mv2[:, :], st2[:, :]).then_inc(s["mv2_ok"], 1)
                    dve.wait_ge(s["mv2_ok"], t)
                    v.tensor_scalar(ve2[:, :], mv2[:, 1:2], EPS, None, ALU.add).then_inc(s["ve2_ok"], 1)
                if cur:
                    mask2(t, 0)
                if prev:
                    dve.wait_ge(s["rs2_ok"], t)
                    need(dve, s["x2_keep"], t - 1)
                    need(dve, s["x2t_ps"], t - 1)
                    v.tensor_scalar(x2s[:, :], z2[:, :], mv2[:, 0:1], rs2[:, 0:1],
                                    ALU.subtract, ALU.mult).then_inc(s["x2_ok"], 1)
                if cur:
                    mask2(t, 1)
                if nxt:
                    value_block(t + 1, 1 - c)

            split_lo(0)
            for n in range(4):
                dve.wait_ge(s["m_hi"], n + 1)
                src = (TR, AV)[n // 2][:, n % 2, :].rearrange("p (j n) -> p j n", j=4)
                h0 = 8 * (n // 2) + n % 2
                v.tensor_tensor(mlo[:, h0:h0 + 7:2, :], src, mhi[:, h0:h0 + 7:2, :].bitcast(F32), ALU.subtract
                                ).then_inc(s["m_lo"], 1)
            dve.wait_ge(s["wv_hi"], 1)
            v.tensor_tensor(wvlo[:, :], wvr, wvhi[:, :].bitcast(F32), ALU.subtract).then_inc(s["wv_lo"], 1)
            dve.wait_ge(s["c_mask"], 48)
            masks = maskadd[:, :].rearrange("p (t k) -> p t k", k=P)
            v.scalar_tensor_tensor(out=masks, in0=kmask[:, :].rearrange("p (t k) -> p t k", k=P), scalar=NEG,
                                   in1=causal[:, :].unsqueeze(1).broadcast_to([P, NT, P]),
                                   op0=ALU.mult, op1=ALU.mult).then_inc(s["mask_mul"], 1)
            dve.wait_ge(s["mask_mul"], 1)
            v.tensor_tensor(masks, masks, window[:, :].unsqueeze(1).broadcast_to([P, NT, P]), ALU.add
                            ).then_inc(s["mask_add"], 1)
            dve.wait_ge(s["c_bias"], 32)
            for hh in range(2):
                bias1(0, hh)
            for hh in range(2):
                max1(0, hh)
                sub1(0, hh)
            for hh in range(2):
                sum1(0, hh)
                recip1(0, hh)
            dve.wait_ge(s["c_small"], 160)
            dve.wait_ge(s["memset_done"], 8)
            dve.wait_ge(s["mask_add"], 1)
            value_block(0, 0)
            step(0, False, prev=False, q=0)
            step(1, True, q=0)
            with dve.Fori(1, NP - 1) as q:
                step(2 * q, False, q=q)
                step(2 * q + 1, True, q=q)
            step(NT - 2, False, fill=False, q=NP - 1)
            step(NT - 1, True, fill=False, nxt=False, q=NP - 1)
            step(NT, False, fill=False, nxt=False)

            dve.wait_ge(s["c_ffn"], 144)
            dve.wait_ge(s["lg_ps"], 1)
            v.tensor_tensor(lg[:, :], G[0:B, 1, 0:E], bp2[:, :], ALU.add).then_inc(s["lg_sb"], 1)
            dve.wait_ge(s["lg_sb"], 1)
            v.tensor_reduce(lm[:, :], lg[:, :], axis=AX, op=ALU.max, negate=True).then_inc(s["lm_ok"], 1)
            for n in range(2):
                dve.wait_ge(s["w2_ps"], 3 + n)
                v.tensor_copy(w12v[:, 4 + 2 * n:6 + 2 * n, O_W2:O_B1], AV[:, n, :].rearrange("p (e n) -> p e n", e=2)
                              ).then_inc(s["w2_sb"], 1)
            dve.wait_ge(s["pexp_ok"], 1)
            v.tensor_reduce(ls[:, :], pe_[:, :], axis=AX, op=ALU.add).then_inc(s["ls_ok"], 1)
            dve.wait_ge(s["ls_ok"], 1)
            v.reciprocal(lr[:, :], ls[:, :]).then_inc(s["lr_ok"], 1)
            dve.wait_ge(s["lr_ok"], 1)
            v.tensor_scalar(pr[:, :], pe_[:, :], lr[:, 0:1], None, ALU.mult).then_inc(s["prob_ok"], 1)
            dve.wait_ge(s["prob_ok"], 1)
            v.max(pm8[:, :], pr[:, :]).then_inc(s["pm_ok"], 1)
            dve.wait_ge(s["pm_ok"], 1)
            v.max_index(ix8[:, :], pm8[:, :], pr[:, :]).then_inc(s["ix_ok"], 1)
            dve.wait_ge(s["ix_ok"], 1)
            v.tensor_copy(ixf[:, :], ix8[:, 0:1]).then_inc(s["ixf_ok"], 1)
            for n in range(2):
                dve.wait_ge(s["b2_ps"], n + 1)
                v.tensor_tensor(w12v[:, 4 * n:4 * n + 4, O_B2:WSEL], SC[:, n, :].rearrange("p (e n) -> p e n", e=4),
                                fbo[:, :].unsqueeze(1).broadcast_to([P, 4, D]), ALU.add).then_inc(s["b2_sb"], 1)
            dve.wait_ge(s["ixt_ps"], 1)
            v.tensor_copy(sel[:, :], G[0:1, 0, 0:B]).then_inc(s["sel_ok"], 1)
            dve.wait_ge(s["sel_ok"], 1)
            dve.wait_ge(s["w2_sb"], 4)
            dve.wait_ge(s["b2_sb"], 2)

            dve.wait_ge(s["x2_keep"], NT)

            def choose(t, w):
                need(dve, s["f_ps"], t - WS + 1)
                e = dve.value_load(sel[0:1, bass.ds(2 * t, 1)], min_val=0, max_val=E - 1)
                v.tensor_copy(wsel[:, w, 0, :], w12[:, bass.ds(e * WSEL, WSEL)]).then_inc(s["wsel0_ok"], 1)

            def scale(t, c):
                dve.wait_ge(s["rs3_ok"], t + 1)
                cols = bass.ds(t * D, D)
                v.tensor_scalar(x2[:, cols], x2[:, cols], mv3[:, c, 0:1], rs3[:, c:c + 1], ALU.subtract, ALU.mult
                                ).then_inc(s["out_ok"], 1)

            def tile(t, w, first=False):
                c = w % 2
                dve.wait_ge(s["f_ps"], t + 1)
                cols = bass.ds(t * D, D)
                v.scalar_tensor_tensor(out=x2[:, cols], in0=TR[:, c, 0:D], scalar=0.3, in1=x2[:, cols],
                                       op0=ALU.mult, op1=ALU.add).then_inc(s["y3_ok"], 1)
                if not isinstance(t, int) or t + 3 < NT:
                    choose(t + 3, (w + 3) % WS)
                dve.wait_ge(s["y3_ok"], t + 1)
                apart(dve, s["wait_apart"])
                v.bn_stats(st3[:, :], x2[:, cols]).then_inc(s["st3_ok"], 1)
                if not first:
                    scale(t - 1, 1 - c)
                dve.wait_ge(s["st3_ok"], t + 1)
                apart(dve, s["wait_apart"])
                v.bn_aggr(mv3[:, c, :], st3[:, :]).then_inc(s["mv3_ok"], 1)
                dve.wait_ge(s["mv3_ok"], t + 1)
                v.tensor_scalar(ve3[:, c:c + 1], mv3[:, c, 1:2], EPS, None, ALU.add).then_inc(s["ve3_ok"], 1)

            choose(0, 0)
            choose(1, 1)
            choose(2, 2)
            for w in range(WS):
                tile(w, w, first=(w == 0))
            with dve.Fori(1, NR - 1) as r:
                for w in range(WS):
                    tile(WS * r + w, w)
            for w in range(WS):
                tile(NT - WS + w, w)
            scale(NT - 1, 1)

        @block.tensor
        def _(pe):
            mm = nc.tensor.matmul

            def split3(out, lhi, llo, rhi, rlo):
                mm(out, lhi, rhi, start=True, stop=False)
                mm(out, lhi, rlo, start=False, stop=False)
                return mm(out, llo, rhi, start=False, stop=True)

            def transposes(dst, src, free, done):
                for hh in range(2):
                    free(hh)
                    for j in range(4):
                        last = nc.tensor.transpose(dst[:, hh, j * P:(j + 1) * P],
                                                   src[:, 4 * hh + j, :, :].rearrange("p b k -> p (b k)"), ident[:, :])
                    last.then_inc(done, 1)

            def y_unit(q, u):
                for par in range(2):
                    last = split3(y_bank(u)[:, par * PT:(par + 1) * PT], mhi[:, 2 * u + par, :], mlo[:, 2 * u + par, :],
                                  xhi[:, :], xlo[:, :])
                last.then_inc(s["y_ps"], 1)

            def v_unit(q, u):
                toks = slice((u // 2) * P, (u // 2 + 1) * P)
                cols = slice((u % 2) * 512, (u % 2 + 1) * 512)
                split3(v_bank(u), xhi[:, toks], xlo[:, toks], wvhi[:, cols], wvlo[:, cols]).then_inc(s["v_ps"], 1)

            def unit(q, odd, f):
                if odd:
                    if f >= 2:
                        pe.wait_ge(s["v_sb"], 4 * q + f - 1)
                    v_unit(q, f)
                else:
                    if f >= 2:
                        pe.wait_ge(s["y_sb"], 8 * q + f + 1)
                    y_unit(q, f + 2)

            def scores1(t, c):
                for hh in range(2):
                    need(pe, s["s2_in"], 2 * t - 2 + hh - 1)
                    for j in range(0, 4, 4):
                        for b in range(2):
                            for par in range(2):
                                dst = SC[par * S:(par + 1) * S, hh, :].rearrange("p (j b k) -> p j b k", j=4, b=2)
                                last = mm(dst[:, :, b, :], xts[:, c * P + b * S:c * P + (b + 1) * S],
                                          Y[:, par, 4 * hh:4 * hh + 4, c * P + b * S:c * P + (b + 1) * S],
                                          start=True, stop=True)
                    last.then_inc(s["s1_ps"], 1)

            def kv(t, c, kt_free, v_free):
                kt_free()
                mm(G[:, 0, 0:P], xwk[:, :], ctxt[:, c * P:(c + 1) * P], start=True, stop=True).then_inc(s["kt_ps"], 1)
                v_free()
                mm(G[:, 1, 0:D], ctxt[:, c * P:(c + 1) * P], xwv[:, :], start=True, stop=True).then_inc(s["vx_ps"], 1)

            def step(t, odd, prev=True, nxt=True, fill=True, q=None):
                cur = not isinstance(t, int) or t < NT
                c = 1 if odd else 0
                if cur:
                    transposes(TR, p1, lambda hh: pe.wait_ge(s["p1_ok"], 2 * t + hh + 1), s["pt1_ps"])
                if nxt:
                    if odd:
                        pe.wait_ge(s["xts_ok"], q + 2)
                        pe.wait_ge(s["y_sb"], 8 * (q + 2))
                    scores1(t + 1, 1 - c)
                if fill and not odd:
                    pe.wait_ge(s["xlo_ok"], q + 2)
                    pe.wait_ge(s["kt_sb"], t + 1)
                    y_unit(q + 1, 0)
                    pe.wait_ge(s["vbd_ok"], 2 * (t + 1))
                    y_unit(q + 1, 1)
                if cur:
                    pe.wait_ge(s["v_sb"], 4 * (q + 1))
                    need(pe, s["x2t_sb"], t - 1)
                    for b in range(2):
                        rows = slice(b * S, (b + 1) * S)
                        for j in range(J):
                            if b == 0 and j % 4 == 0:
                                pe.wait_ge(s["pt1_sb"], 2 * t + j // 4 + 1)
                                apart(pe, s["wait_apart"])
                            for par in range(2):
                                h = 2 * j + par
                                last = mm(AV[par * S:(par + 1) * S, b, j * S:(j + 1) * S],
                                          V[rows, c, h * HD:(h + 1) * HD], pt1[rows, j, par * S:(par + 1) * S],
                                          start=True, stop=True)
                        last.then_inc(s["av_ps"], 1)
                if prev:
                    def free2(hh):
                        pe.wait_ge(s["s2_exp"], 2 * t + hh - 1)
                        if fill and not odd:
                            pe.wait_ge(s["y_sb"], 8 * (q + 1) + hh + 1)
                        elif cur and hh == 0:
                            pe.wait_ge(s["kt_sb"], t + 1)
                        elif cur:
                            pe.wait_ge(s["vbd_ok"], 2 * (t + 1))
                        elif hh == 1:
                            pe.wait_ge(s["z2_ok"], t - 1)
                    transposes(G, s2, free2, s["pt2_ps"])
                if cur:
                    pe.wait_ge(s["at_sb"], 2 * (t + 1))
                    for j in range(J):
                        last = mm(TR[:, 0, 0:D], at[:, j, :, :].rearrange("p b q -> p (b q)"), wo[:, j, :],
                                  start=(j == 0), stop=(j == J - 1))
                    last.then_inc(s["wo_ps"], 1)
                if prev:
                    pe.wait_ge(s["pt2_sb"], 2 * t)
                    for j in range(J):
                        last = mm(G[:, 0, j * 2 * VW:(j + 1) * 2 * VW], pt2[:, j, :], vbd[:, 1 - c, j, :],
                                  start=True, stop=True)
                    last.then_inc(s["pv2_ps"], 1)
                if fill:
                    unit(q + 1, odd, 0)
                if cur:
                    pe.wait_ge(s["x1_ok"], t + 1)
                    nc.tensor.transpose(TR[:, 1, 0:P], x1[:, :], ident[:, :]).then_inc(s["x1t_ps"], 1)
                if fill:
                    unit(q + 1, odd, 1)
                if cur:
                    pe.wait_ge(s["x1t_sb"], t + 1)
                    mm(TR[:, 0, 0:P], xwq[:, :], x1t[:, :], start=True, stop=True).then_inc(s["q_ps"], 1)
                if prev:
                    pe.wait_ge(s["on_ok"], 4 * t)
                    nc.tensor.transpose(G[:, 1, 0:P], on[:, :, :, :].rearrange("p r j d -> p (r j d)"), ident[:, :]
                                        ).then_inc(s["ot_ps"], 1)
                if fill:
                    unit(q + 1, odd, 2)
                if prev:
                    pe.wait_ge(s["ot_sb"], t)
                    mm(G[:, 1, 0:D], ot[:, :], xwo[:, :], start=True, stop=True).then_inc(s["wox_ps"], 1)
                if fill:
                    unit(q + 1, odd, 3)
                if cur:
                    pe.wait_ge(s["qpad_ok"], 2 * (t + 1))
                    pe.wait_ge(s["kbd_ok"], 2 * (t + 1))
                    for hh in range(2):
                        if nxt:
                            pe.wait_ge(s["s1_in"], 2 * t + 3 + hh)
                        dst = SC[:, hh, :].rearrange("p (j b k) -> p j b k", j=4, b=2)
                        for b in range(2):
                            last = mm(dst[:, :, b, :], qpad[:, b, :, :].rearrange("p r q -> p (r q)"),
                                      kbd[:, b, 4 * hh:4 * hh + 4, :], start=True, stop=True)
                        last.then_inc(s["s2_ps"], 1)
                if fill and not odd:
                    for u in (6, 7):
                        pe.wait_ge(s["y_sb"], 8 * (q + 1) + u - 1)
                        y_unit(q + 1, u)
                if nxt:
                    if odd:
                        pe.wait_ge(s["ctx_ld"], 16 * (q + 2))
                    kv(t + 1, 1 - c, lambda: None, lambda: need(pe, s["z2_ok"], t if prev else 0))
                if prev:
                    pe.wait_ge(s["x2_ok"], t)
                    if fill:
                        pe.wait_ge(*((s["v_sb"], 4 * (q + 1) + 3) if odd else (s["y_sb"], 8 * (q + 1) + 7)))
                    nc.tensor.transpose(AV[:, 0, 0:P], x2s[:, :], ident[:, :]).then_inc(s["x2t_ps"], 1)

            pe.wait_ge(s["c_table"], 32)
            mm(SC[0:H, 0, 0:NREL], table[:, :], onehot[:, :], start=True, stop=True).then_inc(s["rel_ps"], 1)
            pe.wait_ge(s["c_m"], 32)
            for n in range(4):
                par, j0 = n % 2, 4 * (n // 2)
                rows = slice(par * S, (par + 1) * S)
                for j in range(4):
                    last = mm((TR, AV)[n // 2][:, n % 2, j * D:(j + 1) * D], wkt[rows, j0 + j, :], wqt[rows, j0 + j, :],
                              start=True, stop=True)
                last.then_inc(s["m_ps"], 1)
            pe.wait_ge(s["xlo_ok"], 1)
            for u in range(8):
                if u == 0:
                    pe.wait_ge(s["m_lo"], 2)
                elif u == 2:
                    pe.wait_ge(s["m_lo"], 4)
                elif u >= 4:
                    pe.wait_ge(s["y_sb"], u - 1)
                y_unit(0, u)
            pe.wait_ge(s["rel_sb"], 1)
            pe.wait_ge(s["xts_ok"], 1)
            pe.wait_ge(s["y_sb"], 8)
            scores1(0, 0)
            pe.wait_ge(s["c_small"], 160)
            pe.wait_ge(s["ctx_ld"], 16)
            kv(0, 0, lambda: None, lambda: None)
            pe.wait_ge(s["wv_lo"], 1)
            for u in range(4):
                if u >= 2:
                    pe.wait_ge(s["v_sb"], u - 1)
                v_unit(0, u)
            pe.wait_ge(s["kt_sb"], 1)
            pe.wait_ge(s["vbd_ok"], 2)
            pe.wait_ge(s["c_ident"], 16)
            pe.wait_ge(s["c_wo"], 16)
            step(0, False, prev=False, q=0)
            step(1, True, q=0)
            with pe.Fori(1, NP - 1) as q:
                step(2 * q, False, q=q)
                step(2 * q + 1, True, q=q)
            step(NT - 2, False, fill=False, q=NP - 1)
            step(NT - 1, True, fill=False, nxt=False, q=NP - 1)
            step(NT, False, fill=False, nxt=False)

            pe.wait_ge(s["c_ffn"], 144)
            pe.wait_ge(s["x2t_sb"], NT)
            mm(G[:, 0, 0:B], wp1[:, :], x2t[:, S - 1::S], start=True, stop=True).then_inc(s["hid_ps"], 1)
            pe.wait_ge(s["c_w2t"], 16)

            def w2wo(n):
                for i in range(4):
                    e, f = 2 * n + i // 2, i % 2
                    last = mm((TR, AV)[n // 2][:, n % 2, i * D:(i + 1) * D], w2t[:, e, f * P:(f + 1) * P], fwo[:, :],
                              start=True, stop=True)
                last.then_inc(s["w2_ps"], 1)

            w2wo(0)
            pe.wait_ge(s["hid_sb"], 1)
            mm(G[0:B, 1, 0:E], gp[:, :], wp2[:, :], start=True, stop=True).then_inc(s["lg_ps"], 1)
            for n in range(1, 4):
                w2wo(n)
            for n in range(2):
                for i in range(4):
                    last = mm(SC[:, n, i * D:(i + 1) * D], b2t[:, 4 * n + i:4 * n + i + 1].broadcast_to([P, P]),
                              fwo[:, :], start=True, stop=True)
                last.then_inc(s["b2_ps"], 1)
            pe.wait_ge(s["ixf_ok"], 1)
            mm(G[0:1, 0, 0:B], ixf[:, :], ident[0:B, 0:B], start=True, stop=True).then_inc(s["ixt_ps"], 1)
            pe.wait_ge(s["sel_ok"], 1)
            pe.wait_ge(s["w2_sb"], 4)

            def up(t, w):
                c = w % 2
                need(pe, s["h_sb"], 4 * (t - 1))
                for b, chosen in ((0, "wsel0_ok"), (1, "wsel1_ok")):
                    pe.wait_ge(s[chosen], t + 1)
                    for f in range(FC):
                        last = mm(G[:, c, (b * FC + f) * S:(b * FC + f + 1) * S], wsel[:, w, b, f * P:(f + 1) * P],
                                  x2t[:, bass.ds(t * P + b * S, S)], start=True, stop=True)
                last.then_inc(s["h_ps"], 1)

            def down(t, w):
                c = w % 2
                pe.wait_ge(s["h_sb"], 4 * (t + 1))
                need(pe, s["y3_ok"], t - 1)
                for b in range(2):
                    dst = TR[b * S:(b + 1) * S, c, 0:D]
                    for f in range(FC):
                        mm(dst, ht[:, c, b, f, :], wsel[:, w, b, O_W2 + f * D:O_W2 + (f + 1) * D],
                           start=(f == 0), stop=False)
                    last = mm(dst, ones[0:1, :], wsel[0:1, w, b, O_B2:WSEL], start=False, stop=True)
                last.then_inc(s["f_ps"], 1)

            up(0, 0)
            for w in range(WS):
                up(w + 1, (w + 1) % WS)
                down(w, w)
            with pe.Fori(1, NR - 1) as r:
                for w in range(WS):
                    up(WS * r + w + 1, (w + 1) % WS)
                    down(WS * r + w, w)
            for w in range(WS):
                if w + 1 < WS:
                    up(NT - WS + w + 1, w + 1)
                down(NT - WS + w, w)


def bucket_rows():
    dist = np.arange(-(S - 1), S)
    nb = BUCKETS // 2
    exact = nb // 2
    out = (dist > 0).astype(np.int32) * nb
    a = np.abs(dist)
    safe = np.maximum(a, 1).astype(np.float32)
    large = exact + (np.log(safe / np.float32(exact)) / np.float32(np.log(MAX_DIST / exact))
                     * np.float32(nb - exact)).astype(np.int32)
    out += np.where(a < exact, a, np.minimum(large, nb - 1))
    return (np.arange(BUCKETS)[:, None] == out[None, :]).astype(np.float32)


def kernel(**inputs):
    import concourse.bacc as bacc
    from concourse.bass_utils import run_bass_kernel_spmd

    a = {k: np.asarray(v) for k, v in inputs.items()}
    x = a["x"].reshape(TOK, D)
    pos = np.arange(S)
    row = np.arange(P)
    arrays = {
        "x": x, "xT": x.T, "ctxT": a["ctx_1024"].reshape(TOK, D).T,
        "mask": a["mask_BxS2_bf1"].reshape(TOK).view(np.uint8),
        "WkT": a["L0_attn_Wk"].T, "WqT": a["L0_attn_Wq"].T, "Wv": a["L0_attn_Wv"], "Wo": a["L0_attn_Wo"],
        "table": a["L0_attn_rel_bias"],
        "xWqT": a["L0_xattn_W_q"].T, "xWkT": a["L0_xattn_W_k"].T, "xWvT": a["L0_xattn_W_v"].T,
        "xWoT": a["L0_xattn_W_o"].T, "xbq": a["L0_xattn_b_q"].reshape(D, 1), "xbk": a["L0_xattn_b_k"].reshape(D, 1),
        "xbv": a["L0_xattn_b_v"], "xbo": a["L0_xattn_b_o"],
        "Wp1": a["L0_ffn_Wp1"], "bp1": a["L0_ffn_bp1"].reshape(P, 1), "Wp2": a["L0_ffn_Wp2"], "bp2": a["L0_ffn_bp2"],
        "W1": a["L0_ffn_W1"], "b1T": a["L0_ffn_b1"].reshape(E, FC, P).transpose(2, 0, 1),
        "W2T": a["L0_ffn_W2"].transpose(0, 2, 1), "b2T": a["L0_ffn_b2"].T,
        "fWo": a["L0_ffn_Wo"], "fbo": a["L0_ffn_bo"],
        "onehot": bucket_rows(),
        "ident": np.eye(P, dtype=np.float32),
        "causal": np.tile((pos[:, None] >= pos[None, :]).astype(np.float32), (2, 2)),
        "window": np.tile(np.where((pos[:, None] < S // 2) & (pos[None, :] >= S // 2), -2 * NEG, -NEG
                                   ).astype(np.float32), (2, 2)),
        "headmask": ((row[:, None] // XD) % J == np.arange(J)[None, :]).astype(np.float32),
        "w0flag": np.where(row % S < S // 2, S // 2, 0).astype(np.float32).reshape(P, 1),
    }
    nc = bacc.Bacc("TRN2", target_bir_lowering=False, num_devices=1)
    arrays = {k: np.ascontiguousarray(v) for k, v in arrays.items()}
    din = {k: nc.dram_tensor(f"in_{k}", v.shape, mybir.dt.from_np(v.dtype), kind="ExternalInput").ap()
           for k, v in arrays.items()}
    out = nc.dram_tensor("out_x", (TOK, D), F32, kind="ExternalOutput").ap()
    build(nc, din, out)
    r = run_bass_kernel_spmd(nc, [{f"in_{k}": v for k, v in arrays.items()}], core_ids=[0])
    return r.results[0]["out_x"].reshape(B, S, D)
```

```python
from contextlib import ExitStack

import numpy as np

import concourse.bass as bass
from concourse import mybir

F32 = mybir.dt.float32
F32R = mybir.dt.float32r
I32 = mybir.dt.int32
U32 = mybir.dt.uint32
U8 = mybir.dt.uint8
ALU = mybir.AluOpType
ACT = mybir.ActivationFunctionType
AX = mybir.AxisListType.X

B, S, D = 32, 64, 128
TOK = B * S
P = 128
NT = TOK // P
NP = NT // 2
PT = 2 * P
H, HD = 16, 64
J = H // 2
XD = D // H
BUCKETS, MAX_DIST = 32, 128
NREL = 2 * S - 1
E, F = 8, 256
FC = F // P
EPS = 1e-5
NEG = float(np.finfo(np.float32).max) / 2
VW = 2 * XD + 1
WEXP = 2 * F + FC + D
WSEL = 2 * F + FC
O_W2, O_B1, O_B2 = F, 2 * F, 2 * F + FC
WS = 4
NR = NT // WS
GROUPS = ((0, B - 4), (B - 4, 4))


def need(eng, sem, value):
    if isinstance(value, int) and value <= 0:
        return
    eng.wait_ge(sem, value)


def apart(eng, sem):
    eng.sem_inc(sem, 1)


def build(nc, din, out_dram):
    with ExitStack() as ctx:
        def sb(name, shape, dt=F32):
            return ctx.enter_context(nc.sbuf_tensor(name, shape, dt))

        def sem(name):
            return ctx.enter_context(nc.semaphore(name))

        SC = ctx.enter_context(nc.psum_tensor("SC", [P, 2, 512], F32))
        TR = ctx.enter_context(nc.psum_tensor("TR", [P, 2, 512], F32))
        AV = ctx.enter_context(nc.psum_tensor("AV", [P, 2, 512], F32))
        G = ctx.enter_context(nc.psum_tensor("G", [P, 2, 512], F32))

        def y_bank(u):
            return G[:, u, :] if u < 2 else AV[:, u % 2, :]

        def v_bank(u):
            return AV[:, u % 2, :]

        ident = sb("ident", [P, P])
        causal = sb("causal", [P, P])
        window = sb("window", [P, P])
        headmask = sb("headmask", [P, J])
        w0flag = sb("w0flag", [P, 1])
        onehot = sb("onehot", [BUCKETS, NREL])
        table = sb("table", [BUCKETS, H])
        rel = sb("rel", [H, NREL])
        bias = sb("bias", [P, J, S])
        maskadd = sb("maskadd", [P, TOK])
        kmask = sb("kmask", [P, TOK], U8)
        mhi = sb("mhi", [P, H, D], F32R)
        mlo = sb("mlo", [P, H, D], F32R)
        wvhi = sb("wvhi", [P, H * HD], F32R)
        wvlo = sb("wvlo", [P, H * HD], F32R)
        wo = sb("wo", [P, J, D])
        xwq = sb("xwq", [P, D])
        xwk = sb("xwk", [P, D])
        xwv = sb("xwv", [P, D])
        xwo = sb("xwo", [P, D])
        xbq = sb("xbq", [P, 1])
        xbk = sb("xbk", [P, 1])
        xbv = sb("xbv", [P, D])
        xbo = sb("xbo", [P, D])
        wp1 = sb("wp1", [D, P])
        bp1 = sb("bp1", [P, 1])
        wp2 = sb("wp2", [P, E])
        bp2 = sb("bp2", [B, E])
        w12 = sb("w12", [P, E * WEXP])
        w12v = w12[:, :].rearrange("p (e w) -> p e w", e=E)
        fwo = sb("fwo", [P, D])
        fbo, fbo3 = sb("fbo", [P, D]), sb("fbo3", [P, D])
        b2t = sb("b2t", [P, E])

        xt_in = sb("xt_in", [P, PT])
        xhi = sb("xhi", [P, PT], F32R)
        xlo = sb("xlo", [P, PT], F32R)
        xts = sb("xts", [P, PT])
        xk = sb("xk", [P, 2, D])
        ctxt = sb("ctxt", [P, PT])
        Y = sb("Y", [P, 2, J, PT])
        V = sb("V", [P, 2, H * HD])
        s1 = sb("s1", [P, J, 2, S])
        p1 = sb("p1", [P, J, 2, S])
        pt1 = sb("pt1", [P, J, P])
        at = sb("at", [P, J, 2, S])
        mx1, sm1, rc1 = (sb(n, [P, J, 2]) for n in ("mx1", "sm1", "rc1"))
        z1, x1 = sb("z1", [P, D]), sb("x1", [P, D])
        x1b = sb("x1b", [P, 2, D])
        x1t = sb("x1t", [P, D])
        qpad = sb("qpad", [P, 2, 2, S])
        ktb = sb("ktb", [P, P])
        kthi, ktlo = sb("kthi", [P, P], F32R), sb("ktlo", [P, P], F32R)
        kbdhi = sb("kbdhi", [P, 2, J, S], F32R)
        kbdlo = sb("kbdlo", [P, 2, J, S], F32R)
        qhi, qlo = sb("qhi", [P, 2, 2, S], F32R), sb("qlo", [P, 2, 2, S], F32R)
        vbd = sb("vbd", [P, 2, J, 2 * VW])
        s2 = sb("s2", [P, J, 2, S])
        mx2, corr, den, rc2 = (sb(n, [P, J, 2]) for n in ("mx2", "corr", "den", "rc2"))
        pt2 = sb("pt2", [P, J, P])
        on = sb("on", [P, 2, J, XD])
        ot = sb("ot", [P, P])
        z2, x2s = sb("z2", [P, D]), sb("x2s", [P, D])
        st1, st2, st3 = (sb(n, [P, 6]) for n in ("st1", "st2", "st3"))
        mv1, mv2 = (sb(n, [P, 2]) for n in ("mv1", "mv2"))
        ve1, ve2, rs1, rs2 = (sb(n, [P, 1]) for n in ("ve1", "ve2", "rs1", "rs2"))
        mv3, ve3, rs3 = sb("mv3", [P, 2, 2]), sb("ve3", [P, 2]), sb("rs3", [P, 2])
        half = sb("half", [P, 1])
        x2 = sb("x2", [P, TOK])
        x2t = sb("x2t", [P, TOK])
        wkt = w12[:, 0:J * D].rearrange("p (j n) -> p j n", j=J)
        wqt = w12[:, J * D:2 * J * D].rearrange("p (j n) -> p j n", j=J)
        wvr = w12[:, 2 * J * D:3 * J * D]
        w2t = Y[:, :, :, :].rearrange("p a j t -> p (a j t)")[:, 0:E * F].rearrange("p (e f) -> p e f", e=E)
        wsel = sb("wsel", [P, WS, 2, WSEL])
        ht = sb("ht", [P, 2, 2, FC, S])
        gp = sb("gp", [P, B])
        lg, pe_, pr = (sb(n, [B, E]) for n in ("lg", "pexp", "prob"))
        lm, ls, lr = (sb(n, [B, 1]) for n in ("lm", "ls", "lr"))
        pm8 = sb("pm8", [B, 8])
        ix8 = sb("ix8", [B, 8], U32)
        ixw, ixr = sb("ixw", [B, B]), sb("ixr", [B, B])
        sel = sb("sel", [1, B], I32)
        scratch = nc.dram_tensor("rel_scratch", (H, S, NREL), F32).ap()

        names = """wait_apart c_ident c_table c_small c_m c_v c_wo c_x c_rel c_relst c_bias c_mask c_ffn c_w2t
            memset_done rel_ps rel_sb mask_mul mask_add m_ps m_hi m_lo wv_hi wv_lo
            xt_ld xk_ld ctx_ld xhi_ok xlo_ok xts_ok y_ps y_sb v_ps v_sb kt_ps kt_sb kthi_ok ktlo_ok vx_ps vbd_ok kbd_ok
            s1_ps s1_in s1_mx s1_sub s1_exp s1_sum s1_rc p1_ok pt1_ps pt1_sb av_ps at_sb wo_ps
            z1_ok st1_ok mv1_ok ve1_ok rs1_ok x1_ok x1b_ok x1t_ps x1t_sb q_ps qpad_ok qhi_ok qlo_ok
            s2_ps s2_in s2_mx s2_sub s2_exp pt2_ps pt2_sb pv2_ps corr_ok den_ok rc2_ok on_ok ot_ps ot_sb wox_ps
            z2_ok st2_ok mv2_ok ve2_ok rs2_ok x2_ok x2_keep x2t_ps x2t_sb
            w2_ps w2_sb b2_ps fbo3_ok b2_sb b2_add0 b2_add1 hid_ps hid_sb lg_ps lg_sb lm_ok pexp_ok ls_ok lr_ok prob_ok pm_ok ix_ok ixw0_ok ixw_ok ixr_ok sel_ok
            wsel0_ok wsel1_ok h_ps h_sb f_ps y3_ok st3_ok mv3_ok ve3_ok rs3_ok out_ok out_st""".split()
        s = {n: sem(n) for n in names}
        block = ctx.enter_context(nc.Block())

        @block.sync
        def _(sp):
            def load_xt(q):
                need(sp, s["xts_ok"], q)
                need(sp, s["xlo_ok"], q)
                sp.dma_start(xt_in[:, :], din["xT"][:, bass.ds(q * PT, PT)]).then_inc(s["xt_ld"], 16)

            def load_ctx(q):
                need(sp, s["kt_ps"], 2 * q)
                need(sp, s["vx_ps"], 2 * q)
                sp.dma_start(ctxt[:, :], din["ctxT"][:, bass.ds(q * PT, PT)]).then_inc(s["ctx_ld"], 16)

            def load_xk(q):
                need(sp, s["z1_ok"], 2 * q)
                sp.dma_start(xk[:, :, :], din["x"][bass.ds(q * PT, PT), :].rearrange("(t p) d -> p t d", p=P)
                             ).then_inc(s["xk_ld"], 16)

            sp.dma_start(wkt, din["WkT"].rearrange("(j p) n -> p j n", p=P)).then_inc(s["c_m"], 16)
            sp.dma_start(wqt, din["WqT"].rearrange("(j p) n -> p j n", p=P)).then_inc(s["c_m"], 16)
            sp.dma_start(wvr, din["Wv"]).then_inc(s["c_v"], 16)
            load_ctx(0)
            for dst, name in ((xwq, "xWqT"), (xwk, "xWkT"), (xwv, "xWvT"), (xwo, "xWoT"), (xbq, "xbq"), (xbk, "xbk"),
                              (headmask, "headmask"), (w0flag, "w0flag")):
                sp.dma_start(dst[:, :], din[name]).then_inc(s["c_small"], 16)
            sp.dma_start(xbv[:, :], din["xbv"].partition_broadcast(P)).then_inc(s["c_small"], 16)
            sp.dma_start(xbo[:, :], din["xbo"].partition_broadcast(P)).then_inc(s["c_small"], 16)
            sp.dma_start(ident[:, :], din["ident"]).then_inc(s["c_ident"], 16)
            sp.dma_start(wo[:, :, :], din["Wo"].rearrange("(j p) n -> p j n", p=P)).then_inc(s["c_wo"], 16)
            load_xk(0)
            sp.wait_ge(s["m_ps"], 4)
            sp.wait_ge(s["wv_lo"], 1)
            sp.dma_start(w12v[:, :, 0:F], din["W1"].rearrange("e h f -> h e f")).then_inc(s["c_ffn"], 16)
            sp.dma_start(w12v[:, :, O_B1:O_B2], din["b1T"]).then_inc(s["c_ffn"], 16)
            sp.dma_start(fwo[:, :], din["fWo"]).then_inc(s["c_ffn"], 16)
            sp.dma_start(fbo[:, :], din["fbo"].partition_broadcast(P)).then_inc(s["c_ffn"], 16)
            sp.dma_start(b2t[:, :], din["b2T"]).then_inc(s["c_ffn"], 16)
            sp.dma_start(wp1[:, :], din["Wp1"]).then_inc(s["c_ffn"], 16)
            sp.dma_start(bp1[:, :], din["bp1"]).then_inc(s["c_ffn"], 16)
            sp.dma_start(wp2[:, :], din["Wp2"]).then_inc(s["c_ffn"], 16)
            sp.dma_start(bp2[:, :], din["bp2"].partition_broadcast(B)).then_inc(s["c_ffn"], 16)
            with sp.Fori(1, NP) as q:
                load_xt(q)
                load_ctx(q)
                load_xk(q)
            sp.wait_ge(s["s1_ps"], 2 * NT)
            sp.dma_start(w2t, din["W2T"].rearrange("e h f -> h e f")).then_inc(s["c_w2t"], 16)
            with sp.Fori(0, NT) as t:
                sp.wait_ge(s["out_ok"], t + 1)
                sp.dma_start(out_dram[bass.ds(t * P, P), :], x2[:, bass.ds(t * D, D)]).then_inc(s["out_st"], 16)
            sp.wait_ge(s["out_st"], 16 * NT)

        @block.scalar
        def _(act):
            A = nc.scalar.activation
            act.dma_start(table[:, :], din["table"]).then_inc(s["c_table"], 16)
            act.dma_start(onehot[:, :], din["onehot"]).then_inc(s["c_table"], 16)
            act.dma_start(xt_in[:, :], din["xT"][:, 0:PT]).then_inc(s["xt_ld"], 16)
            nc.scalar.preload_act_table(ACT.Exp)

            def split_hi(q):
                act.wait_ge(s["xt_ld"], 16 * (q + 1))
                need(act, s["v_ps"], 4 * q)
                A(xhi[:, :], xt_in[:, :], ACT.Copy).then_inc(s["xhi_ok"], 1)

            def copy_xts(q):
                need(act, s["s1_ps"], 4 * q)
                A(xts[:, :], xt_in[:, :], ACT.Copy).then_inc(s["xts_ok"], 1)

            def y_out(q, u):
                act.wait_ge(s["y_ps"], 8 * q + u + 1)
                A(Y[:, :, u, :], y_bank(u).rearrange("p (a t) -> p a t", a=2), ACT.Copy).then_inc(s["y_sb"], 1)

            def v_out(q, u):
                act.wait_ge(s["v_ps"], 4 * q + u + 1)
                A(V[:, u // 2, (u % 2) * 512:(u % 2) * 512 + 512], v_bank(u), ACT.Copy).then_inc(s["v_sb"], 1)

            def kt_out(t):
                act.wait_ge(s["kt_ps"], t + 1)
                need(act, s["kbd_ok"], 4 * t)
                A(ktb[:, :], G[:, 0, 0:P], ACT.Identity, bias=xbk[:, 0:1]).then_inc(s["kt_sb"], 1)
                act.wait_ge(s["kt_sb"], t + 1)
                A(kthi[:, :], ktb[:, :], ACT.Copy).then_inc(s["kthi_ok"], 1)

            def q_hi(t):
                act.wait_ge(s["qpad_ok"], 2 * (t + 1))
                A(qhi[:, :, :, :], qpad[:, :, :, :], ACT.Copy).then_inc(s["qhi_ok"], 1)

            def exp1(t, hh):
                act.wait_ge(s["s1_sub"], 2 * t + hh + 1)
                A(s1[:, 4 * hh:4 * hh + 4], s1[:, 4 * hh:4 * hh + 4], ACT.Exp).then_inc(s["s1_exp"], 1)

            def exp2(t, hh):
                act.wait_ge(s["s2_sub"], 2 * t + hh + 1)
                A(s2[:, 4 * hh:4 * hh + 4], s2[:, 4 * hh:4 * hh + 4], ACT.Exp).then_inc(s["s2_exp"], 1)

            def pt2_out(t):
                for hh in range(2):
                    act.wait_ge(s["pt2_ps"], 2 * t + hh + 1)
                    A(pt2[:, 4 * hh:4 * hh + 4, :], G[:, hh, :].rearrange("p (j n) -> p j n", j=4), ACT.Copy
                      ).then_inc(s["pt2_sb"], 1)

            def ot_out(t):
                act.wait_ge(s["ot_ps"], t + 1)
                A(ot[:, :], G[:, 1, 0:P], ACT.Copy).then_inc(s["ot_sb"], 1)

            def x2t_out(t, bank):
                act.wait_ge(s["x2t_ps"], t + 1)
                A(x2t[:, bass.ds(t * P, P)], bank[:, 0:P], ACT.Copy).then_inc(s["x2t_sb"], 1)

            def w2_out(n):
                act.wait_ge(s["w2_ps"], n + 1)
                A(w12v[:, 2 * n:2 * n + 2, O_W2:O_B1].rearrange("p e (c n) -> p e c n", c=FC),
                  AV[:, n % 2, :].rearrange("p (e c n) -> p e c n", e=2, c=FC), ACT.Copy).then_inc(s["w2_sb"], 1)

            def route_gelu(g, bank):
                n = GROUPS[g][1]
                act.wait_ge(s["hid_ps"], g + 1)
                A(gp[:, 0:n], bank[:, 0:n], ACT.Gelu, bias=bp1[:, 0:1]).then_inc(s["hid_sb"], 1)

            def route_exp(g):
                n = GROUPS[g][1]
                act.wait_ge(s["lm_ok"], g + 1)
                A(pe_[0:n, :], lg[0:n, :], ACT.Exp, bias=lm[0:n, 0:1]).then_inc(s["pexp_ok"], 1)

            def step(t, odd, prev=True, nxt=True, fill=True, q=None, final=False):
                if fill and not odd:
                    split_hi(q + 1)
                for hh in range(2):
                    act.wait_ge(s["pt1_ps"], 2 * t + hh + 1)
                    A(pt1[:, 4 * hh:4 * hh + 4, :], TR[:, hh, :].rearrange("p (j n) -> p j n", j=4),
                      ACT.Copy).then_inc(s["pt1_sb"], 1)
                if not isinstance(t, int) or t >= 2:
                    x2t_out(t - 2, AV[:, 0, :])
                if prev:
                    exp2(t - 1, 0)
                    exp2(t - 1, 1)
                if fill and not odd:
                    y_out(q + 1, 0)
                    y_out(q + 1, 1)
                    copy_xts(q + 1)
                for b in range(2):
                    act.wait_ge(s["av_ps"], 2 * t + b + 1)
                    A(at[:, :, b, :], AV[:, b, :].rearrange("p (j q) -> p j q", j=J), ACT.Copy
                      ).then_inc(s["at_sb"], 1)
                if nxt and not odd:
                    exp1(t + 1, 0)
                if prev:
                    pt2_out(t - 1)
                if final:
                    nc.scalar.preload_act_table(ACT.Gelu)
                    route_gelu(0, SC[:, 1, :])
                    nc.scalar.preload_act_table(ACT.Exp)
                if nxt and odd:
                    exp1(t + 1, 0)
                if nxt:
                    exp1(t + 1, 1)
                act.wait_ge(s["x1t_ps"], t + 1)
                A(x1t[:, :], TR[:, 1, 0:P], ACT.Copy).then_inc(s["x1t_sb"], 1)
                if fill:
                    for f in range(2):
                        y_out(q + 1, 2 + f) if not odd else v_out(q + 1, f)
                elif final:
                    w2_out(0)
                    w2_out(1)
                if prev:
                    ot_out(t - 1)
                q_hi(t)
                if fill:
                    for f in range(2, 4):
                        y_out(q + 1, 2 + f) if not odd else v_out(q + 1, f)
                    if not odd:
                        y_out(q + 1, 6)
                        y_out(q + 1, 7)
                elif final:
                    route_exp(0)
                    w2_out(2)
                    w2_out(3)
                if nxt:
                    kt_out(t + 1)

            act.wait_ge(s["rel_ps"], 1)
            A(rel[:, :], SC[0:H, 0, 0:NREL], ACT.Copy).then_inc(s["rel_sb"], 1)
            act.wait_ge(s["rel_sb"], 1)
            act.dma_start(scratch, rel[:, :].unsqueeze(1).broadcast_to([H, S, NREL])).then_inc(s["c_relst"], 16)
            split_hi(0)
            for n in range(4):
                act.wait_ge(s["m_ps"], n + 1)
                src = (TR, AV)[n // 2][:, n % 2, :].rearrange("p (j n) -> p j n", j=4)
                h0 = 8 * (n // 2) + n % 2
                A(mhi[:, h0:h0 + 7:2, :], src, ACT.Copy).then_inc(s["m_hi"], 1)
            copy_xts(0)
            act.wait_ge(s["c_relst"], 16)
            for par in range(2):
                act.dma_start(bias[par * S:(par + 1) * S, :, :],
                              bass.AP(scratch.tensor, par * S * NREL + S - 1,
                                      [[NREL - 1, S], [2 * S * NREL, J], [1, S]])
                              ).then_inc(s["c_bias"], 16)
            act.wait_ge(s["c_v"], 16)
            A(wvhi[:, :], wvr, ACT.Copy).then_inc(s["wv_hi"], 1)
            for u in range(8):
                y_out(0, u)
            v_out(0, 0)
            v_out(0, 1)
            exp1(0, 0)
            v_out(0, 2)
            exp1(0, 1)
            v_out(0, 3)
            act.wait_ge(s["c_small"], 160)
            kt_out(0)
            step(0, False, prev=False, q=0)
            step(1, True, q=0)
            with act.Fori(1, NP - 1) as q:
                step(2 * q, False, q=q)
                step(2 * q + 1, True, q=q)
            step(NT - 2, False, fill=False)
            step(NT - 1, True, fill=False, nxt=False, final=True)

            def gelus(t, w):
                c = w % 2
                act.wait_ge(s["h_ps"], t + 1)
                need(act, s["f_ps"], t - 1)
                for b in range(2):
                    for f in range(FC):
                        A(ht[:, c, b, f, :], TR[:, c, (b * FC + f) * S:(b * FC + f + 1) * S], ACT.Gelu,
                          bias=wsel[:, w, b, O_B1 + f:O_B1 + f + 1]).then_inc(s["h_sb"], 1)

            def choose(t, w):
                need(act, s["f_ps"], t - WS + 1)
                e = act.value_load(sel[0:1, bass.ds(2 * t + 1, 1)], min_val=0, max_val=E - 1)
                A(wsel[:, w, 1, :], w12[:, bass.ds(e * WEXP, WSEL)], ACT.Copy).then_inc(s["wsel1_ok"], 1)

            def tile(t, w):
                if not isinstance(t, int) or t + 2 < NT:
                    gelus(t + 2, (w + 2) % WS)
                if not isinstance(t, int) or t + WS < NT:
                    choose(t + WS, w)

            x2t_out(NT - 2, AV[:, 0, :])
            act.wait_ge(s["sel_ok"], 1)
            act.wait_ge(s["c_ffn"], 144)
            act.wait_ge(s["w2_sb"], 4)
            act.wait_ge(s["b2_sb"], 2)
            choose(0, 0)
            choose(1, 1)
            choose(2, 2)
            exp2(NT - 1, 0)
            exp2(NT - 1, 1)
            nc.scalar.preload_act_table(ACT.Gelu)
            gelus(0, 0)
            pt2_out(NT - 1)
            gelus(1, 1)
            choose(3, 3)
            tile(0, 0)
            ot_out(NT - 1)
            tile(1, 1)
            tile(2, 2)
            x2t_out(NT - 1, G[:, 1, :])
            gelus(5, 1)
            route_gelu(1, AV[:, 0, :])
            nc.scalar.preload_act_table(ACT.Exp)
            choose(7, 3)
            route_exp(1)
            nc.scalar.preload_act_table(ACT.Gelu)
            with act.Fori(1, NR - 1) as r:
                for w in range(WS):
                    if w == 1:
                        act.wait_ge(s["sel_ok"], 2)
                    tile(WS * r + w, w)
            for w in range(WS):
                tile(NT - WS + w, w)

        @block.gpsimd
        def _(pool):
            pl = nc.gpsimd
            pool.dma_start(causal[:, :], din["causal"]).then_inc(s["c_mask"], 16)
            pool.dma_start(window[:, :], din["window"]).then_inc(s["c_mask"], 16)
            pool.dma_start(kmask[:, :], din["mask"].partition_broadcast(P)).then_inc(s["c_mask"], 16)
            pl.memset(half[:, :], -0.5).then_inc(s["memset_done"], 1)
            pl.memset(qpad[:, :, :, :], 0.0).then_inc(s["memset_done"], 1)
            pl.memset(vbd[:, :, :, :], 0.0).then_inc(s["memset_done"], 1)
            pool.wait_ge(s["memset_done"], 3)
            for b in range(2):
                for c in range(2):
                    pl.memset(vbd[b * S:(b + 1) * S, c, :, b * VW + 2 * XD:b * VW + 2 * XD + 1], 1.0
                              ).then_inc(s["memset_done"], 1)
                    pool.wait_ge(s["memset_done"], 4 + 2 * b + c)
            pool.wait_ge(s["c_small"], 160)

            def key_block(t):
                pool.wait_ge(s["kthi_ok"], t + 1)
                pl.tensor_tensor(ktlo[:, :], ktb[:, :], kthi[:, :].bitcast(F32), ALU.subtract).then_inc(s["ktlo_ok"], 1)
                need(pool, s["s2_ps"], 2 * t)
                for part, block, ok in ((kthi, kbdhi, "kthi_ok"), (ktlo, kbdlo, "ktlo_ok")):
                    pool.wait_ge(s[ok], t + 1)
                    for b in range(2):
                        pl.tensor_tensor(block[:, b, :, :],
                                         part[:, b * S:(b + 1) * S].bitcast(F32).unsqueeze(1).broadcast_to([P, J, S]),
                                         headmask[:, :].unsqueeze(2).broadcast_to([P, J, S]), ALU.mult
                                         ).then_inc(s["kbd_ok"], 1)

            def normalise1(t, hh):
                pool.wait_ge(s["s1_rc"], 2 * t + hh + 1)
                need(pool, s["pt1_ps"], 2 * t)
                js = slice(4 * hh, 4 * hh + 4)
                pl.tensor_tensor(p1[:, js, :, :].rearrange("p j b k -> p (j b) k"),
                                 s1[:, js, :, :].rearrange("p j b k -> p (j b) k"),
                                 rc1[:, js, :].rearrange("p j b -> p (j b)").unsqueeze(2).broadcast_to([P, 8, S]),
                                 ALU.mult).then_inc(s["p1_ok"], 1)

            def scale2(t):
                pool.wait_ge(s["ve2_ok"], t + 1)
                pl.tensor_tensor(rs2[:, :], ve2[:, :], half[:, :], ALU.pow).then_inc(s["rs2_ok"], 1)
                pool.wait_ge(s["x2_ok"], t + 1)
                pl.tensor_tensor(x2[:, bass.ds(t * D, D)], x2s[:, :], x2s[:, :], ALU.add).then_inc(s["x2_keep"], 1)

            def step(t, c, prev=True, nxt=True, q=None):
                if q is not None and c == 0:
                    pool.wait_ge(s["xhi_ok"], q + 2)
                    pl.tensor_tensor(xlo[:, :], xt_in[:, :], xhi[:, :].bitcast(F32), ALU.subtract
                                     ).then_inc(s["xlo_ok"], 1)
                key_block(t)
                pool.wait_ge(s["ve1_ok"], t + 1)
                pl.tensor_tensor(rs1[:, :], ve1[:, :], half[:, :], ALU.pow).then_inc(s["rs1_ok"], 1)
                pool.wait_ge(s["x1_ok"], t + 1)
                need(pool, s["z2_ok"], t - 1)
                pl.tensor_tensor(x1b[:, c, :], x1[:, :], xbo[:, :], ALU.add).then_inc(s["x1b_ok"], 1)
                if nxt:
                    normalise1(t + 1, 0)
                    normalise1(t + 1, 1)
                if prev:
                    scale2(t - 1)
            def add_bias(t):
                e = pool.value_load(sel[0:1, bass.ds(2 * t + 1, 1)], min_val=0, max_val=E - 1)
                rows, cols = slice(S, P), bass.ds(t * D, D)
                need(pool, s["rs3_ok"], t - 2)
                apart(pool, s["wait_apart"])
                pl.tensor_tensor(x2[rows, cols], x2[rows, cols], w12[rows, bass.ds(e * WEXP + O_B2, D)], ALU.add
                                 ).then_inc(s["b2_add1"], 1)
                pool.wait_ge(s["b2_add1"], t + 1)
                apart(pool, s["wait_apart"])

            def ln3(t, c):
                pool.wait_ge(s["ve3_ok"], t + 1)
                pl.tensor_tensor(rs3[:, c:c + 1], ve3[:, c:c + 1], half[:, :], ALU.pow).then_inc(s["rs3_ok"], 1)

            normalise1(0, 0)
            normalise1(0, 1)
            step(0, 0, prev=False, q=0)
            step(1, 1)
            with pool.Fori(1, NP - 1) as q:
                step(2 * q, 0, q=q)
                step(2 * q + 1, 1)
            step(NT - 2, 0)
            step(NT - 1, 1, nxt=False)
            pool.wait_ge(s["b2_sb"], 2)
            pool.wait_ge(s["sel_ok"], 1)
            pool.wait_ge(s["x2_keep"], NT - 1)
            add_bias(0)
            add_bias(1)
            add_bias(2)
            ln3(0, 0)
            scale2(NT - 1)
            pool.wait_ge(s["x2_keep"], NT)
            add_bias(3)
            ln3(1, 1)
            with pool.Fori(2, NP - 1) as q:
                add_bias(2 * q)
                ln3(2 * q - 2, 0)
                add_bias(2 * q + 1)
                ln3(2 * q - 1, 1)
            pool.wait_ge(s["sel_ok"], 2)
            for q in range(NP - 1, NP + 1):
                for c in range(2):
                    if q < NP:
                        add_bias(2 * q + c)
                    ln3(2 * q - 2 + c, c)

        @block.vector
        def _(dve):
            v = nc.vector

            def flat(x):
                return x.rearrange("p j b k -> p (j b) k")

            def wide(x, js):
                return x[:, js, :].rearrange("p j b -> p (j b)").unsqueeze(2).broadcast_to([P, 8, S])

            def bias1(t, hh):
                dve.wait_ge(s["s1_ps"], 2 * t + hh + 1)
                need(dve, s["p1_ok"], 2 * t)
                js = slice(4 * hh, 4 * hh + 4)
                v.tensor_tensor(s1[:, js, :, :], SC[:, hh, :].rearrange("p (j b k) -> p j b k", j=4, b=2),
                                bias[:, js, :].unsqueeze(2).broadcast_to([P, 4, 2, S]), ALU.add
                                ).then_inc(s["s1_in"], 1)

            def max1(t, hh):
                dve.wait_ge(s["s1_in"], 2 * t + hh + 1)
                js = slice(4 * hh, 4 * hh + 4)
                v.tensor_reduce(mx1[:, js, :].rearrange("p j b -> p (j b)"), flat(s1[:, js, :, :]), axis=AX, op=ALU.max
                                ).then_inc(s["s1_mx"], 1)

            def sub1(t, hh):
                dve.wait_ge(s["s1_mx"], 2 * t + hh + 1)
                js = slice(4 * hh, 4 * hh + 4)
                v.tensor_tensor(flat(s1[:, js, :, :]), flat(s1[:, js, :, :]), wide(mx1, js), ALU.subtract
                                ).then_inc(s["s1_sub"], 1)

            def sum1(t, hh):
                dve.wait_ge(s["s1_exp"], 2 * t + hh + 1)
                js = slice(4 * hh, 4 * hh + 4)
                v.tensor_reduce(sm1[:, js, :].rearrange("p j b -> p (j b)"), flat(s1[:, js, :, :]), axis=AX, op=ALU.add
                                ).then_inc(s["s1_sum"], 1)

            def recip1(t, hh):
                dve.wait_ge(s["s1_sum"], 2 * t + hh + 1)
                js = slice(4 * hh, 4 * hh + 4)
                v.reciprocal(rc1[:, js, :], sm1[:, js, :]).then_inc(s["s1_rc"], 1)

            def mask2(t, hh):
                dve.wait_ge(s["s2_ps"], 2 * t + hh + 1)
                need(dve, s["pt2_ps"], 2 * t)
                js = slice(4 * hh, 4 * hh + 4)
                v.tensor_tensor(s2[:, js, :, :].rearrange("p j b k -> p j (b k)"),
                                SC[:, hh, :].rearrange("p (j n) -> p j n", j=4),
                                maskadd[:, bass.ds(t * P, P)].unsqueeze(1).broadcast_to([P, 4, P]), ALU.add
                                ).then_inc(s["s2_in"], 1)

            def max2(t, hh):
                dve.wait_ge(s["s2_in"], 2 * t + hh + 1)
                js = slice(4 * hh, 4 * hh + 4)
                v.tensor_reduce(mx2[:, js, :].rearrange("p j b -> p (j b)"), flat(s2[:, js, :, :]), axis=AX, op=ALU.max
                                ).then_inc(s["s2_mx"], 1)

            def sub2(t, hh):
                dve.wait_ge(s["s2_mx"], 2 * t + hh + 1)
                js = slice(4 * hh, 4 * hh + 4)
                v.tensor_tensor(flat(s2[:, js, :, :]), flat(s2[:, js, :, :]), wide(mx2, js), ALU.subtract
                                ).then_inc(s["s2_sub"], 1)

            def value_block(t, c):
                dve.wait_ge(s["vx_ps"], t + 1)
                for b in range(2):
                    rows = slice(b * S, (b + 1) * S)
                    dst = vbd[rows, c, :, b * VW:b * VW + 2 * XD].rearrange("p j (r d) -> p r j d", r=2)
                    src = G[rows, 1, 0:D].rearrange("p (r j d) -> p r j d", r=2, j=J)
                    add = xbv[rows, :].rearrange("p (r j d) -> p r j d", r=2, j=J)
                    v.tensor_tensor(dst, src, add, ALU.add).then_inc(s["vbd_ok"], 1)

            def padding(t):
                dve.wait_ge(s["s2_mx"], 2 * t + 2)
                v.tensor_scalar(corr[:, :, :], mx2[:, :, :], -NEG, w0flag[:, 0:1], ALU.is_equal, ALU.mult
                                ).then_inc(s["corr_ok"], 1)

            def out_norm(t):
                dve.wait_ge(s["pv2_ps"], t + 1)
                dve.wait_ge(s["corr_ok"], t + 1)
                o = G[:, 0, 0:J * 2 * VW].rearrange("p (j b w) -> p j b w", j=J, b=2)
                v.tensor_tensor(den[:, :, :].unsqueeze(3), o[:, :, :, 2 * XD:VW], corr[:, :, :].unsqueeze(3), ALU.add
                                ).then_inc(s["den_ok"], 1)
                dve.wait_ge(s["den_ok"], t + 1)
                v.reciprocal(rc2[:, :, :], den[:, :, :]).then_inc(s["rc2_ok"], 1)
                dve.wait_ge(s["rc2_ok"], t + 1)
                for r in range(2):
                    rows = slice(r * S, (r + 1) * S)
                    for b in range(2):
                        v.tensor_tensor(on[b * S:(b + 1) * S, r, :, :], o[rows, :, b, r * XD:(r + 1) * XD],
                                        rc2[rows, :, b].unsqueeze(2).broadcast_to([S, J, XD]), ALU.mult
                                        ).then_inc(s["on_ok"], 1)

            def variance2(t, c):
                dve.wait_ge(s["wox_ps"], t + 1)
                dve.wait_ge(s["x1b_ok"], t + 1)
                v.tensor_tensor(z2[:, :], G[:, 1, 0:D], x1b[:, c, :], ALU.add).then_inc(s["z2_ok"], 1)
                dve.wait_ge(s["z2_ok"], t + 1)
                v.bn_stats(st2[:, :], z2[:, :]).then_inc(s["st2_ok"], 1)
                dve.wait_ge(s["st2_ok"], t + 1)
                apart(dve, s["wait_apart"])
                v.bn_aggr(mv2[:, :], st2[:, :]).then_inc(s["mv2_ok"], 1)
                dve.wait_ge(s["mv2_ok"], t + 1)
                v.tensor_scalar(ve2[:, :], mv2[:, 1:2], EPS, None, ALU.add).then_inc(s["ve2_ok"], 1)

            def norm2(t):
                dve.wait_ge(s["rs2_ok"], t + 1)
                need(dve, s["x2_keep"], t)
                need(dve, s["x2t_ps"], t)
                v.tensor_scalar(x2s[:, :], z2[:, :], mv2[:, 0:1], rs2[:, 0:1], ALU.subtract, ALU.mult
                                ).then_inc(s["x2_ok"], 1)

            def route_logits(g, bank):
                n = GROUPS[g][1]
                dve.wait_ge(s["lg_ps"], g + 1)
                v.tensor_tensor(lg[0:n, :], bank[0:n, 0:E], bp2[0:n, :], ALU.add).then_inc(s["lg_sb"], 1)
                dve.wait_ge(s["lg_sb"], g + 1)
                v.tensor_reduce(lm[0:n, :], lg[0:n, :], axis=AX, op=ALU.max, negate=True).then_inc(s["lm_ok"], 1)

            def route_probs(g):
                n = GROUPS[g][1]
                dve.wait_ge(s["pexp_ok"], g + 1)
                v.tensor_reduce(ls[0:n, :], pe_[0:n, :], axis=AX, op=ALU.add).then_inc(s["ls_ok"], 1)
                dve.wait_ge(s["ls_ok"], g + 1)
                v.reciprocal(lr[0:n, :], ls[0:n, :]).then_inc(s["lr_ok"], 1)
                dve.wait_ge(s["lr_ok"], g + 1)
                v.tensor_scalar(pr[0:n, :], pe_[0:n, :], lr[0:n, 0:1], None, ALU.mult).then_inc(s["prob_ok"], 1)

            def route_index(g):
                first, n = GROUPS[g]
                dve.wait_ge(s["prob_ok"], g + 1)
                v.max(pm8[0:n, :], pr[0:n, :]).then_inc(s["pm_ok"], 1)
                dve.wait_ge(s["pm_ok"], g + 1)
                v.max_index(ix8[0:n, :], pm8[0:n, :], pr[0:n, :]).then_inc(s["ix_ok"], 1)
                dve.wait_ge(s["ix_ok"], g + 1)
                dve.wait_ge(s["ixw0_ok"], 1)
                v.tensor_copy(ixw[0:n, 0:1], ix8[0:n, 0:1]).then_inc(s["ixw_ok"], 1)
                dve.wait_ge(s["ixw_ok"], g + 1)
                v.transpose(ixr[:, :], ixw[:, :]).then_inc(s["ixr_ok"], 1)
                dve.wait_ge(s["ixr_ok"], g + 1)
                v.tensor_copy(sel[:, first:first + n], ixr[0:1, 0:n]).then_inc(s["sel_ok"], 1)

            def b2_out(n):
                dve.wait_ge(s["b2_ps"], n + 1)
                v.scalar_tensor_tensor(out=w12v[:, 4 * n:4 * n + 4, O_B2:WEXP],
                                       in0=AV[:, n, :].rearrange("p (e n) -> p e n", e=4), scalar=0.3,
                                       in1=fbo3[:, :].unsqueeze(1).broadcast_to([P, 4, D]),
                                       op0=ALU.mult, op1=ALU.add).then_inc(s["b2_sb"], 1)

            def step(t, odd, prev=True, nxt=True, fill=True, q=None, final=False):
                c = 1 if odd else 0
                if prev:
                    max2(t - 1, 0)
                    max2(t - 1, 1)
                if prev:
                    sub2(t - 1, 0)
                if nxt:
                    bias1(t + 1, 0)
                if prev:
                    sub2(t - 1, 1)
                if nxt:
                    bias1(t + 1, 1)
                if prev:
                    padding(t - 1)
                if nxt:
                    max1(t + 1, 0)
                    max1(t + 1, 1)
                    sub1(t + 1, 0)
                    sub1(t + 1, 1)
                dve.wait_ge(s["wo_ps"], t + 1)
                dve.wait_ge(s["xk_ld"], 16 * (q + 1))
                v.tensor_tensor(z1[:, :], TR[:, 0, 0:D], xk[:, c, :], ALU.add).then_inc(s["z1_ok"], 1)
                dve.wait_ge(s["z1_ok"], t + 1)
                v.bn_stats(st1[:, :], z1[:, :]).then_inc(s["st1_ok"], 1)
                dve.wait_ge(s["st1_ok"], t + 1)
                apart(dve, s["wait_apart"])
                v.bn_aggr(mv1[:, :], st1[:, :]).then_inc(s["mv1_ok"], 1)
                dve.wait_ge(s["mv1_ok"], t + 1)
                v.tensor_scalar(ve1[:, :], mv1[:, 1:2], EPS, None, ALU.add).then_inc(s["ve1_ok"], 1)
                if nxt:
                    sum1(t + 1, 0)
                dve.wait_ge(s["rs1_ok"], t + 1)
                need(dve, s["x1b_ok"], t)
                need(dve, s["x1t_ps"], t)
                v.tensor_scalar(x1[:, :], z1[:, :], mv1[:, 0:1], rs1[:, 0:1], ALU.subtract, ALU.mult
                                ).then_inc(s["x1_ok"], 1)
                if nxt:
                    recip1(t + 1, 0)
                if prev:
                    out_norm(t - 1)
                dve.wait_ge(s["q_ps"], t + 1)
                for r in range(2):
                    rows = slice(r * S, (r + 1) * S)
                    v.tensor_scalar(qpad[rows, :, r, :], TR[rows, 0, 0:P].rearrange("p (b q) -> p b q", b=2),
                                    xbq[rows, 0:1], float(np.float32(XD ** -0.5)), ALU.add, ALU.mult
                                    ).then_inc(s["qpad_ok"], 1)
                if nxt:
                    sum1(t + 1, 1)
                if nxt and not fill:
                    b2_out(0)
                if final:
                    route_logits(0, SC[:, 1, :])
                dve.wait_ge(s["qhi_ok"], t + 1)
                v.tensor_tensor(qlo[:, :, :, :], qpad[:, :, :, :], qhi[:, :, :, :].bitcast(F32), ALU.subtract
                                ).then_inc(s["qlo_ok"], 1)
                if nxt:
                    recip1(t + 1, 1)
                if prev:
                    variance2(t - 1, 1 - c)
                if nxt and not fill:
                    b2_out(1)
                if final:
                    route_probs(0)
                mask2(t, 0)
                if prev:
                    norm2(t - 1)
                if final:
                    route_index(0)
                mask2(t, 1)
                if nxt:
                    value_block(t + 1, 1 - c)

            v.memset(ixw[:, :], 0.0).then_inc(s["ixw0_ok"], 1)
            dve.wait_ge(s["xhi_ok"], 1)
            v.tensor_tensor(xlo[:, :], xt_in[:, :], xhi[:, :].bitcast(F32), ALU.subtract).then_inc(s["xlo_ok"], 1)
            for n in range(4):
                dve.wait_ge(s["m_hi"], n + 1)
                src = (TR, AV)[n // 2][:, n % 2, :].rearrange("p (j n) -> p j n", j=4)
                h0 = 8 * (n // 2) + n % 2
                v.tensor_tensor(mlo[:, h0:h0 + 7:2, :], src, mhi[:, h0:h0 + 7:2, :].bitcast(F32), ALU.subtract
                                ).then_inc(s["m_lo"], 1)
            dve.wait_ge(s["wv_hi"], 1)
            v.tensor_tensor(wvlo[:, :], wvr, wvhi[:, :].bitcast(F32), ALU.subtract).then_inc(s["wv_lo"], 1)
            dve.wait_ge(s["c_mask"], 48)
            masks = maskadd[:, :].rearrange("p (t k) -> p t k", k=P)
            v.scalar_tensor_tensor(out=masks, in0=kmask[:, :].rearrange("p (t k) -> p t k", k=P), scalar=NEG,
                                   in1=causal[:, :].unsqueeze(1).broadcast_to([P, NT, P]),
                                   op0=ALU.mult, op1=ALU.mult).then_inc(s["mask_mul"], 1)
            dve.wait_ge(s["mask_mul"], 1)
            v.tensor_tensor(masks, masks, window[:, :].unsqueeze(1).broadcast_to([P, NT, P]), ALU.add
                            ).then_inc(s["mask_add"], 1)
            dve.wait_ge(s["c_bias"], 32)
            for hh in range(2):
                bias1(0, hh)
            for hh in range(2):
                max1(0, hh)
                sub1(0, hh)
            for hh in range(2):
                sum1(0, hh)
                recip1(0, hh)
            dve.wait_ge(s["c_small"], 160)
            dve.wait_ge(s["memset_done"], 7)
            dve.wait_ge(s["mask_add"], 1)
            value_block(0, 0)
            step(0, False, prev=False, q=0)
            step(1, True, q=0)
            with dve.Fori(1, NP - 1) as q:
                step(2 * q, False, q=q)
                step(2 * q + 1, True, q=q)
            dve.wait_ge(s["c_ffn"], 144)
            v.tensor_scalar(fbo3[:, :], fbo[:, :], 0.3, None, ALU.mult).then_inc(s["fbo3_ok"], 1)
            dve.wait_ge(s["fbo3_ok"], 1)
            step(NT - 2, False, fill=False, q=NP - 1)
            step(NT - 1, True, fill=False, nxt=False, q=NP - 1, final=True)

            def choose(t, w):
                need(dve, s["f_ps"], t - WS + 1)
                e = dve.value_load(sel[0:1, bass.ds(2 * t, 1)], min_val=0, max_val=E - 1)
                v.tensor_copy(wsel[:, w, 0, :], w12[:, bass.ds(e * WEXP, WSEL)]).then_inc(s["wsel0_ok"], 1)
                rows, cols = slice(0, S), bass.ds(t * D, D)
                v.tensor_tensor(x2[rows, cols], x2[rows, cols], w12[rows, bass.ds(e * WEXP + O_B2, D)], ALU.add
                                ).then_inc(s["b2_add0"], 1)

            def scale(t, c):
                dve.wait_ge(s["rs3_ok"], t + 1)
                cols = bass.ds(t * D, D)
                v.tensor_scalar(x2[:, cols], x2[:, cols], mv3[:, c, 0:1], rs3[:, c:c + 1], ALU.subtract, ALU.mult
                                ).then_inc(s["out_ok"], 1)

            def tile(t, w, first=False):
                c = w % 2
                dve.wait_ge(s["f_ps"], t + 1)
                dve.wait_ge(s["b2_add0"], t + 1)
                dve.wait_ge(s["b2_add1"], t + 1)
                cols = bass.ds(t * D, D)
                v.scalar_tensor_tensor(out=x2[:, cols], in0=SC[:, c, 0:D], scalar=0.3, in1=x2[:, cols],
                                       op0=ALU.mult, op1=ALU.add).then_inc(s["y3_ok"], 1)
                if not isinstance(t, int) or t + WS < NT:
                    choose(t + WS, w)
                dve.wait_ge(s["y3_ok"], t + 1)
                apart(dve, s["wait_apart"])
                v.bn_stats(st3[:, :], x2[:, cols]).then_inc(s["st3_ok"], 1)
                if not first:
                    scale(t - 1, 1 - c)
                dve.wait_ge(s["st3_ok"], t + 1)
                apart(dve, s["wait_apart"])
                v.bn_aggr(mv3[:, c, :], st3[:, :]).then_inc(s["mv3_ok"], 1)
                dve.wait_ge(s["mv3_ok"], t + 1)
                v.tensor_scalar(ve3[:, c:c + 1], mv3[:, c, 1:2], EPS, None, ALU.add).then_inc(s["ve3_ok"], 1)

            dve.wait_ge(s["sel_ok"], 1)
            dve.wait_ge(s["w2_sb"], 4)
            dve.wait_ge(s["x2_keep"], NT - 1)
            dve.wait_ge(s["b2_sb"], 2)
            choose(0, 0)
            for hh in range(2):
                max2(NT - 1, hh)
            for hh in range(2):
                sub2(NT - 1, hh)
            choose(1, 1)
            padding(NT - 1)
            choose(2, 2)
            choose(3, 3)
            out_norm(NT - 1)
            tile(0, 0, first=True)
            variance2(NT - 1, 1)
            tile(1, 1)
            norm2(NT - 1)
            tile(2, 2)
            tile(3, 3)
            route_logits(1, AV[:, 0, :])
            route_probs(1)
            route_index(1)
            dve.wait_ge(s["sel_ok"], 2)
            dve.wait_ge(s["x2_keep"], NT)
            with dve.Fori(1, NR - 1) as r:
                for w in range(WS):
                    tile(WS * r + w, w)
            for w in range(WS):
                tile(NT - WS + w, w)
            scale(NT - 1, 1)

        @block.tensor
        def _(pe):
            mm = nc.tensor.matmul

            def split3(out, lhi, llo, rhi, rlo):
                mm(out, lhi, rhi, start=True, stop=False)
                mm(out, lhi, rlo, start=False, stop=False)
                return mm(out, llo, rhi, start=False, stop=True)

            def transposes(dst, src, free, done):
                for hh in range(2):
                    free(hh)
                    for j in range(4):
                        last = nc.tensor.transpose(dst[:, hh, j * P:(j + 1) * P],
                                                   src[:, 4 * hh + j, :, :].rearrange("p b k -> p (b k)"), ident[:, :])
                    last.then_inc(done, 1)

            def y_unit(q, u):
                for par in range(2):
                    last = split3(y_bank(u)[:, par * PT:(par + 1) * PT], mhi[:, 2 * u + par, :], mlo[:, 2 * u + par, :],
                                  xhi[:, :], xlo[:, :])
                last.then_inc(s["y_ps"], 1)

            def v_unit(q, u):
                toks = slice((u // 2) * P, (u // 2 + 1) * P)
                cols = slice((u % 2) * 512, (u % 2 + 1) * 512)
                split3(v_bank(u), xhi[:, toks], xlo[:, toks], wvhi[:, cols], wvlo[:, cols]).then_inc(s["v_ps"], 1)

            def unit(q, odd, f):
                if odd:
                    if f >= 2:
                        pe.wait_ge(s["v_sb"], 4 * q + f - 1)
                    v_unit(q, f)
                else:
                    if f >= 2:
                        pe.wait_ge(s["y_sb"], 8 * q + f + 1)
                    y_unit(q, f + 2)

            def scores1(t, c, ready=None):
                for hh in range(2):
                    if ready:
                        ready(hh)
                    need(pe, s["s2_in"], 2 * t - 2 + hh - 1)
                    for j in range(0, 4, 4):
                        for b in range(2):
                            for par in range(2):
                                dst = SC[par * S:(par + 1) * S, hh, :].rearrange("p (j b k) -> p j b k", j=4, b=2)
                                last = mm(dst[:, :, b, :], xts[:, c * P + b * S:c * P + (b + 1) * S],
                                          Y[:, par, 4 * hh:4 * hh + 4, c * P + b * S:c * P + (b + 1) * S],
                                          start=True, stop=True)
                    last.then_inc(s["s1_ps"], 1)

            def kv(t, c, kt_free, v_free):
                kt_free()
                mm(G[:, 0, 0:P], xwk[:, :], ctxt[:, c * P:(c + 1) * P], start=True, stop=True).then_inc(s["kt_ps"], 1)
                v_free()
                mm(G[:, 1, 0:D], ctxt[:, c * P:(c + 1) * P], xwv[:, :], start=True, stop=True).then_inc(s["vx_ps"], 1)

            def pv2(t, c):
                pe.wait_ge(s["pt2_sb"], 2 * t + 2)
                for j in range(J):
                    last = mm(G[:, 0, j * 2 * VW:(j + 1) * 2 * VW], pt2[:, j, :], vbd[:, c, j, :],
                              start=True, stop=True)
                last.then_inc(s["pv2_ps"], 1)

            def out_transpose(t):
                pe.wait_ge(s["on_ok"], 4 * t + 4)
                nc.tensor.transpose(G[:, 1, 0:P], on[:, :, :, :].rearrange("p r j d -> p (r j d)"), ident[:, :]
                                    ).then_inc(s["ot_ps"], 1)

            def out_product(t):
                pe.wait_ge(s["ot_sb"], t + 1)
                mm(G[:, 1, 0:D], ot[:, :], xwo[:, :], start=True, stop=True).then_inc(s["wox_ps"], 1)

            def x2_transpose(t):
                pe.wait_ge(s["x2_ok"], t + 1)
                nc.tensor.transpose(AV[:, 0, 0:P], x2s[:, :], ident[:, :]).then_inc(s["x2t_ps"], 1)

            def route_hidden(g, bank):
                first, n = GROUPS[g]
                mm(bank[:, 0:n], wp1[:, :], x2t[:, first * S + S - 1:(first + n) * S:S], start=True, stop=True
                   ).then_inc(s["hid_ps"], 1)

            def route_logits(g, bank):
                n = GROUPS[g][1]
                pe.wait_ge(s["hid_sb"], g + 1)
                mm(bank[0:n, 0:E], gp[:, 0:n], wp2[:, :], start=True, stop=True).then_inc(s["lg_ps"], 1)

            def w2wo(n):
                if n >= 2:
                    pe.wait_ge(s["w2_sb"], n - 1)
                for i in range(4):
                    e, f = 2 * n + i // 2, i % 2
                    last = mm(AV[:, n % 2, i * D:(i + 1) * D], w2t[:, e, f * P:(f + 1) * P], fwo[:, :],
                              start=True, stop=True)
                last.then_inc(s["w2_ps"], 1)

            def b2wo(n):
                for i in range(4):
                    last = mm(AV[:, n, i * D:(i + 1) * D], b2t[:, 4 * n + i:4 * n + i + 1].broadcast_to([P, P]),
                              fwo[:, :], start=True, stop=True)
                last.then_inc(s["b2_ps"], 1)

            def step(t, odd, prev=True, nxt=True, fill=True, q=None, final=False):
                c = 1 if odd else 0

                def between(f):
                    if fill:
                        unit(q + 1, odd, f)
                    elif final:
                        w2wo(f)
                    elif f < 2:
                        b2wo(f)

                if not prev:
                    scores1(t + 1, 1 - c, lambda hh: pe.wait_ge(s["s1_in"], hh + 1))
                transposes(TR, p1, lambda hh: pe.wait_ge(s["p1_ok"], 2 * t + hh + 1), s["pt1_ps"])
                if not isinstance(t, int) or t >= 2:
                    if final:
                        pe.wait_ge(s["b2_sb"], 1)
                    elif odd:
                        pe.wait_ge(s["y_sb"], 8 * (q + 1) + 7)
                    else:
                        pe.wait_ge(s["v_sb"], 4 * q + 3)
                    x2_transpose(t - 2)
                if nxt and prev:
                    if odd:
                        pe.wait_ge(s["xts_ok"], q + 2)
                        pe.wait_ge(s["y_sb"], 8 * (q + 2))
                    scores1(t + 1, 1 - c)
                if fill and not odd:
                    pe.wait_ge(s["xlo_ok"], q + 2)
                    pe.wait_ge(s["kt_sb"], t + 1)
                    y_unit(q + 1, 0)
                    pe.wait_ge(s["vbd_ok"], 2 * (t + 1))
                    y_unit(q + 1, 1)
                pe.wait_ge(s["v_sb"], 4 * (q + 1))
                need(pe, s["x2t_sb"], t - 1)
                if final:
                    pe.wait_ge(s["b2_sb"], 2)
                for b in range(2):
                    rows = slice(b * S, (b + 1) * S)
                    for j in range(J):
                        if b == 0 and j % 4 == 0:
                            pe.wait_ge(s["pt1_sb"], 2 * t + j // 4 + 1)
                            apart(pe, s["wait_apart"])
                        for par in range(2):
                            h = 2 * j + par
                            last = mm(AV[par * S:(par + 1) * S, b, j * S:(j + 1) * S],
                                      V[rows, c, h * HD:(h + 1) * HD], pt1[rows, j, par * S:(par + 1) * S],
                                      start=True, stop=True)
                    last.then_inc(s["av_ps"], 1)
                if final:
                    pe.wait_ge(s["s2_in"], 2 * t)
                    pe.wait_ge(s["x2t_sb"], NT - 2)
                    route_hidden(0, SC[:, 1, :])
                if prev:
                    def free2(hh):
                        pe.wait_ge(s["s2_exp"], 2 * t + hh - 1)
                        if fill and not odd:
                            pe.wait_ge(s["y_sb"], 8 * (q + 1) + hh + 1)
                        elif hh == 0:
                            pe.wait_ge(s["kt_sb"], t + 1)
                        else:
                            pe.wait_ge(s["vbd_ok"], 2 * (t + 1))
                    transposes(G, s2, free2, s["pt2_ps"])
                pe.wait_ge(s["at_sb"], 2 * (t + 1))
                for j in range(J):
                    last = mm(TR[:, 0, 0:D], at[:, j, :, :].rearrange("p b q -> p (b q)"), wo[:, j, :],
                              start=(j == 0), stop=(j == J - 1))
                last.then_inc(s["wo_ps"], 1)
                if prev:
                    pv2(t - 1, 1 - c)
                between(0)
                pe.wait_ge(s["x1_ok"], t + 1)
                nc.tensor.transpose(TR[:, 1, 0:P], x1[:, :], ident[:, :]).then_inc(s["x1t_ps"], 1)
                between(1)
                pe.wait_ge(s["x1t_sb"], t + 1)
                mm(TR[:, 0, 0:P], xwq[:, :], x1t[:, :], start=True, stop=True).then_inc(s["q_ps"], 1)
                if final:
                    route_logits(0, SC[:, 1, :])
                if prev:
                    out_transpose(t - 1)
                between(2)
                if prev:
                    out_product(t - 1)
                between(3)
                pe.wait_ge(s["qlo_ok"], t + 1)
                pe.wait_ge(s["kbd_ok"], 4 * (t + 1))
                for hh in range(2):
                    if nxt:
                        pe.wait_ge(s["s1_in"], 2 * t + 3 + hh)
                    elif hh == 1:
                        pe.wait_ge(s["lg_sb"], 1)
                    dst = SC[:, hh, :].rearrange("p (j b k) -> p j b k", j=4, b=2)
                    for b in range(2):
                        qh, ql = (x[:, b, :, :].rearrange("p r q -> p (r q)") for x in (qhi, qlo))
                        js = slice(4 * hh, 4 * hh + 4)
                        last = split3(dst[:, :, b, :], qh, ql, kbdhi[:, b, js, :], kbdlo[:, b, js, :])
                    last.then_inc(s["s2_ps"], 1)
                if fill and not odd:
                    for u in (6, 7):
                        pe.wait_ge(s["y_sb"], 8 * (q + 1) + u - 1)
                        y_unit(q + 1, u)
                if nxt:
                    if odd:
                        pe.wait_ge(s["ctx_ld"], 16 * (q + 2))
                    kv(t + 1, 1 - c, lambda: None, lambda: need(pe, s["z2_ok"], t if prev else 0))

            pe.wait_ge(s["c_table"], 32)
            mm(SC[0:H, 0, 0:NREL], table[:, :], onehot[:, :], start=True, stop=True).then_inc(s["rel_ps"], 1)
            pe.wait_ge(s["c_m"], 32)
            for n in range(4):
                par, j0 = n % 2, 4 * (n // 2)
                rows = slice(par * S, (par + 1) * S)
                for j in range(4):
                    last = mm((TR, AV)[n // 2][:, n % 2, j * D:(j + 1) * D], wkt[rows, j0 + j, :], wqt[rows, j0 + j, :],
                              start=True, stop=True)
                last.then_inc(s["m_ps"], 1)
            pe.wait_ge(s["xlo_ok"], 1)
            for u in range(8):
                if u == 0:
                    pe.wait_ge(s["m_lo"], 2)
                elif u == 2:
                    pe.wait_ge(s["m_lo"], 4)
                elif u >= 4:
                    pe.wait_ge(s["y_sb"], u - 1)
                y_unit(0, u)
            pe.wait_ge(s["rel_sb"], 1)
            pe.wait_ge(s["xts_ok"], 1)
            scores1(0, 0, lambda hh: pe.wait_ge(s["y_sb"], 4 * hh + 4))
            pe.wait_ge(s["c_small"], 160)
            pe.wait_ge(s["ctx_ld"], 16)
            kv(0, 0, lambda: None, lambda: None)
            pe.wait_ge(s["wv_lo"], 1)
            for u in range(4):
                if u >= 2:
                    pe.wait_ge(s["v_sb"], u - 1)
                v_unit(0, u)
            pe.wait_ge(s["kt_sb"], 1)
            pe.wait_ge(s["vbd_ok"], 2)
            pe.wait_ge(s["c_ident"], 16)
            pe.wait_ge(s["c_wo"], 16)
            step(0, False, prev=False, q=0)
            step(1, True, q=0)
            with pe.Fori(1, NP - 1) as q:
                step(2 * q, False, q=q)
                step(2 * q + 1, True, q=q)
            pe.wait_ge(s["c_ffn"], 144)
            step(NT - 2, False, fill=False, q=NP - 1)
            pe.wait_ge(s["c_w2t"], 16)
            step(NT - 1, True, fill=False, nxt=False, q=NP - 1, final=True)


            def up_free(t):
                pe.wait_ge(s["wsel0_ok"], t + 1)
                pe.wait_ge(s["wsel1_ok"], t + 1)
                need(pe, s["h_sb"], 4 * (t - 1))

            def up_part(t, w, b, f):
                return mm(TR[:, w % 2, (b * FC + f) * S:(b * FC + f + 1) * S], wsel[:, w, b, f * P:(f + 1) * P],
                          x2t[:, bass.ds(t * P + b * S, S)], start=True, stop=True)

            def up(t, w):
                up_free(t)
                for b in range(2):
                    for f in range(FC):
                        done = up_part(t, w, b, f)
                done.then_inc(s["h_ps"], 1)

            def down_free(t):
                pe.wait_ge(s["h_sb"], 4 * (t + 1))
                need(pe, s["y3_ok"], t - 1)

            def down_part(w, b, f):
                dst = SC[b * S:(b + 1) * S, w % 2, 0:D]
                return mm(dst, ht[:, w % 2, b, f, :], wsel[:, w, b, O_W2 + f * D:O_W2 + (f + 1) * D],
                          start=(f == 0), stop=(f == FC - 1))

            def down(t, w):
                down_free(t)
                for b in range(2):
                    for f in range(FC):
                        done = down_part(w, b, f)
                done.then_inc(s["f_ps"], 1)

            def pair(t, w):
                down_free(t)
                up_free(t + 2)
                for b in range(2):
                    for f in range(FC):
                        up_done = up_part(t + 2, (w + 2) % WS, b, f)
                        if b == 1 and f == FC - 1:
                            up_done.then_inc(s["h_ps"], 1)
                        down_done = down_part(w, b, f)
                down_done.then_inc(s["f_ps"], 1)

            def free2_last(hh):
                pe.wait_ge(s["s2_exp"], 2 * NT + hh - 1)
                if hh == 1:
                    pe.wait_ge(s["z2_ok"], NT - 1)

            pe.wait_ge(s["w2_sb"], 3)
            x2_transpose(NT - 2)
            up(0, 0)
            transposes(G, s2, free2_last, s["pt2_ps"])
            up(1, 1)
            pv2(NT - 1, 1)
            pair(0, 0)
            out_transpose(NT - 1)
            pair(1, 1)
            out_product(NT - 1)
            pair(2, 2)
            pe.wait_ge(s["x2_ok"], NT)
            nc.tensor.transpose(G[:, 1, 0:P], x2s[:, :], ident[:, :]).then_inc(s["x2t_ps"], 1)
            pair(3, 3)
            pe.wait_ge(s["x2t_sb"], NT)
            route_hidden(1, AV[:, 0, :])
            route_logits(1, AV[:, 0, :])
            with pe.Fori(1, NR - 1) as r:
                for w in range(WS):
                    pair(WS * r + w, w)
            pair(NT - 4, 0)
            pair(NT - 3, 1)
            down(NT - 2, 2)
            down(NT - 1, 3)


def bucket_rows():
    dist = np.arange(-(S - 1), S)
    nb = BUCKETS // 2
    exact = nb // 2
    out = (dist > 0).astype(np.int32) * nb
    a = np.abs(dist)
    safe = np.maximum(a, 1).astype(np.float32)
    large = exact + (np.log(safe / np.float32(exact)) / np.float32(np.log(MAX_DIST / exact))
                     * np.float32(nb - exact)).astype(np.int32)
    out += np.where(a < exact, a, np.minimum(large, nb - 1))
    return (np.arange(BUCKETS)[:, None] == out[None, :]).astype(np.float32)


def kernel(**inputs):
    import concourse.bacc as bacc
    from concourse.bass_utils import run_bass_kernel_spmd

    a = {k: np.asarray(v) for k, v in inputs.items()}
    x = a["x"].reshape(TOK, D)
    pos = np.arange(S)
    row = np.arange(P)
    arrays = {
        "x": x, "xT": x.T, "ctxT": a["ctx_1024"].reshape(TOK, D).T,
        "mask": a["mask_BxS2_bf1"].reshape(TOK).view(np.uint8),
        "WkT": a["L0_attn_Wk"].T, "WqT": a["L0_attn_Wq"].T, "Wv": a["L0_attn_Wv"], "Wo": a["L0_attn_Wo"],
        "table": a["L0_attn_rel_bias"],
        "xWqT": a["L0_xattn_W_q"].T, "xWkT": a["L0_xattn_W_k"].T, "xWvT": a["L0_xattn_W_v"].T,
        "xWoT": a["L0_xattn_W_o"].T, "xbq": a["L0_xattn_b_q"].reshape(D, 1), "xbk": a["L0_xattn_b_k"].reshape(D, 1),
        "xbv": a["L0_xattn_b_v"], "xbo": a["L0_xattn_b_o"],
        "Wp1": a["L0_ffn_Wp1"], "bp1": a["L0_ffn_bp1"].reshape(P, 1), "Wp2": a["L0_ffn_Wp2"], "bp2": a["L0_ffn_bp2"],
        "W1": a["L0_ffn_W1"], "b1T": a["L0_ffn_b1"].reshape(E, FC, P).transpose(2, 0, 1),
        "W2T": a["L0_ffn_W2"].transpose(0, 2, 1), "b2T": a["L0_ffn_b2"].T,
        "fWo": a["L0_ffn_Wo"], "fbo": a["L0_ffn_bo"],
        "onehot": bucket_rows(),
        "ident": np.eye(P, dtype=np.float32),
        "causal": np.tile((pos[:, None] >= pos[None, :]).astype(np.float32), (2, 2)),
        "window": np.tile(np.where((pos[:, None] < S // 2) & (pos[None, :] >= S // 2), -2 * NEG, -NEG
                                   ).astype(np.float32), (2, 2)),
        "headmask": ((row[:, None] // XD) % J == np.arange(J)[None, :]).astype(np.float32),
        "w0flag": np.where(row % S < S // 2, S // 2, 0).astype(np.float32).reshape(P, 1),
    }
    nc = bacc.Bacc("TRN2", target_bir_lowering=False, num_devices=1)
    arrays = {k: np.ascontiguousarray(v) for k, v in arrays.items()}
    din = {k: nc.dram_tensor(f"in_{k}", v.shape, mybir.dt.from_np(v.dtype), kind="ExternalInput").ap()
           for k, v in arrays.items()}
    out = nc.dram_tensor("out_x", (TOK, D), F32, kind="ExternalOutput").ap()
    build(nc, din, out)
    r = run_bass_kernel_spmd(nc, [{f"in_{k}": v for k, v in arrays.items()}], core_ids=[0])
    return r.results[0]["out_x"].reshape(B, S, D)
```
